# Optimizing a Trainium2 kernel written in Bass

```python
import numpy as np
import jax
import jax.numpy as jnp

def _softmax(x, axis=-1):
    return jax.nn.softmax(x, axis=axis)

def _gelu(x):
    return jax.nn.gelu(x, approximate=True)

def _silu(x):
    return jax.nn.silu(x)

def _sigmoid(x):
    return jax.nn.sigmoid(x)

def _layernorm(x, axis=-1, eps=1e-05):
    m = jnp.mean(x, axis=axis, keepdims=True)
    v = jnp.var(x, axis=axis, keepdims=True)
    return (x - m) / jnp.sqrt(v + eps)

def _scatter_add(tgt, idx, src, axis=0):
    return tgt.at[idx].add(src)

def _segment_sum(src, seg, n):
    return jax.ops.segment_sum(src, seg, n)
kernel_name = 'mk_early_fusion_embed_d1_tok_img256_r4_4a6d5a'

def setup_inputs(seed: int=0):
    np.random.seed(seed)
    _w = jnp.asarray

    def _rec_inputs():
        import jax
        import jax.numpy as jnp
        _rk = jax.random.key(seed)
        x = 9.04603e-05 + 1.00016 * jax.random.normal(jax.random.fold_in(_rk, 1), (8, 1, 224, 224), jnp.float32)
        x_txt = jax.random.randint(jax.random.fold_in(_rk, 51), (8, 32), 0, 64, jnp.int32)
        fside_BS_continuous_positions = jax.random.uniform(jax.random.fold_in(_rk, 71), (8, 32), jnp.float32, 0.0, 0.999927)
        return (x, x_txt, fside_BS_continuous_positions)
    x, x_txt, fside_BS_continuous_positions = _rec_inputs()

    def _L0_tok_setup():
        import jax, jax.numpy as jnp
        import numpy as np
        WS = 7
        H = W = 56
        C = 64
        NH = 8
        HD = C // NH
        SCALE = HD ** (-0.5)
        SHIFT = WS // 2
        N = WS * WS

        def _rel_pos_index():
            coords = np.stack(np.meshgrid(np.arange(WS), np.arange(WS), indexing='ij'))
            cf = coords.reshape(2, -1)
            rel = (cf[:, :, None] - cf[:, None, :]).transpose(1, 2, 0).copy()
            rel[..., 0] += WS - 1
            rel[..., 1] += WS - 1
            rel[..., 0] *= 2 * WS - 1
            return jnp.array(rel.sum(-1))

        def _attn_mask():
            img = np.zeros((H, W), np.int32)
            cnt = 0
            for h in (slice(0, -WS), slice(-WS, -SHIFT), slice(-SHIFT, None)):
                for w in (slice(0, -WS), slice(-WS, -SHIFT), slice(-SHIFT, None)):
                    cnt += 1
                    img[h, w] = cnt
            mw = img.reshape(H // WS, WS, W // WS, WS).transpose(0, 2, 1, 3).reshape(-1, N)
            diff = mw[:, None, :] - mw[:, :, None]
            return jnp.array(np.where(diff != 0, -100.0, 0.0).astype(np.float32))

        def _layernorm(x, g, b):
            m = x.mean(-1, keepdims=True)
            v = ((x - m) ** 2).mean(-1, keepdims=True)
            return (x - m) * jax.lax.rsqrt(v + 1e-05) * g + b

        def _window_partition(x):
            B = x.shape[0]
            x = x.reshape(B, H // WS, WS, W // WS, WS, C).transpose(0, 1, 3, 2, 4, 5)
            return x.reshape(-1, N, C)

        def _window_reverse(xw, B):
            x = xw.reshape(B, H // WS, W // WS, WS, WS, C).transpose(0, 1, 3, 2, 4, 5)
            return x.reshape(B, H, W, C)

        def _swin_block(x, p, shift, rpi, amask):
            B = x.shape[0]
            shortcut = x
            h = _layernorm(x, p['n1g'], p['n1b']).reshape(B, H, W, C)
            if shift > 0:
                h = jnp.roll(h, (-shift, -shift), axis=(1, 2))
            xw = _window_partition(h)
            B_ = xw.shape[0]
            qkv = (xw @ p['qkv_w'].T + p['qkv_b']).reshape(B_, N, 3, NH, HD).transpose(2, 0, 3, 1, 4)
            q, k, v = (qkv[0], qkv[1], qkv[2])
            attn = jnp.einsum('bhnd,bhmd->bhnm', q * SCALE, k)
            attn = attn + p['rpb'][rpi].transpose(2, 0, 1)[None]
            if shift > 0:
                nW = amask.shape[0]
                attn = attn.reshape(B_ // nW, nW, NH, N, N) + amask[None, :, None]
                attn = attn.reshape(B_, NH, N, N)
            attn = jax.nn.softmax(attn, axis=-1)
            o = jnp.einsum('bhnm,bhmd->bhnd', attn, v).transpose(0, 2, 1, 3).reshape(B_, N, C)
            o = o @ p['proj_w'].T + p['proj_b']
            h = _window_reverse(o, B)
            if shift > 0:
                h = jnp.roll(h, (shift, shift), axis=(1, 2))
            x = shortcut + h.reshape(B, H * W, C)
            y = _layernorm(x, p['n2g'], p['n2b'])
            y = jax.nn.gelu(y @ p['w1'].T + p['b1'], approximate=False)
            return x + y @ p['w2'].T + p['b2']
        key = jax.random.key(seed)
        ks = jax.random.split(key, 8)
        s = 0.02
        return {'x': jax.random.normal(ks[0], (16, 1, 224, 224), jnp.float32), 'pe_w': jax.random.normal(ks[1], (C, 1, 4, 4), jnp.float32) * s, 'pe_b': jnp.zeros((C,), jnp.float32), 'pe_ng': jnp.ones((C,), jnp.float32), 'pe_nb': jnp.zeros((C,), jnp.float32), 'n1g': jnp.ones((2, C), jnp.float32), 'n1b': jnp.zeros((2, C), jnp.float32), 'qkv_w': jax.random.normal(ks[2], (2, 3 * C, C), jnp.float32) * s, 'qkv_b': jnp.zeros((2, 3 * C), jnp.float32), 'rpb': jax.random.normal(ks[3], (2, (2 * WS - 1) ** 2, NH), jnp.float32) * s, 'proj_w': jax.random.normal(ks[4], (2, C, C), jnp.float32) * s, 'proj_b': jnp.zeros((2, C), jnp.float32), 'n2g': jnp.ones((2, C), jnp.float32), 'n2b': jnp.zeros((2, C), jnp.float32), 'w1': jax.random.normal(ks[5], (2, 4 * C, C), jnp.float32) * s, 'b1': jnp.zeros((2, 4 * C), jnp.float32), 'w2': jax.random.normal(ks[6], (2, C, 4 * C), jnp.float32) * s, 'b2': jnp.zeros((2, C), jnp.float32)}
    _L0_tok_all = _L0_tok_setup()
    _L0_tok_in = {k: v for k, v in _L0_tok_all.items() if k in ('pe_w', 'pe_b', 'pe_ng', 'pe_nb', 'n1g', 'n1b', 'qkv_w', 'qkv_b', 'rpb', 'proj_w', 'proj_b', 'n2g', 'n2b', 'w1', 'b1', 'w2', 'b2')}
    del _L0_tok_all

    def _L0_txt_setup():
        import jax, jax.numpy as jnp
        import numpy as np
        N_SCALES = 4

        def _conv1d(x, w, b, pad):
            y = jax.lax.conv_general_dilated(x, w, window_strides=(1,), padding=[(pad, pad)], dimension_numbers=('NCH', 'OIH', 'NCH'))
            return y + b[None, :, None]
        key = jax.random.key(seed)
        ks = jax.random.split(key, 12)
        B, S, P, D = (8, 512, 512, 64)
        byte_sequence = jax.random.randint(ks[0], (B, S), 0, 64, dtype=jnp.int64)
        continuous_positions = jax.random.uniform(ks[1], (B, P), dtype=jnp.float32)
        emb = jax.random.normal(ks[2], (64, D), dtype=jnp.float32)
        locality_shapes = jax.random.normal(ks[3], (64, 4), dtype=jnp.float32)
        w1 = jax.random.normal(ks[4], (128, 64, 7), dtype=jnp.float32) * 0.02
        b1 = jnp.zeros((128,), dtype=jnp.float32)
        w2 = jax.random.normal(ks[5], (64, 128, 5), dtype=jnp.float32) * 0.02
        b2 = jnp.zeros((64,), dtype=jnp.float32)
        w3 = jax.random.normal(ks[6], (1, 64, 3), dtype=jnp.float32) * 0.02
        b3 = jnp.zeros((1,), dtype=jnp.float32)
        multiscale_widths = jnp.array([0.01, 0.02, 0.05, 0.1], dtype=jnp.float32)
        scale_weights = jnp.ones((4,), dtype=jnp.float32)
        return {'byte_sequence': byte_sequence, 'continuous_positions': continuous_positions, 'emb': emb, 'locality_shapes': locality_shapes, 'w1': w1, 'b1': b1, 'w2': w2, 'b2': b2, 'w3': w3, 'b3': b3, 'multiscale_widths': multiscale_widths, 'scale_weights': scale_weights}
    _L0_txt_all = _L0_txt_setup()
    _L0_txt_in = {k: v for k, v in _L0_txt_all.items() if k in ('emb', 'locality_shapes', 'w1', 'b1', 'w2', 'b2', 'w3', 'b3', 'multiscale_widths', 'scale_weights')}
    del _L0_txt_all

    def _L0_attn_setup():
        import jax, jax.numpy as jnp
        import numpy as np
        DIM = 64
        key = jax.random.key(seed)
        ks = jax.random.split(key, 7)
        s = 1.0 / np.sqrt(DIM)
        x = jax.random.normal(ks[0], (4, 1024, DIM), dtype=jnp.float32)
        Wq = jax.random.uniform(ks[1], (DIM, DIM), jnp.float32, -s, s)
        bq = jax.random.uniform(ks[2], (DIM,), jnp.float32, -s, s)
        Wk = jax.random.uniform(ks[3], (DIM, DIM), jnp.float32, -s, s)
        bk = jax.random.uniform(ks[4], (DIM,), jnp.float32, -s, s)
        Wv = jax.random.uniform(ks[5], (DIM, DIM), jnp.float32, -s, s)
        bv = jax.random.uniform(ks[6], (DIM,), jnp.float32, -s, s)
        return {'x': x, 'Wq': Wq, 'bq': bq, 'Wk': Wk, 'bk': bk, 'Wv': Wv, 'bv': bv}
    _L0_attn_all = _L0_attn_setup()
    _L0_attn_in = {k: v for k, v in _L0_attn_all.items() if k in ('Wq', 'bq', 'Wk', 'bk', 'Wv', 'bv')}
    del _L0_attn_all

    def _L0_ffn_setup():
        import jax, jax.numpy as jnp
        import numpy as np
        B, K, D = (128, 16, 64)
        E = 32
        H = int(D * 0.25)
        key = jax.random.key(seed)
        ks = jax.random.split(key, 7)
        d_rs = D ** (-0.5)
        h_rs = H ** (-0.5)
        x = jax.random.normal(ks[0], (B, K, D), dtype=jnp.float32)
        router_w = jax.random.uniform(ks[1], (E, D), jnp.float32, -d_rs, d_rs)
        router_b = jax.random.uniform(ks[2], (E,), jnp.float32, -d_rs, d_rs)
        W1 = jax.random.uniform(ks[3], (E, D, H), jnp.float32, -h_rs, h_rs)
        b1 = jax.random.uniform(ks[4], (E, H), jnp.float32, -h_rs, h_rs)
        W2 = jax.random.uniform(ks[5], (E, H, D), jnp.float32, -d_rs, d_rs)
        b2 = jax.random.uniform(ks[6], (E, D), jnp.float32, -d_rs, d_rs)
        return {'x': x, 'router_w': router_w, 'router_b': router_b, 'W1': W1, 'b1': b1, 'W2': W2, 'b2': b2}
    _L0_ffn_all = _L0_ffn_setup()
    _L0_ffn_in = {k: v for k, v in _L0_ffn_all.items() if k in ('router_w', 'router_b', 'W1', 'b1', 'W2', 'b2')}
    del _L0_ffn_all
    return {'x': x, 'x_txt': x_txt, 'fside_BS_continuous_positions': fside_BS_continuous_positions, 'L0_tok_pe_w': _L0_tok_in['pe_w'], 'L0_tok_pe_b': _L0_tok_in['pe_b'], 'L0_tok_pe_ng': _L0_tok_in['pe_ng'], 'L0_tok_pe_nb': _L0_tok_in['pe_nb'], 'L0_tok_n1g': _L0_tok_in['n1g'], 'L0_tok_n1b': _L0_tok_in['n1b'], 'L0_tok_qkv_w': _L0_tok_in['qkv_w'], 'L0_tok_qkv_b': _L0_tok_in['qkv_b'], 'L0_tok_rpb': _L0_tok_in['rpb'], 'L0_tok_proj_w': _L0_tok_in['proj_w'], 'L0_tok_proj_b': _L0_tok_in['proj_b'], 'L0_tok_n2g': _L0_tok_in['n2g'], 'L0_tok_n2b': _L0_tok_in['n2b'], 'L0_tok_w1': _L0_tok_in['w1'], 'L0_tok_b1': _L0_tok_in['b1'], 'L0_tok_w2': _L0_tok_in['w2'], 'L0_tok_b2': _L0_tok_in['b2'], 'L0_txt_emb': _L0_txt_in['emb'], 'L0_txt_locality_shapes': _L0_txt_in['locality_shapes'], 'L0_txt_w1': _L0_txt_in['w1'], 'L0_txt_b1': _L0_txt_in['b1'], 'L0_txt_w2': _L0_txt_in['w2'], 'L0_txt_b2': _L0_txt_in['b2'], 'L0_txt_w3': _L0_txt_in['w3'], 'L0_txt_b3': _L0_txt_in['b3'], 'L0_txt_multiscale_widths': _L0_txt_in['multiscale_widths'], 'L0_txt_scale_weights': _L0_txt_in['scale_weights'], 'L0_attn_Wq': _L0_attn_in['Wq'], 'L0_attn_bq': _L0_attn_in['bq'], 'L0_attn_Wk': _L0_attn_in['Wk'], 'L0_attn_bk': _L0_attn_in['bk'], 'L0_attn_Wv': _L0_attn_in['Wv'], 'L0_attn_bv': _L0_attn_in['bv'], 'L0_ffn_router_w': _L0_ffn_in['router_w'], 'L0_ffn_router_b': _L0_ffn_in['router_b'], 'L0_ffn_W1': _L0_ffn_in['W1'], 'L0_ffn_b1': _L0_ffn_in['b1'], 'L0_ffn_W2': _L0_ffn_in['W2'], 'L0_ffn_b2': _L0_ffn_in['b2']}

def reference(x, x_txt, fside_BS_continuous_positions, L0_tok_pe_w, L0_tok_pe_b, L0_tok_pe_ng, L0_tok_pe_nb, L0_tok_n1g, L0_tok_n1b, L0_tok_qkv_w, L0_tok_qkv_b, L0_tok_rpb, L0_tok_proj_w, L0_tok_proj_b, L0_tok_n2g, L0_tok_n2b, L0_tok_w1, L0_tok_b1, L0_tok_w2, L0_tok_b2, L0_txt_emb, L0_txt_locality_shapes, L0_txt_w1, L0_txt_b1, L0_txt_w2, L0_txt_b2, L0_txt_w3, L0_txt_b3, L0_txt_multiscale_widths, L0_txt_scale_weights, L0_attn_Wq, L0_attn_bq, L0_attn_Wk, L0_attn_bk, L0_attn_Wv, L0_attn_bv, L0_ffn_router_w, L0_ffn_router_b, L0_ffn_W1, L0_ffn_b1, L0_ffn_W2, L0_ffn_b2):
    import jax
    import jax.numpy as jnp

    def _L0_tok_ref(x, pe_w, pe_b, pe_ng, pe_nb, n1g, n1b, qkv_w, qkv_b, rpb, proj_w, proj_b, n2g, n2b, w1, b1, w2, b2):
        import jax, jax.numpy as jnp
        import numpy as np
        WS = 7
        H = W = 56
        C = 64
        NH = 8
        HD = C // NH
        SCALE = HD ** (-0.5)
        SHIFT = WS // 2
        N = WS * WS

        def _rel_pos_index():
            coords = np.stack(np.meshgrid(np.arange(WS), np.arange(WS), indexing='ij'))
            cf = coords.reshape(2, -1)
            rel = (cf[:, :, None] - cf[:, None, :]).transpose(1, 2, 0).copy()
            rel[..., 0] += WS - 1
            rel[..., 1] += WS - 1
            rel[..., 0] *= 2 * WS - 1
            return jnp.array(rel.sum(-1))

        def _attn_mask():
            img = np.zeros((H, W), np.int32)
            cnt = 0
            for h in (slice(0, -WS), slice(-WS, -SHIFT), slice(-SHIFT, None)):
                for w in (slice(0, -WS), slice(-WS, -SHIFT), slice(-SHIFT, None)):
                    cnt += 1
                    img[h, w] = cnt
            mw = img.reshape(H // WS, WS, W // WS, WS).transpose(0, 2, 1, 3).reshape(-1, N)
            diff = mw[:, None, :] - mw[:, :, None]
            return jnp.array(np.where(diff != 0, -100.0, 0.0).astype(np.float32))

        def _layernorm(x, g, b):
            m = x.mean(-1, keepdims=True)
            v = ((x - m) ** 2).mean(-1, keepdims=True)
            return (x - m) * jax.lax.rsqrt(v + 1e-05) * g + b

        def _window_partition(x):
            B = x.shape[0]
            x = x.reshape(B, H // WS, WS, W // WS, WS, C).transpose(0, 1, 3, 2, 4, 5)
            return x.reshape(-1, N, C)

        def _window_reverse(xw, B):
            x = xw.reshape(B, H // WS, W // WS, WS, WS, C).transpose(0, 1, 3, 2, 4, 5)
            return x.reshape(B, H, W, C)

        def _swin_block(x, p, shift, rpi, amask):
            B = x.shape[0]
            shortcut = x
            h = _layernorm(x, p['n1g'], p['n1b']).reshape(B, H, W, C)
            if shift > 0:
                h = jnp.roll(h, (-shift, -shift), axis=(1, 2))
            xw = _window_partition(h)
            B_ = xw.shape[0]
            qkv = (xw @ p['qkv_w'].T + p['qkv_b']).reshape(B_, N, 3, NH, HD).transpose(2, 0, 3, 1, 4)
            q, k, v = (qkv[0], qkv[1], qkv[2])
            attn = jnp.einsum('bhnd,bhmd->bhnm', q * SCALE, k)
            attn = attn + p['rpb'][rpi].transpose(2, 0, 1)[None]
            if shift > 0:
                nW = amask.shape[0]
                attn = attn.reshape(B_ // nW, nW, NH, N, N) + amask[None, :, None]
                attn = attn.reshape(B_, NH, N, N)
            attn = jax.nn.softmax(attn, axis=-1)
            o = jnp.einsum('bhnm,bhmd->bhnd', attn, v).transpose(0, 2, 1, 3).reshape(B_, N, C)
            o = o @ p['proj_w'].T + p['proj_b']
            h = _window_reverse(o, B)
            if shift > 0:
                h = jnp.roll(h, (shift, shift), axis=(1, 2))
            x = shortcut + h.reshape(B, H * W, C)
            y = _layernorm(x, p['n2g'], p['n2b'])
            y = jax.nn.gelu(y @ p['w1'].T + p['b1'], approximate=False)
            return x + y @ p['w2'].T + p['b2']
        B = x.shape[0]
        h = jax.lax.conv_general_dilated(x, pe_w, (4, 4), 'VALID', dimension_numbers=('NCHW', 'OIHW', 'NCHW'))
        h = h + pe_b[None, :, None, None]
        t = h.reshape(B, C, H * W).transpose(0, 2, 1)
        t = _layernorm(t, pe_ng, pe_nb)
        rpi = _rel_pos_index()
        amask = _attn_mask()
        for i, shift in enumerate((0, SHIFT)):
            p = {'n1g': n1g[i], 'n1b': n1b[i], 'qkv_w': qkv_w[i], 'qkv_b': qkv_b[i], 'rpb': rpb[i], 'proj_w': proj_w[i], 'proj_b': proj_b[i], 'n2g': n2g[i], 'n2b': n2b[i], 'w1': w1[i], 'b1': b1[i], 'w2': w2[i], 'b2': b2[i]}
            t = _swin_block(t, p, shift, rpi, amask)
        return t

    def _L0_txt_ref(byte_sequence, continuous_positions, emb, locality_shapes, w1, b1, w2, b2, w3, b3, multiscale_widths, scale_weights):
        import jax, jax.numpy as jnp
        import numpy as np
        N_SCALES = 4

        def _conv1d(x, w, b, pad):
            y = jax.lax.conv_general_dilated(x, w, window_strides=(1,), padding=[(pad, pad)], dimension_numbers=('NCH', 'OIH', 'NCH'))
            return y + b[None, :, None]
        B, S = byte_sequence.shape
        P = continuous_positions.shape[1]
        amps = emb[byte_sequence]
        onehot = jax.nn.one_hot(byte_sequence, 64, dtype=jnp.float32)
        onehot = jnp.transpose(onehot, (0, 2, 1))
        h = jax.nn.gelu(_conv1d(onehot, w1, b1, 3), approximate=False)
        h = jax.nn.gelu(_conv1d(h, w2, b2, 2), approximate=False)
        ctx = jax.nn.sigmoid(_conv1d(h, w3, b3, 1))[:, 0, :]
        amps = amps * ctx[:, :, None]
        lp = locality_shapes[byte_sequence]
        byte_pos = jnp.linspace(0.0, 1.0, S, dtype=jnp.float32)
        center = byte_pos[None, :] + lp[..., 0] * 0.05
        xd = continuous_positions[:, None, :] - center[..., None]
        amp_scale = jax.nn.sigmoid(lp[..., 2])
        phase = lp[..., 3] * jnp.pi
        abs_w = jnp.abs(lp[..., 1])
        TWO_PI = 2.0 * jnp.pi
        basis_total = jnp.zeros((B, S, P), dtype=jnp.float32)
        for s in range(N_SCALES):
            width = abs_w * multiscale_widths[s] + 1e-05
            z = xd / width[..., None]
            basis = jnp.exp(-0.5 * z * z) * jnp.cos(phase[..., None] + TWO_PI * z)
            basis_total = basis_total + basis * (amp_scale[..., None] * scale_weights[s] ** 2)
        semantic_field = jnp.einsum('bsp,bsd->bpd', basis_total, amps)
        return semantic_field

    def _L0_attn_ref(x, Wq, bq, Wk, bk, Wv, bv):
        import jax, jax.numpy as jnp
        import numpy as np
        DIM = 64
        Q = jnp.einsum('bsd,ed->bse', x, Wq) + bq
        K = jnp.einsum('bsd,ed->bse', x, Wk) + bk
        V = jnp.einsum('bsd,ed->bse', x, Wv) + bv
        scale = 1.0 / jnp.sqrt(jnp.asarray(Q.shape[-1], Q.dtype))
        scores = jnp.einsum('bqd,bkd->bqk', Q, K) * scale
        attn = jax.nn.softmax(scores, axis=-1)
        return jnp.einsum('bqk,bkd->bqd', attn, V)

    def _L0_ffn_ref(x, router_w, router_b, W1, b1, W2, b2):
        import jax, jax.numpy as jnp
        import numpy as np
        B, K, D = (128, 16, 64)
        E = 32
        H = int(D * 0.25)
        xf = x.reshape(-1, D)
        logits = xf @ router_w.T + router_b
        idx = jnp.argmax(logits, axis=-1)
        w1t = jnp.take(W1, idx, axis=0)
        h = jnp.einsum('nd,ndh->nh', xf, w1t) + jnp.take(b1, idx, axis=0)
        h = jax.nn.relu(h)
        w2t = jnp.take(W2, idx, axis=0)
        out = jnp.einsum('nh,nhd->nd', h, w2t) + jnp.take(b2, idx, axis=0)
        out = jax.nn.relu(out)
        return out.reshape(x.shape)
    h = _L0_tok_ref(x, L0_tok_pe_w, L0_tok_pe_b, L0_tok_pe_ng, L0_tok_pe_nb, L0_tok_n1g, L0_tok_n1b, L0_tok_qkv_w, L0_tok_qkv_b, L0_tok_rpb, L0_tok_proj_w, L0_tok_proj_b, L0_tok_n2g, L0_tok_n2b, L0_tok_w1, L0_tok_b1, L0_tok_w2, L0_tok_b2)
    h = jnp.concatenate([h, _L0_txt_ref(x_txt, fside_BS_continuous_positions, L0_txt_emb, L0_txt_locality_shapes, L0_txt_w1, L0_txt_b1, L0_txt_w2, L0_txt_b2, L0_txt_w3, L0_txt_b3, L0_txt_multiscale_widths, L0_txt_scale_weights)], axis=1)
    h = h + _L0_attn_ref(_layernorm(h, axis=-1), L0_attn_Wq, L0_attn_bq, L0_attn_Wk, L0_attn_bk, L0_attn_Wv, L0_attn_bv)
    h = h + _L0_ffn_ref(_layernorm(h, axis=-1), L0_ffn_router_w, L0_ffn_router_b, L0_ffn_W1, L0_ffn_b1, L0_ffn_W2, L0_ffn_b2)
    return h

_drawn_inputs = setup_inputs


def setup_inputs(seed=0):
    import zlib

    import numpy as np

    out = dict(_drawn_inputs(seed))
    spreads = {'L0_tok_pe_b': (0.0, 0.1),
     'L0_tok_pe_ng': (1.0, 0.2),
     'L0_tok_pe_nb': (0.0, 0.1),
     'L0_tok_n1g': (1.0, 0.6),
     'L0_tok_n1b': (0.0, 0.568),
     'L0_tok_qkv_b': (0.0, 0.1),
     'L0_tok_proj_b': (0.0, 0.1),
     'L0_tok_n2g': (1.0, 0.6),
     'L0_tok_n2b': (0.0, 0.619),
     'L0_tok_b1': (0.0, 0.1),
     'L0_tok_b2': (0.0, 0.1),
     'L0_txt_b1': (0.0, 0.8),
     'L0_txt_b2': (0.0, 2.0),
     'L0_txt_scale_weights': (1.0, 0.6)}
    factors = {'L0_tok_rpb': 200.0,
     'L0_txt_w1': 8.0,
     'L0_txt_w2': 8.0,
     'L0_txt_w3': 8.0,
     'L0_txt_multiscale_widths': 8.0,
     'L0_attn_bq': 6.303,
     'L0_attn_bk': 200.0,
     'L0_ffn_b1': 3.039}
    for name, (base, spread) in spreads.items():
        noise = np.random.default_rng([zlib.crc32(name.encode()), seed]).standard_normal(out[name].shape)
        drawn = base * np.exp(spread * noise) if base else spread * noise
        out[name] = jnp.asarray(drawn.astype(out[name].dtype))
    for name, factor in factors.items():
        out[name] = (out[name] * factor).astype(out[name].dtype)
    return out
```

```python
IMG, SIDE, WIN, CH, HEADS = 8, 56, 7, 64, 8
PAIRS = IMG // 2
STRIPS = SIDE // WIN
WTOK = WIN * WIN
UTOK = STRIPS * WTOK
UNITS = PAIRS * STRIPS
TXT = 32
TOK = SIDE * SIDE + TXT
EXPERTS, EH = 32, 16
EPS = 1e-5


def pack_columns(parts):
    at, where = 0, {}
    for name, rows, cols in parts:
        where[name] = (rows, at, cols)
        at += cols
    return where, at


PARTS = [
    ("ident", 128, 128), ("center2", 128, 128), ("mean2", 128, 128), ("mean128", 128, 128),
    ("rot", 128, 256), ("pick", 128, 128), ("rot64", 64, 64), ("e0", 128, 1), ("e0row", 1, 128), ("vbmask", 98, 64),
    ("headmask", 128, 8), ("vones", 98, 144), ("winmask", 128, 196), ("den", 128, 1), ("revidx", 128, 32), ("big", 32, 512),
    ("pe_w", 128, 32), ("pe_b", 128, 1), ("pe_g", 128, 1), ("pe_nb", 128, 1),
    *[(f"{n}{l}", r, c) for l in range(2) for n, r, c in (
        ("wq", 128, 128), ("wk", 128, 128), ("wv", 128, 128), ("wp", 64, 128), ("w1", 128, 512), ("w2", 128, 128),
        ("n1g", 128, 1), ("n1b", 128, 1), ("n2g", 128, 1), ("n2b", 128, 1), ("bq", 128, 1), ("bk", 128, 1), ("bv", 128, 1),
        ("bp", 128, 1), ("b1", 128, 2), ("b2", 128, 1), ("rpb", 128, 392))],
    ("awq", 64, 64), ("awk", 64, 64), ("awv", 64, 64), ("abq", 64, 1), ("abk", 64, 1), ("abv", 1, 64),
    ("rw", 65, 32), ("fw1", 65, 512), ("fw2", 128, 256), ("fb2", 32, 64),
    ("tw1", 64, 896), ("tw2", 128, 320), ("tw3", 64, 3), ("tb1", 128, 1), ("tb2", 64, 1), ("tb3", 128, 1),
    ("emb", 64, 68), ("cpos", 128, 64), ("bpos", 128, 1), ("widths", 128, 4), ("scales", 128, 4), ("chan", 64, 1),
]
WHERE, PACKED = pack_columns(PARTS)


def shape_constants():
    import numpy as np
    eye, c = np.eye(CH), {}
    two = lambda m: np.kron(np.eye(2), m)
    c["ident"] = np.eye(128)
    c["center2"] = two(eye - 1.0 / CH)
    c["mean2"] = two(np.full((CH, CH), 1.0 / CH))
    c["mean128"] = np.full((128, 128), 1.0 / 128)
    u = np.full(CH, 1.0 / np.sqrt(CH))
    v = u.copy()
    v[0] -= 1.0
    house = eye - 2.0 * np.outer(v, v) / (v @ v)
    house[0, :] = 0.0
    c["rot"] = np.concatenate([np.concatenate([np.tile(house.T, (1, 2)) if j == i else np.zeros((CH, 128)) for j in range(2)]) for i in range(2)], 1)
    c["pick"] = np.concatenate([np.concatenate([eye if j == i else np.zeros((CH, CH)) for j in range(2)]) for i in range(2)], 1)
    c["rot64"] = house.T
    e0 = np.zeros((128, 1))
    e0[0] = 1.0
    c["e0"] = e0
    c["e0row"] = np.zeros((1, 128))
    c["e0row"][0, [0, 64]] = 1.0
    c["den"] = c["e0row"].T
    row2 = np.repeat(np.arange(2), WTOK)
    vm = (row2[:, None, None] == np.arange(2)[None, :, None]) * np.ones((1, 1, 8))
    c["vbmask"] = np.tile(vm.reshape(98, 16), (1, 4))
    on = np.zeros((98, 4, 2, 18))
    on[:, :, :, 16:] = (row2[:, None] == np.arange(2)[None, :])[:, None, None, :]
    c["vones"] = on.reshape(98, 144)
    c["headmask"] = (np.arange(128)[:, None] % CH // 8 == np.arange(8)[None, :]) * 1.0
    shift = WIN // 2
    part = lambda last: np.where(np.arange(WIN) < WIN - shift, 0, 1) if last else np.zeros(WIN, int)
    wm = np.zeros((128, 4, WTOK))
    for rt in range(2):
        for ct in range(2):
            g = (part(rt)[:, None] * 2 + part(ct)[None, :]).reshape(-1)
            m = np.where(g[:, None] != g[None, :], -100.0, 0.0)
            wm[0:WTOK, rt * 2 + ct] = m
            wm[64:64 + WTOK, rt * 2 + ct] = m
    c["winmask"] = wm.reshape(128, 196)
    c["revidx"] = np.tile(float(EXPERTS) - np.arange(EXPERTS), (128, 1))
    c["big"] = (np.arange(32)[:, None] == np.arange(512)[None, :] // EH) * float(2.0 ** 100)
    c["bpos"] = np.tile(np.linspace(0.0, 1.0, TXT, dtype=np.float32)[:, None], (4, 1))
    c["chan"] = np.arange(CH)[:, None] * 1.0
    return {k: np.asarray(v, np.float32) for k, v in c.items()}


def windows_first(img):
    s = img.shape[:-2]
    a = img.reshape(*s, STRIPS, WIN, STRIPS, WIN)
    k = len(s)
    return a.transpose(*range(k), k, k + 2, k + 1, k + 3)


def lay_out(x, inp):
    import numpy as np
    f = lambda n: np.asarray(inp[n])
    p = dict(shape_constants())

    def diag2(m):
        z = np.zeros((2 * m.shape[0], 2 * m.shape[1]), np.float32)
        z[:m.shape[0], :m.shape[1]] = m
        z[m.shape[0]:, m.shape[1]:] = m
        return z

    twice = lambda v: np.concatenate([v, v]).reshape(128, -1)
    p["pe_w"] = diag2(f("L0_tok_pe_w").reshape(CH, 16))
    p["pe_b"], p["pe_g"], p["pe_nb"] = twice(f("L0_tok_pe_b")), twice(f("L0_tok_pe_ng")), twice(f("L0_tok_pe_nb"))
    for l in range(2):
        qkv, qb = f("L0_tok_qkv_w")[l].reshape(3, CH, CH), f("L0_tok_qkv_b")[l].reshape(3, CH)
        for i, n in enumerate("qkv"):
            p[f"w{n}{l}"], p[f"b{n}{l}"] = diag2(qkv[i].T), twice(qb[i])
        p[f"wp{l}"] = np.concatenate([f("L0_tok_proj_w")[l].T] * 2, 1)
        p[f"bp{l}"] = twice(f("L0_tok_proj_b")[l])
        w1 = f("L0_tok_w1")[l].T
        z = np.zeros((2, CH, 2, 2, 128), np.float32)
        for i in range(2):
            z[i, :, i] = w1.reshape(CH, 2, 128)
        p[f"w1{l}"] = z.reshape(128, 512)
        p[f"w2{l}"] = f("L0_tok_w2")[l].T.reshape(2, 128, CH).transpose(1, 0, 2).reshape(128, 128)
        p[f"b1{l}"] = f("L0_tok_b1")[l].reshape(2, 128).T
        for n in ("n1g", "n1b", "n2g", "n2b", "b2"):
            p[f"{n}{l}"] = twice(f("L0_tok_" + n)[l])
        t = f("L0_tok_rpb")[l].T.reshape(HEADS, 13, 13)
        b = np.zeros((128, HEADS, WIN, WIN), np.float32)
        for qr in range(WIN):
            for qc in range(WIN):
                piece = t[:, qr:qr + WIN, qc:qc + WIN][:, ::-1, ::-1]
                b[qr * WIN + qc] = piece
                b[64 + qr * WIN + qc] = piece
        p[f"rpb{l}"] = b.reshape(128, 392)
    p["awq"], p["awk"], p["awv"] = f("L0_attn_Wq").T, f("L0_attn_Wk").T, f("L0_attn_Wv").T
    p["abq"], p["abk"], p["abv"] = f("L0_attn_bq")[:, None], f("L0_attn_bk")[:, None], f("L0_attn_bv")[None, :]
    p["rw"] = np.concatenate([f("L0_ffn_router_w").T, f("L0_ffn_router_b")[None, :]])
    p["fw1"] = np.concatenate([f("L0_ffn_W1").transpose(1, 0, 2).reshape(CH, 512), f("L0_ffn_b1").reshape(1, 512)])
    p["fw2"] = f("L0_ffn_W2").reshape(4, 128, CH).transpose(1, 0, 2).reshape(128, 256)
    p["fb2"] = f("L0_ffn_b2")
    p["tw1"] = f("L0_txt_w1").transpose(1, 2, 0).reshape(64, 7 * 128)
    p["tw2"] = f("L0_txt_w2").transpose(1, 2, 0).reshape(128, 5 * 64)
    p["tw3"] = f("L0_txt_w3")[0]
    p["tb1"], p["tb2"] = f("L0_txt_b1")[:, None], f("L0_txt_b2")[:, None]
    p["tb3"] = np.broadcast_to(f("L0_txt_b3").reshape(1, 1), (128, 1))
    p["emb"] = np.concatenate([f("L0_txt_emb"), f("L0_txt_locality_shapes")], 1)
    cp = f("fside_BS_continuous_positions")
    p["cpos"] = np.broadcast_to(cp.reshape(2, 4, 1, TXT).transpose(1, 2, 0, 3), (4, TXT, 2, TXT)).reshape(128, 64)
    p["widths"] = np.broadcast_to(f("L0_txt_multiscale_widths")[None, :], (128, 4))
    p["scales"] = np.broadcast_to(f("L0_txt_scale_weights")[None, :], (128, 4))
    packed = np.zeros((128, PACKED), np.float32)
    for name, (rows, at, cols) in WHERE.items():
        packed[0:rows, at:at + cols] = p[name]
    a = np.asarray(x).reshape(PAIRS, 2, SIDE, 4, SIDE, 4).transpose(1, 3, 5, 0, 2, 4)
    patches = np.ascontiguousarray(windows_first(a)).reshape(32, UNITS * UTOK)
    text = np.ascontiguousarray(np.broadcast_to(np.asarray(inp["x_txt"]).reshape(1, IMG * TXT), (64, IMG * TXT)))
    return packed, patches, text
def program(nc, packed, patches, text, out):
    import concourse.bass as bass
    from concourse import mybir
    from contextlib import ExitStack
    with ExitStack() as ctx:
        keep = {}
        fp32 = mybir.dt.float32

        def sb(name, cols, dt=fp32, rows=128):
            keep[name] = ctx.enter_context(nc.sbuf_tensor(name, [rows, cols], dt))

        sb("W", PACKED)
        sb("X", PAIRS * TOK)
        for l in range(2):
            for n, c in (("wq", 128), ("wk", 128), ("wv", 128), ("w1", 512), ("bq", 1), ("bk", 1), ("bv", 1), ("bp", 1), ("b1", 2)):
                sb(f"{n}g{l}", c)
        sb("winbias", 4 * 392)
        sb("peT", 128, rows=32)
        sb("peb", 1)
        sb("MH", 128, mybir.dt.float32r)
        sb("ML", 128, mybir.dt.float32r)
        sb("LT", 65)
        setup_phase(nc, keep, packed)
        with nc.sbuf_tensor("Y", [128, PAIRS * TOK], fp32) as spare:
            streams = [(spare, keep["X"]), (keep["X"], spare)]
            keep["X"], keep["XN"] = streams[0]
            embed_phase(nc, keep, patches)
            text_phase(nc, keep, text)
            for l in range(2):
                attention_phase(nc, keep, l)
                mlp_phase(nc, keep, l)
                if l == 0:
                    roll_phase(nc, keep)
                    keep["X"], keep["XN"] = streams[1]
        global_phase(nc, keep, out)


def setup_phase(nc, keep, packed):
    from contextlib import ExitStack
    from concourse import mybir
    fp32, f32r = mybir.dt.float32, mybir.dt.float32r
    ALU = mybir.AluOpType
    W = keep["W"]

    def w(name, a=0, b=None):
        rows, at, cols = WHERE[name]
        return W[0:rows, at + a:at + (cols if b is None else b)]

    with ExitStack() as ctx:
        loaded, pe_one, dve_one, pe_two, chain = (ctx.enter_context(nc.semaphore("set_" + n)) for n in ("loaded", "pe_one", "dve_one", "pe_two", "chain"))
        ps = [ctx.enter_context(nc.psum_tensor(f"set_ps{i}", [128, 512], fp32)) for i in range(5)]
        GG = ctx.enter_context(nc.sbuf_tensor("set_G", [64, 128], fp32))
        JJ = ctx.enter_context(nc.sbuf_tensor("set_J", [64, 128], fp32))
        M32 = ctx.enter_context(nc.sbuf_tensor("set_M", [128, 128], fp32))
        block = ctx.enter_context(nc.Block())

        @block.sync
        def _(sp):
            half = PACKED // 2
            sp.dma_start(W[:, 0:half], packed[:, 0:half]).then_inc(loaded, 16)
            sp.dma_start(W[:, half:PACKED], packed[:, half:PACKED]).then_inc(loaded, 16)

        @block.tensor
        def _(pe):
            pe.wait_ge(loaded, 32)
            mm = nc.tensor.matmul
            mm(ps[0][:, 0:1], w("center2"), w("pe_b"), start=True, stop=True)
            for l in range(2):
                for i, n in enumerate(("wq", "wk", "wv")):
                    mm(ps[0][:, 1 + 8 * l + i:2 + 8 * l + i], w(f"{n}{l}"), w(f"n1b{l}"), start=True, stop=True)
                for h in range(2):
                    mm(ps[0][:, 4 + 8 * l + h:5 + 8 * l + h], w(f"w1{l}", 128 * h, 128 * h + 128), w(f"n2b{l}"), start=True, stop=True)
            mm(ps[1][0:32, 0:128], w("pe_w"), w("center2"), start=True, stop=True)
            mm(ps[2][0:64, 0:64], w("awq"), w("rot64"), start=True, stop=True)
            mm(ps[2][0:64, 64:128], w("awk"), w("rot64"), start=True, stop=True)
            mm(ps[3][:, 0:64], w("rot", 0, 128)[0:64, :], w("awv"), start=True, stop=False)
            mm(ps[3][:, 0:64], w("e0row"), w("abv"), start=False, stop=True).then_inc(pe_one, 1)
            pe.wait_ge(dve_one, 1)
            for l in range(2):
                mm(ps[0][:, 20 + l:21 + l], w(f"wp{l}"), keep[f"bvg{l}"][0:64, :], start=True, stop=True)
            mm(ps[4][:, 0:128], GG[:, :], JJ[:, :], start=True, stop=True).then_inc(pe_two, 1)

        @block.vector
        def _(dve):
            v = nc.vector
            dve.wait_ge(loaded, 32)
            for l in range(2):
                for n in ("wq", "wk", "wv"):
                    v.tensor_scalar(keep[f"{n}g{l}"][:, :], w(f"{n}{l}"), w(f"n1g{l}"), None, ALU.mult)
                v.tensor_scalar(keep[f"w1g{l}"][:, :], w(f"w1{l}"), w(f"n2g{l}"), None, ALU.mult)
            for kind in range(4):
                v.tensor_tensor(keep["winbias"][:, kind * 392:(kind + 1) * 392].rearrange("p (h k) -> p h k", h=HEADS),
                                w("rpb1").rearrange("p (h k) -> p h k", h=HEADS),
                                w("winmask", kind * WTOK, (kind + 1) * WTOK).unsqueeze(1).to_broadcast([128, HEADS, WTOK]), ALU.add)
            v.tensor_copy(keep["LT"][:, 64:65], w("den"))
            dve.wait_ge(pe_one, 1)
            v.tensor_copy(keep["peb"][:, :], ps[0][:, 0:1])
            v.tensor_copy(keep["peT"][:, :], ps[1][0:32, 0:128])
            for l in range(2):
                c = 1 + 8 * l
                v.tensor_scalar(keep[f"bqg{l}"][:, :], ps[0][:, c:c + 1], w(f"bq{l}"), float(8 ** -0.5), ALU.add, ALU.mult)
                v.tensor_scalar(keep[f"bkg{l}"][:, :], ps[0][:, c + 1:c + 2], w(f"bk{l}"), None, ALU.add)
                v.tensor_scalar(keep[f"bvg{l}"][:, :], ps[0][:, c + 2:c + 3], w(f"bv{l}"), None, ALU.add)
                v.tensor_tensor(keep[f"b1g{l}"][:, :], ps[0][:, c + 3:c + 5], w(f"b1{l}"), ALU.add)
            v.tensor_copy(keep["LT"][:, 0:64], ps[3][:, 0:64])
            for i in range(2):
                v.tensor_copy(GG[:, 64 * i + 1:64 * i + 64], ps[2][0:64, 1:64])
                v.tensor_copy(GG[:, 64 * i:64 * i + 1], w("abq"))
                v.tensor_copy(JJ[:, 64 * i + 1:64 * i + 64], ps[2][0:64, 65:128])
                last = v.tensor_copy(JJ[:, 64 * i:64 * i + 1], w("abk"))
            last.then_inc(dve_one, 1)
            dve.wait_ge(pe_two, 1)
            for l in range(2):
                v.tensor_scalar(keep[f"bpg{l}"][:, :], ps[0][:, 20 + l:21 + l], w(f"bp{l}"), None, ALU.add)
            v.tensor_scalar(M32[:, :], ps[4][:, 0:128], float(CH ** -0.5), None, ALU.mult)
            v.tensor_scalar(keep["MH"][:, :], ps[4][:, 0:128], float(CH ** -0.5), None, ALU.mult).then_inc(chain, 1)
            dve.wait_ge(chain, 1)
            v.tensor_tensor(keep["ML"][:, :], M32[:, :], keep["MH"][:, :].bitcast(fp32), ALU.subtract)


def unit_at(u):
    return u * UTOK + (u // STRIPS) * TXT


def embed_phase(nc, keep, patches):
    from contextlib import ExitStack
    import concourse.bass as bass
    from concourse import mybir
    fp32, ALU, ACT = mybir.dt.float32, mybir.AluOpType, mybir.ActivationFunctionType
    W, X, XN, peT, peb = keep["W"], keep["X"], keep["XN"], keep["peT"], keep["peb"]

    def w(name):
        rows, at, cols = WHERE[name]
        return W[0:rows, at:at + cols]

    with ExitStack() as ctx:
        sem = lambda n: ctx.enter_context(nc.semaphore("emb_" + n))
        loaded, pe_xc, act_sq, pe_var, act_ln, act_rs, dve_t, dve_x, eps_set = map(sem, "loaded pe_xc act_sq pe_var act_ln act_rs dve_t dve_x eps_set".split())
        buf = lambda n: [ctx.enter_context(nc.sbuf_tensor(f"emb_{n}{i}", [128, UTOK], fp32)) for i in range(2)]
        sq, ln, rs, t = buf("sq"), buf("ln"), buf("rs"), buf("t")
        eps = ctx.enter_context(nc.sbuf_tensor("emb_eps", [128, 1], fp32))
        bank = lambda n: [ctx.enter_context(nc.psum_tensor(f"emb_{n}{i}", [128, 512], fp32)) for i in range(2)]
        xc, var = bank("xc"), bank("var")
        block = ctx.enter_context(nc.Block())
        n_cols = UNITS * UTOK

        @block.sync
        def _(sp):
            sp.dma_start(XN[0:32, 0:n_cols], patches).then_inc(loaded, 16)

        def embed(pe, u, par):
            if not isinstance(u, int) or u >= 2:
                pe.wait_ge(dve_t, u - 1)
            nc.tensor.matmul(xc[par][:, 0:UTOK], peT[:, :], XN[0:32, bass.ds(u * UTOK, UTOK)], start=True, stop=True).then_inc(pe_xc, 1)

        def variance(pe, u, par):
            pe.wait_ge(act_sq, u + 1)
            nc.tensor.matmul(var[par][:, 0:UTOK], w("mean2"), sq[par][:, :], start=True, stop=True).then_inc(pe_var, 1)

        @block.tensor
        def _(pe):
            pe.wait_ge(loaded, 16)
            embed(pe, 0, 0)
            embed(pe, 1, 1)
            variance(pe, 0, 0)
            with pe.Fori(0, UNITS // 2 - 1) as i:
                for k in range(2):
                    embed(pe, i * 2 + (k + 2), k)
                    variance(pe, i * 2 + (k + 1), 1 - k)
            variance(pe, UNITS - 1, 1)

        def act_step(act, u, par, head):
            if head:
                act.wait_ge(pe_xc, u + 1)
                if not isinstance(u, int) or u >= 2:
                    act.wait_ge(pe_var, u - 1)
                nc.scalar.activation(sq[par][:, :], xc[par][:, 0:UTOK], ACT.Square, bias=peb[:, :]).then_inc(act_sq, 1)
            else:
                act.wait_ge(pe_var, u + 1)
                nc.scalar.activation(ln[par][:, :], var[par][:, 0:UTOK], ACT.Ln, bias=eps[:, :]).then_inc(act_ln, 1)
                act.wait_ge(act_ln, u + 1)
                if not isinstance(u, int) or u >= 2:
                    act.wait_ge(dve_t, u - 1)
                nc.scalar.activation(rs[par][:, :], ln[par][:, :], ACT.Exp, scale=-0.5).then_inc(act_rs, 1)

        @block.scalar
        def _(act):
            nc.scalar.preload_act_table_set("natural_log_exp_and_others")
            act.wait_ge(eps_set, 1)
            act_step(act, 0, 0, True)
            act_step(act, 1, 1, True)
            act_step(act, 0, 0, False)
            with act.Fori(0, UNITS // 2 - 1) as i:
                for k in range(2):
                    act_step(act, i * 2 + (k + 2), k, True)
                    act_step(act, i * 2 + (k + 1), 1 - k, False)
            act_step(act, UNITS - 1, 1, False)

        @block.vector
        def _(dve):
            nc.vector.memset(eps[:, :], EPS).then_inc(eps_set, 1)

            def step(u, par):
                dve.wait_ge(act_rs, u + 1)
                if not isinstance(u, int) or u >= 2:
                    dve.wait_ge(dve_x, u - 1)
                nc.vector.scalar_tensor_tensor(t[par][:, :], xc[par][:, 0:UTOK], peb[:, :], rs[par][:, :], ALU.add, ALU.mult).then_inc(dve_t, 1)
                dve.wait_ge(dve_t, u + 1)
                nc.vector.tensor_scalar(X[:, bass.ds(unit_at(u), UTOK)], t[par][:, :], w("pe_g"), w("pe_nb"), ALU.mult, ALU.add).then_inc(dve_x, 1)

            step(0, 0)
            step(1, 1)
            with dve.Fori(0, UNITS // 2 - 1) as i:
                for k in range(2):
                    step(i * 2 + (k + 2), k)


def text_phase(nc, keep, text):
    from contextlib import ExitStack
    import math
    from concourse import mybir
    fp32, i32, ALU, ACT = mybir.dt.float32, mybir.dt.int32, mybir.AluOpType, mybir.ActivationFunctionType
    AXX = mybir.AxisListType.X
    W, X = keep["W"], keep["X"]
    GROUPS, SC, ROUND = 2, 4, float(3 << 22)

    def w(name, a=0, b=None):
        rows, at, cols = WHERE[name]
        return W[0:rows, at + a:at + (cols if b is None else b)]

    with ExitStack() as ctx:
        sem = lambda n: ctx.enter_context(nc.semaphore("txt_" + n))
        loaded, zeroed, coded, pe_c1, act_h1, pe_c2, act_h2, pe_nat, act_gate, dve_z, act_wave, dve_amp, pe_field, link = map(
            sem, "loaded zeroed coded pe_c1 act_h1 pe_c2 act_h2 pe_nat act_gate dve_z act_wave dve_amp pe_field link".split())
        tile = lambda n, c, dt=fp32, r=128: ctx.enter_context(nc.sbuf_tensor("txt_" + n, [r, c], dt))
        tok, tokf = tile("tok", IMG * TXT, i32, 64), tile("tokf", IMG * TXT, r=64)
        code, h1, h2 = tile("code", IMG * (TXT + 6), r=64), tile("h1", IMG * (TXT + 4)), tile("h2", IMG * (TXT + 2), r=64)
        code3, h13, h23 = (t[:, :].rearrange("c (b s) -> c b s", b=IMG) for t in (code, h1, h2))
        emb, lp, gate, amp = tile("emb", 128), tile("lp", 8), tile("gate", 2), tile("amp", 2)
        center, absw, widths, inv, phase, sw2 = tile("center", 2), tile("absw", 2), tile("widths", 8), tile("inv", 8), tile("phase", 2), tile("sw2", 4)
        xd, z, z2, r, whole, frac, basis, wave = tile("xd", 64), tile("z", 256), tile("z2", 256), tile("r", 256), tile("whole", 256), tile("frac", 256), tile("basis", 256), tile("wave", 256)
        field, xr = tile("field", 64), tile("xr", 256)
        ps = [ctx.enter_context(nc.psum_tensor(f"txt_ps{i}", [128, 512], fp32)) for i in range(7)]
        nat = ps[2][:, 0:160].rearrange("p (g c) -> p g c", g=GROUPS)
        block = ctx.enter_context(nc.Block())

        @block.sync
        def _(sp):
            sp.dma_start(tok[:, :], text).then_inc(loaded, 16)

        @block.gpsimd
        def _(pool):
            nc.gpsimd.memset(code[:, :], 0.0).then_inc(zeroed, 1)
            nc.gpsimd.memset(h1[:, :], 0.0).then_inc(zeroed, 1)
            nc.gpsimd.memset(h2[:, :], 0.0).then_inc(zeroed, 1)

        @block.tensor
        def _(pe):
            mm = nc.tensor.matmul
            pe.wait_ge(coded, 1)
            for k in range(7):
                last = mm(ps[0][:, 0:256], w("tw1", 128 * k, 128 * k + 128), code3[:, :, k:k + TXT], start=k == 0, stop=k == 6)
            last.then_inc(pe_c1, 1)
            pe.wait_ge(act_h1, 1)
            for k in range(5):
                last = mm(ps[1][0:64, 0:256], w("tw2", 64 * k, 64 * k + 64), h13[:, :, k:k + TXT], start=k == 0, stop=k == 4)
            last.then_inc(pe_c2, 1)
            pe.wait_ge(act_h2, 1)
            for g in range(GROUPS):
                for j in range(4):
                    image, at = 4 * g + j, slice(32 * j, 32 * j + 32)
                    mm(nat[at, g, 0:68], code3[:, image, 3:3 + TXT], w("emb"), start=True, stop=True)
                    for k in range(3):
                        last = mm(nat[at, g, 68:69], h23[:, image, k:k + TXT], w("tw3", k, k + 1), start=k == 0, stop=k == 2)
            last.then_inc(pe_nat, 1)
            pe.wait_ge(dve_amp, 1)
            for g in range(GROUPS):
                for j in range(4):
                    at, i = slice(32 * j, 32 * j + 32), j % 2
                    last = mm(ps[3 + j][64 * i:64 * i + 64, 32 * g:32 * g + 32], emb[at, 64 * g:64 * g + 64], field[at, 32 * g:32 * g + 32], start=True, stop=True)
            last.then_inc(pe_field, 1)

        @block.scalar
        def _(act):
            a = nc.scalar.activation
            act.wait_ge(zeroed, 3)
            act.wait_ge(pe_c1, 1)
            a(h13[:, :, 2:2 + TXT], ps[0][:, 0:256].rearrange("c (b s) -> c b s", b=IMG), ACT.Gelu, bias=w("tb1")).then_inc(act_h1, 1)
            act.wait_ge(pe_c2, 1)
            a(h23[:, :, 1:1 + TXT], ps[1][0:64, 0:256].rearrange("c (b s) -> c b s", b=IMG), ACT.Gelu, bias=w("tb2")).then_inc(act_h2, 1)
            act.wait_ge(pe_nat, 1)
            a(gate[:, :], nat[:, :, 68], ACT.Sigmoid, bias=w("tb3")).then_inc(act_gate, 1)
            a(amp[:, :], nat[:, :, 66], ACT.Sigmoid).then_inc(act_gate, 1)
            act.wait_ge(dve_z, 1)
            a(basis[:, :], z2[:, :], ACT.Exp, scale=-0.5).then_inc(act_wave, 1)
            act.wait_ge(dve_z, 2)
            a(wave[:, :], frac[:, :], ACT.Sin, scale=2.0 * math.pi).then_inc(act_wave, 1)

        @block.vector
        def _(dve):
            v, n = nc.vector, [0]

            def linked(ins):
                n[0] += 1
                ins.then_inc(link, 1)
                dve.wait_ge(link, n[0])

            dve.wait_ge(loaded, 16)
            linked(v.tensor_copy(tokf[:, :], tok[:, :]))
            dve.wait_ge(zeroed, 3)
            v.tensor_scalar(code3[:, :, 3:3 + TXT], tokf[:, :].rearrange("c (b s) -> c b s", b=IMG), w("chan"), None, ALU.is_equal).then_inc(coded, 1)
            dve.wait_ge(act_gate, 2)
            v.tensor_copy(emb[:, :].rearrange("p (g c) -> p g c", g=GROUPS), nat[:, :, 0:64])
            linked(v.tensor_copy(lp[:, :].rearrange("p (g c) -> p g c", g=GROUPS), nat[:, :, 64:68]))
            lp3 = lp[:, :].rearrange("p (g c) -> p g c", g=GROUPS)
            v.tensor_scalar(center[:, :], lp3[:, :, 0], 0.05, w("bpos"), ALU.mult, ALU.add)
            v.tensor_scalar(phase[:, :], lp3[:, :, 3], 0.5, 0.25, ALU.mult, ALU.add)
            v.tensor_tensor(sw2[:, :], w("scales"), w("scales"), ALU.mult)
            linked(v.scalar_tensor_tensor(absw[:, :], lp3[:, :, 1], -1.0, lp3[:, :, 1], ALU.mult, ALU.max))
            linked(v.tensor_tensor(widths[:, :].rearrange("p (g s) -> p g s", g=GROUPS), absw[:, :].unsqueeze(2).to_broadcast([128, 2, SC]),
                                   w("widths").unsqueeze(1).to_broadcast([128, 2, SC]), ALU.mult))
            linked(v.tensor_scalar(inv[:, :], widths[:, :], 1e-5, None, ALU.add))
            linked(v.reciprocal(widths[:, :], inv[:, :]))
            linked(v.tensor_tensor(xd[:, :].rearrange("p (g t) -> p g t", g=GROUPS), w("cpos").rearrange("p (g t) -> p g t", g=GROUPS),
                                   center[:, :].unsqueeze(2).to_broadcast([128, 2, TXT]), ALU.subtract))
            for g in range(GROUPS):
                last = v.tensor_tensor(z[:, 128 * g:128 * g + 128].rearrange("p (s t) -> p s t", s=SC),
                                       xd[:, TXT * g:TXT * g + TXT].unsqueeze(1).to_broadcast([128, SC, TXT]),
                                       widths[:, SC * g:SC * g + SC].unsqueeze(2).to_broadcast([128, SC, TXT]), ALU.mult)
            linked(last)
            v.tensor_tensor(z2[:, :], z[:, :], z[:, :], ALU.mult).then_inc(dve_z, 1)
            linked(v.tensor_tensor(r[:, :].rearrange("p (g t) -> p g t", g=GROUPS), z[:, :].rearrange("p (g t) -> p g t", g=GROUPS),
                                   phase[:, :].unsqueeze(2).to_broadcast([128, 2, SC * TXT]), ALU.add))
            linked(v.tensor_scalar(whole[:, :], r[:, :], ROUND, ROUND, ALU.add, ALU.subtract))
            linked(v.tensor_tensor(xr[:, :], r[:, :], whole[:, :], ALU.subtract))
            v.tensor_scalar(frac[:, :], xr[:, :], -0.4999999, 0.4999999, ALU.max, ALU.min).then_inc(dve_z, 1)
            dve.wait_ge(act_wave, 2)
            linked(v.tensor_tensor(z[:, :], basis[:, :], wave[:, :], ALU.mult))
            for g in range(GROUPS):
                last = v.tensor_tensor(r[:, 128 * g:128 * g + 128].rearrange("p (s t) -> p s t", s=SC), z[:, 128 * g:128 * g + 128].rearrange("p (s t) -> p s t", s=SC),
                                       sw2[:, :].unsqueeze(2).to_broadcast([128, SC, TXT]), ALU.mult)
            linked(last)
            for g in range(GROUPS):
                v.tensor_reduce(xd[:, TXT * g:TXT * g + TXT], r[:, 128 * g:128 * g + 128].rearrange("p (s t) -> p t s", s=SC), AXX, ALU.add)
            linked(v.tensor_tensor(phase[:, :], gate[:, :], amp[:, :], ALU.mult))
            v.tensor_tensor(field[:, :].rearrange("p (g t) -> p g t", g=GROUPS), xd[:, :].rearrange("p (g t) -> p g t", g=GROUPS),
                            phase[:, :].unsqueeze(2).to_broadcast([128, 2, TXT]), ALU.mult).then_inc(dve_amp, 1)
            dve.wait_ge(pe_field, 1)
            for g in range(GROUPS):
                for j in range(4):
                    pair, i = 2 * g + j // 2, j % 2
                    at = pair * TOK + SIDE * SIDE
                    v.tensor_copy(X[64 * i:64 * i + 64, at:at + TXT], ps[3 + j][64 * i:64 * i + 64, 32 * g:32 * g + 32])
def attention_phase(nc, keep, l):
    from contextlib import ExitStack
    import concourse.bass as bass
    from concourse import mybir
    fp32, ALU, ACT = mybir.dt.float32, mybir.AluOpType, mybir.ActivationFunctionType
    AXX = mybir.AxisListType.X
    W, X, XN = keep["W"], keep["X"], keep["XN"]
    QSCALE = float((CH // HEADS) ** -0.5)
    HP = HEADS // 2

    def w(name, a=0, b=None):
        rows, at, cols = WHERE[name]
        return W[0:rows, at + a:at + (cols if b is None else b)]

    g = lambda name: keep[f"{name}{l}"][:, :]
    with ExitStack() as ctx:
        sem = lambda n: ctx.enter_context(nc.semaphore(f"att{l}_{n}"))
        pe_xc, act_sq, pe_var, act_ln, act_rs, dve_xn, pe_q, act_q, pe_k, dve_k, pe_v, dve_v = map(
            sem, "pe_xc act_sq pe_var act_ln act_rs dve_xn pe_q act_q pe_k dve_k pe_v dve_v".split())
        pool_kx, pe_s, dve_add, dve_max, pool_sub, act_exp, pe_tr, act_pt, pe_pv, dve_r, dve_o = map(
            sem, "pool_kx pe_s dve_add dve_max pool_sub act_exp pe_tr act_pt pe_pv dve_r dve_o".split())
        pe_ot, act_ot, pe_pr, dve_x, pe_xc2, act_sq2, pe_var2, act_ln2, act_rs2, dve_xn2, ready, pe_go = map(
            sem, "pe_ot act_ot pe_pr dve_x pe_xc2 act_sq2 pe_var2 act_ln2 act_rs2 dve_xn2 ready pe_go".split())
        tile = lambda n, c, r=128: ctx.enter_context(nc.sbuf_tensor(f"att{l}_{n}", [r, c], fp32))
        sq, ln, rs, ksb = tile("sq", UTOK), tile("ln", UTOK), tile("rs", UTOK), tile("ksb", UTOK)
        xn = tile("xn", 2 * UTOK)
        qbd = [tile(f"qbd{i}", STRIPS * 128) for i in range(2)]
        kx = [tile(f"kx{i}", HEADS * WTOK) for i in range(4)]
        vx = [tile(f"vx{i}", STRIPS * 144, 2 * WTOK) for i in range(2)]
        t, m = [tile(f"t{i}", 392) for i in range(2)], [tile(f"m{i}", HEADS) for i in range(2)]
        t2, e = [tile(f"t2{i}", 392) for i in range(2)], [tile(f"e{i}", 392) for i in range(2)]
        pt = [tile(f"pt{i}", HP * 128, 2 * WTOK) for i in range(2)]
        rden = tile("rden", 16)
        o = tile("o", STRIPS * CH)
        ot = tile("ot", 2 * UTOK, CH)
        sq2, ln2, rs2, eps = tile("sq2", UTOK), tile("ln2", UTOK), tile("rs2", UTOK), tile("eps", 1)
        bank = lambda n: ctx.enter_context(nc.psum_tensor(f"att{l}_ps_{n}", [128, 512], fp32))
        ps_s, ps_pt, ps_o = [bank("s0"), bank("s1")], bank("pt"), bank("o")
        ps_a, ps_b, ps_c, ps_d = bank("a"), bank("b"), bank("c"), bank("d")
        xn4 = xn[:, :].rearrange("p (w r k) -> p w r k", w=STRIPS, r=2)
        by_window = lambda ap: ap.rearrange("p (w k) -> p w k", w=STRIPS)
        by_head = lambda ap: ap.rearrange("p (h k) -> p h k", h=HEADS)
        o3 = o[:, :].rearrange("p (w c) -> p w c", w=STRIPS)
        ot4 = ot[:, :].rearrange("c (i w k) -> c i w k", i=2, w=STRIPS)
        block = ctx.enter_context(nc.Block())

        @block.tensor
        def _(pe):
            mm = nc.tensor.matmul
            ident = w("ident")

            def deviations(u):
                if not (isinstance(u, int) and u == 0):
                    pe.wait_ge(dve_v, 2 * u - 1)
                mm(ps_a[:, 0:UTOK], w("center2"), X[:, bass.ds(unit_at(u), UTOK)], start=True, stop=True).then_inc(pe_xc, 1)

            def variance(u):
                pe.wait_ge(act_sq, u + 1)
                if not (isinstance(u, int) and u == 0):
                    pe.wait_ge(dve_v, 2 * u)
                mm(ps_b[:, 0:UTOK], w("mean2"), sq[:, :], start=True, stop=True).then_inc(pe_var, 1)

            def query_key(u):
                pe.wait_ge(dve_xn, u + 1)
                mm(ps_a[:, 0:UTOK], g("wqg"), xn4[:, :, 0, :], start=True, stop=True).then_inc(pe_q, 1)
                mm(ps_b[:, 0:UTOK], g("wkg"), xn4[:, :, 0, :], start=True, stop=True).then_inc(pe_k, 1)

            def values(u, half):
                pe.wait_ge(*((act_q, 2 * (u + 1)) if half == 0 else (dve_k, u + 1)))
                for k in range(4):
                    at = (4 * half + k) * 2 * WTOK
                    last = mm((ps_a, ps_b)[half][0:2 * WTOK, 128 * k:128 * k + 128], xn[:, at:at + 2 * WTOK], g("wvg"), start=True, stop=True)
                last.then_inc(pe_v, 1)

            def scores(u, wi, p):
                n = u * 8 + wi
                pe.wait_ge(pool_kx, n + 1)
                if wi == 0:
                    pe.wait_ge(act_q, 2 * (u + 1))
                if not (isinstance(u, int) and u == 0 and wi < 2):
                    pe.wait_ge(dve_add, n - 1)
                mm(ps_s[wi % 2][:, 0:392], qbd[p][:, 128 * wi:128 * wi + 128], kx[wi % 4][:, :], start=True, stop=True).then_inc(pe_s, 1)

            def transposes(u, wi):
                n = u * 8 + wi
                pe.wait_ge(act_exp, n + 1)
                if not (isinstance(u, int) and u == 0 and wi == 0):
                    pe.wait_ge(act_pt, n)
                for hp in range(HP):
                    last = nc.tensor.transpose(ps_pt[0:98, 128 * hp:128 * hp + 128], e[wi % 2][:, 98 * hp:98 * hp + 98], ident)
                last.then_inc(pe_tr, 1)

            def weighted(u, wi, p):
                n = u * 8 + wi
                pe.wait_ge(act_pt, n + 1)
                pe.wait_ge(dve_v, 2 * u + 1 + wi // 4)
                if not (isinstance(u, int) and u == 0 and wi == 0):
                    pe.wait_ge(dve_o, n)
                for hp in range(HP):
                    at = 144 * wi + 36 * hp
                    last = mm(ps_o[:, 36 * hp:36 * hp + 36], pt[wi % 2][:, 128 * hp:128 * hp + 128], vx[p][:, at:at + 36], start=True, stop=True)
                last.then_inc(pe_pv, 1)

            def outputs_transposed(u):
                pe.wait_ge(dve_o, 8 * (u + 1))
                if not (isinstance(u, int) and u == 0):
                    pe.wait_ge(dve_xn2, u)
                pe.sem_inc(pe_go, 1)
                for wi in range(8):
                    last = nc.tensor.transpose((ps_c, ps_d)[wi // 4][0:CH, 128 * (wi % 4):128 * (wi % 4) + 128], o3[:, wi, :], ident)
                last.then_inc(pe_ot, 1)

            def project(u):
                pe.wait_ge(act_ot, 2 * (u + 1))
                pe.sem_inc(pe_go, 1)
                for i in range(2):
                    last = mm(ps_c[64 * i:64 * i + 64, 0:UTOK], w(f"wp{l}", 0, 64), ot[:, UTOK * i:UTOK * i + UTOK], start=True, stop=True)
                last.then_inc(pe_pr, 1)

            def deviations2(u):
                pe.wait_ge(dve_x, u + 1)
                mm(ps_d[:, 0:UTOK], w("center2"), X[:, bass.ds(unit_at(u), UTOK)], start=True, stop=True).then_inc(pe_xc2, 1)

            def variance2(u):
                pe.wait_ge(act_sq2, u + 1)
                mm(ps_c[:, 0:UTOK], w("mean2"), sq2[:, :], start=True, stop=True).then_inc(pe_var2, 1)

            def unit(u, p, first=False, last=False):
                for st in range(11):
                    if st < 8:
                        scores(u, st, p)
                    if st == 1 and not first:
                        outputs_transposed(u - 1)
                    if st == 1 and not last:
                        deviations(u + 1)
                    if st == 2 and not first:
                        project(u - 1)
                    if st == 3 and not last:
                        variance(u + 1)
                    if st == 4 and not first:
                        deviations2(u - 1)
                    if 2 <= st < 10:
                        transposes(u, st - 2)
                    if st == 5 and not last:
                        query_key(u + 1)
                    if st == 6 and not first:
                        variance2(u - 1)
                    if st >= 3:
                        weighted(u, st - 3, p)
                    if st in (8, 9) and not last:
                        values(u + 1, st - 8)

            pe.wait_ge(ready, 1)
            deviations(0)
            variance(0)
            query_key(0)
            values(0, 0)
            values(0, 1)
            unit(0, 0, first=True)
            with pe.Fori(0, UNITS // 2 - 1) as i:
                for k in (1, 2):
                    unit(i * 2 + k, k % 2)
            unit(UNITS - 1, 1, last=True)
            outputs_transposed(UNITS - 1)
            project(UNITS - 1)
            deviations2(UNITS - 1)
            variance2(UNITS - 1)

        @block.scalar
        def _(act):
            a = nc.scalar.activation

            def squares(u):
                act.wait_ge(pe_xc, u + 1)
                if not (isinstance(u, int) and u == 0):
                    act.wait_ge(pe_var, u)
                a(sq[:, :], ps_a[:, 0:UTOK], ACT.Square).then_inc(act_sq, 1)

            def deviation_scale(u):
                act.wait_ge(pe_var, u + 1)
                a(ln[:, :], ps_b[:, 0:UTOK], ACT.Ln, bias=eps[:, :]).then_inc(act_ln, 1)
                act.wait_ge(act_ln, u + 1)
                if not (isinstance(u, int) and u == 0):
                    act.wait_ge(dve_xn, u)
                a(rs[:, :], ln[:, :], ACT.Exp, scale=-0.5).then_inc(act_rs, 1)

            def queries(u, p):
                act.wait_ge(pe_q, u + 1)
                if not (isinstance(u, int) and u < 2):
                    act.wait_ge(pe_s, 8 * (u - 1))
                for i in range(2):
                    at = slice(64 * i, 64 * i + 64)
                    a(qbd[p][at, :].rearrange("c (w k) -> c w k", w=STRIPS)[:, :, 64 * i:64 * i + WTOK], by_window(ps_a[at, 0:UTOK]),
                      ACT.Identity, bias=g("bqg")[at, :], scale=QSCALE).then_inc(act_q, 1)

            def exponentials(u, wi):
                n = u * 8 + wi
                act.wait_ge(pool_sub, n + 1)
                if not (isinstance(u, int) and u == 0 and wi < 2):
                    act.wait_ge(pe_tr, n - 1)
                a(e[wi % 2][:, :], t2[wi % 2][:, :], ACT.Exp).then_inc(act_exp, 1)

            def probabilities(u, wi):
                n = u * 8 + wi
                act.wait_ge(pe_tr, n + 1)
                if not (isinstance(u, int) and u == 0 and wi < 2):
                    act.wait_ge(pe_pv, n - 1)
                a(pt[wi % 2][:, :], ps_pt[0:98, :], ACT.Copy).then_inc(act_pt, 1)

            def outputs(u):
                act.wait_ge(pe_ot, u + 1)
                if not (isinstance(u, int) and u == 0):
                    act.wait_ge(pe_pr, u)
                for h in range(2):
                    a(ot4[:, :, 4 * h:4 * h + 4, :].rearrange("c i w k -> c w i k"),
                      (ps_c, ps_d)[h][0:CH, :].rearrange("c (w i k) -> c w i k", w=4, i=2)[:, :, :, 0:WTOK], ACT.Copy).then_inc(act_ot, 1)

            def squares2(u):
                act.wait_ge(pe_xc2, u + 1)
                if not (isinstance(u, int) and u == 0):
                    act.wait_ge(pe_var2, u)
                a(sq2[:, :], ps_d[:, 0:UTOK], ACT.Square).then_inc(act_sq2, 1)

            def deviation_scale2(u):
                act.wait_ge(pe_var2, u + 1)
                a(ln2[:, :], ps_c[:, 0:UTOK], ACT.Ln, bias=eps[:, :]).then_inc(act_ln2, 1)
                act.wait_ge(act_ln2, u + 1)
                if not (isinstance(u, int) and u == 0):
                    act.wait_ge(dve_xn2, u)
                a(rs2[:, :], ln2[:, :], ACT.Exp, scale=-0.5).then_inc(act_rs2, 1)

            def unit(u, p, first=False, last=False):
                for st in range(11):
                    if 1 <= st <= 8:
                        exponentials(u, st - 1)
                    if st == 1 and not first:
                        outputs(u - 1)
                    if st == 1 and not last:
                        squares(u + 1)
                    if 2 <= st < 10:
                        probabilities(u, st - 2)
                    if st == 3 and not last:
                        deviation_scale(u + 1)
                    if st == 4 and not first:
                        squares2(u - 1)
                    if st == 5 and not last:
                        queries(u + 1, 1 - p)
                    if st == 6 and not first:
                        deviation_scale2(u - 1)

            nc.scalar.preload_act_table_set("natural_log_exp_and_others")
            act.wait_ge(ready, 1)
            squares(0)
            deviation_scale(0)
            queries(0, 0)
            unit(0, 0, first=True)
            with act.Fori(0, UNITS // 2 - 1) as i:
                for k in (1, 2):
                    unit(i * 2 + k, k % 2)
            unit(UNITS - 1, 1, last=True)
            outputs(UNITS - 1)
            squares2(UNITS - 1)
            deviation_scale2(UNITS - 1)

        @block.vector
        def _(dve):
            v = nc.vector
            for i in range(2):
                v.memset(qbd[i][:, :], 0.0)
                for wi in range(STRIPS):
                    last = v.tensor_copy(vx[i][:, 144 * wi:144 * wi + 144], w("vones"))
            v.memset(eps[:, :], EPS).then_inc(ready, 1)

            def normalised(u):
                dve.wait_ge(act_rs, u + 1)
                if not (isinstance(u, int) and u == 0):
                    dve.wait_ge(pe_v, 2 * u)
                v.tensor_tensor(xn4, by_window(ps_a[:, 0:UTOK]).unsqueeze(2).to_broadcast([128, STRIPS, 2, WTOK]),
                                by_window(rs[:, :]).unsqueeze(2).to_broadcast([128, STRIPS, 2, WTOK]), ALU.mult).then_inc(dve_xn, 1)

            def keys(u):
                dve.wait_ge(pe_k, u + 1)
                if not (isinstance(u, int) and u == 0):
                    dve.wait_ge(pool_kx, 8 * u)
                v.tensor_scalar(ksb[:, :], ps_b[:, 0:UTOK], g("bkg"), None, ALU.add).then_inc(dve_k, 1)

            def values(u, half, p):
                dve.wait_ge(pe_v, 2 * u + 1 + half)
                if not (isinstance(u, int) and u < 2):
                    dve.wait_ge(pe_pv, 8 * (u - 1))
                src = (ps_a, ps_b)[half][0:98, :].rearrange("t (w i c) -> t w i c", w=4, i=2)
                dst = vx[p][:, 576 * half:576 * half + 576].rearrange("t (w q i c) -> t w q i c", w=4, q=HP, i=2)
                for i in range(2):
                    last = v.tensor_tensor(dst[:, :, :, i, 0:16], src[:, :, i, :].rearrange("t w (q c) -> t w q c", q=HP),
                                           w("vbmask", 0, 16).unsqueeze(1).unsqueeze(1).to_broadcast([98, 4, HP, 16]), ALU.mult)
                last.then_inc(dve_v, 1)

            def add(u, wi, row_kind):
                n = u * 8 + wi
                dve.wait_ge(pe_s, n + 1)
                if not (isinstance(u, int) and u == 0 and wi < 2):
                    dve.wait_ge(pool_sub, n - 1)
                if l == 0:
                    bias = w("rpb0")
                else:
                    bias = keep["winbias"][:, bass.ds((row_kind * 2 + int(wi == STRIPS - 1)) * 392, 392)]
                v.tensor_tensor(t[wi % 2][:, :], ps_s[wi % 2][:, 0:392], bias, ALU.add).then_inc(dve_add, 1)

            def maxima(u, wi):
                n = u * 8 + wi
                dve.wait_ge(dve_add, n + 1)
                v.tensor_reduce(m[wi % 2][:, :], by_head(t[wi % 2][:, :]), AXX, ALU.max).then_inc(dve_max, 1)

            def sums(u, wi):
                n = u * 8 + wi
                dve.wait_ge(pe_pv, n + 1)
                if not (isinstance(u, int) and u == 0 and wi == 0):
                    dve.wait_ge(dve_o, n)
                v.reciprocal(rden[:, :].rearrange("p (q i h) -> p q i h", q=HP, i=2),
                             ps_o[:, 0:144].rearrange("p (q i c) -> p q i c", q=HP, i=2)[:, :, :, 16:18]).then_inc(dve_r, 1)

            def outputs(u, wi):
                n = u * 8 + wi
                dve.wait_ge(dve_r, n + 1)
                if wi == 0 and not (isinstance(u, int) and u == 0):
                    dve.wait_ge(pe_ot, u)
                for i in range(2):
                    at = slice(64 * i, 64 * i + 64)
                    last = v.tensor_tensor(o3[at, wi, :].rearrange("p (q h c) -> p q h c", q=HP, h=2),
                                           ps_o[at, 0:144].rearrange("p (q i c) -> p q i c", q=HP, i=2)[:, :, i, 0:16].rearrange("p q (h c) -> p q h c", h=2),
                                           rden[at, :].rearrange("p (q i h) -> p q i h", q=HP, i=2)[:, :, i, :].unsqueeze(3).to_broadcast([64, HP, 2, 8]), ALU.mult)
                last.then_inc(dve_o, 1)

            def residual(u):
                dve.wait_ge(pe_pr, u + 1)
                at = X[:, bass.ds(unit_at(u), UTOK)]
                v.scalar_tensor_tensor(at, ps_c[:, 0:UTOK], g("bpg"), at, ALU.add, ALU.add).then_inc(dve_x, 1)

            def normalised2(u):
                dve.wait_ge(act_rs2, u + 1)
                v.tensor_tensor(XN[:, bass.ds(unit_at(u), UTOK)], ps_d[:, 0:UTOK], rs2[:, :], ALU.mult).then_inc(dve_xn2, 1)

            def unit(u, p, first=False, last=False):
                row_kind = 0
                if l == 1:
                    row_kind = (u % STRIPS) // (STRIPS - 1)
                for st in range(12):
                    if st >= 4:
                        sums(u, st - 4)
                    if 1 <= st <= 8:
                        maxima(u, st - 1)
                    if st >= 4:
                        outputs(u, st - 4)
                    if st < 8:
                        add(u, st, row_kind)
                    if st == 3 and not first:
                        residual(u - 1)
                    if st == 4 and not last:
                        normalised(u + 1)
                    if st == 6 and not last:
                        keys(u + 1)
                    if st == 7 and not first:
                        normalised2(u - 1)
                    if st in (9, 10) and not last:
                        values(u + 1, st - 9, 1 - p)

            normalised(0)
            keys(0)
            values(0, 0, 0)
            values(0, 1, 0)
            unit(0, 0, first=True)
            with dve.Fori(0, UNITS // 2 - 1) as i:
                for k in (1, 2):
                    unit(i * 2 + k, k % 2)
            unit(UNITS - 1, 1, last=True)
            residual(UNITS - 1)
            normalised2(UNITS - 1)

        @block.gpsimd
        def _(pool):
            def expand(u, wi):
                n = u * 8 + wi
                if wi == 0:
                    pool.wait_ge(dve_k, u + 1)
                if not (isinstance(u, int) and u == 0 and wi < 4):
                    pool.wait_ge(pe_s, n - 3)
                nc.gpsimd.tensor_tensor(by_head(kx[wi % 4][:, :]), ksb[:, WTOK * wi:WTOK * wi + WTOK].unsqueeze(1).to_broadcast([128, HEADS, WTOK]),
                                        w("headmask").unsqueeze(2).to_broadcast([128, HEADS, WTOK]), ALU.mult).then_inc(pool_kx, 1)

            def subtract(u, wi):
                n = u * 8 + wi
                pool.wait_ge(dve_max, n + 1)
                if not (isinstance(u, int) and u == 0 and wi < 2):
                    pool.wait_ge(act_exp, n - 1)
                nc.gpsimd.tensor_tensor(by_head(t2[wi % 2][:, :]), by_head(t[wi % 2][:, :]), m[wi % 2][:, :].unsqueeze(2).to_broadcast([128, HEADS, WTOK]),
                                        ALU.subtract).then_inc(pool_sub, 1)

            def unit(u, last=False):
                for wi in range(8):
                    if wi + 2 < 8:
                        expand(u, wi + 2)
                    subtract(u, wi)
                if not last:
                    expand(u + 1, 0)
                    expand(u + 1, 1)

            expand(0, 0)
            expand(0, 1)
            unit(0)
            with pool.Fori(0, UNITS // 2 - 1) as i:
                for k in (1, 2):
                    unit(i * 2 + k)
            unit(UNITS - 1, last=True)


def mlp_phase(nc, keep, l):
    from contextlib import ExitStack
    import concourse.bass as bass
    from concourse import mybir
    fp32, ALU, ACT = mybir.dt.float32, mybir.AluOpType, mybir.ActivationFunctionType
    W, X, XN = keep["W"], keep["X"], keep["XN"]
    w1, b1 = keep[f"w1g{l}"], keep[f"b1g{l}"]
    HALVES = [(i, c) for c in range(2) for i in range(2)]

    def w(name, a=0, b=None):
        rows, at, cols = WHERE[name]
        return W[0:rows, at + a:at + (cols if b is None else b)]

    with ExitStack() as ctx:
        sem = lambda n: ctx.enter_context(nc.semaphore(f"mlp{l}_{n}"))
        pe_h, act_h, pe_y, dve_y = map(sem, "pe_h act_h pe_y dve_y".split())
        hid = [[ctx.enter_context(nc.sbuf_tensor(f"mlp{l}_h{p}{k}", [128, UTOK], fp32)) for k in range(4)] for p in range(2)]
        ps_h = [ctx.enter_context(nc.psum_tensor(f"mlp{l}_ps_h{k}", [128, 512], fp32)) for k in range(4)]
        ps_y = [ctx.enter_context(nc.psum_tensor(f"mlp{l}_ps_y{k}", [128, 512], fp32)) for k in range(2)]
        block = ctx.enter_context(nc.Block())

        @block.tensor
        def _(pe):
            mm = nc.tensor.matmul

            def up(u):
                for k, (i, c) in enumerate(HALVES):
                    if not (isinstance(u, int) and u == 0):
                        pe.wait_ge(act_h, 4 * u - 3 + k)
                    at = 256 * i + 128 * c
                    mm(ps_h[k][:, 0:UTOK], w1[:, at:at + 128], XN[:, bass.ds(unit_at(u), UTOK)], start=True, stop=True).then_inc(pe_h, 1)

            def down(u, p):
                if not (isinstance(u, int) and u < 2):
                    pe.wait_ge(dve_y, u - 1)
                for k, (i, c) in enumerate(HALVES):
                    pe.wait_ge(act_h, 4 * u + 1 + k)
                    last = mm(ps_y[p][64 * i:64 * i + 64, 0:UTOK], w(f"w2{l}", 64 * c, 64 * c + 64), hid[p][k][:, :], start=c == 0, stop=c == 1)
                last.then_inc(pe_y, 1)

            up(0)
            up(1)
            down(0, 0)
            with pe.Fori(0, UNITS // 2 - 1) as j:
                for k in range(2):
                    up(j * 2 + (k + 2))
                    down(j * 2 + (k + 1), 1 - k)
            down(UNITS - 1, 1)

        @block.scalar
        def _(act):
            def gelu(u, p):
                if not (isinstance(u, int) and u < 2):
                    act.wait_ge(pe_y, u - 1)
                for k, (i, c) in enumerate(HALVES):
                    act.wait_ge(pe_h, 4 * u + 1 + k)
                    nc.scalar.activation(hid[p][k][:, :], ps_h[k][:, 0:UTOK], ACT.Gelu, bias=b1[:, c:c + 1]).then_inc(act_h, 1)

            gelu(0, 0)
            gelu(1, 1)
            with act.Fori(0, UNITS // 2 - 1) as j:
                for k in range(2):
                    gelu(j * 2 + (k + 2), k)

        @block.vector
        def _(dve):
            with dve.Fori(0, UNITS // 2) as j:
                for k in range(2):
                    u = j * 2 + k
                    dve.wait_ge(pe_y, u + 1)
                    at = X[:, bass.ds(unit_at(u), UTOK)]
                    nc.vector.scalar_tensor_tensor(at, ps_y[k][:, 0:UTOK], w(f"b2{l}"), at, ALU.add, ALU.add).then_inc(dve_y, 1)


def roll_phase(nc, keep):
    import concourse.bass as bass
    X, XN = keep["X"], keep["XN"]
    S = WIN // 2

    def views(t, col):
        return t[:, bass.ds(col, UTOK)].rearrange("p (w r c) -> p w r c", w=STRIPS, r=WIN)

    def shift(copy, u, carry):
        s = u % STRIPS
        src = views(X, (u // STRIPS) * TOK + ((s + carry) % STRIPS) * UTOK)
        dst = views(XN, unit_at(u))
        rd, rs = (slice(0, WIN - S), slice(S, WIN)) if carry == 0 else (slice(WIN - S, WIN), slice(0, S))
        copy(dst[:, :, rd, 0:WIN - S], src[:, :, rs, S:WIN])
        copy(dst[:, 0:STRIPS - 1, rd, WIN - S:WIN], src[:, 1:STRIPS, rs, 0:S])
        copy(dst[:, STRIPS - 1, rd, WIN - S:WIN], src[:, 0, rs, 0:S])

    with nc.Block() as block:
        @block.vector
        def _(dve):
            for pair in range(PAIRS):
                at = pair * TOK + SIDE * SIDE
                nc.vector.tensor_copy(XN[:, at:at + TXT], X[:, at:at + TXT])
            with dve.Fori(0, UNITS) as u:
                shift(nc.vector.tensor_copy, u, 0)

        @block.gpsimd
        def _(pool):
            with pool.Fori(0, UNITS) as u:
                shift(nc.gpsimd.tensor_copy, u, 1)


def global_phase(nc, keep, out):
    from contextlib import ExitStack
    import concourse.bass as bass
    from concourse import mybir
    fp32, f32r, bf16 = mybir.dt.float32, mybir.dt.float32r, mybir.dt.bfloat16
    ALU, ACT, AXX = mybir.AluOpType, mybir.ActivationFunctionType, mybir.AxisListType.X
    W, X = keep["W"], keep["X"]
    QC, SUBS = 352, 3
    CHUNKS, QP = TOK // QC, SUBS * 128
    KT = -(-TOK // 128)
    NC, NCH = 396, TOK // 396
    MAXES = SUBS * NCH
    CREDIT = 2

    def rows_of(t):
        return min(128, TOK - 128 * t)

    def w(name, a=0, b=None):
        rows, at, cols = WHERE[name]
        return W[0:rows, at + a:at + (cols if b is None else b)]

    with ExitStack() as ctx:
        made = {}

        def sems(names):
            for n in names.split():
                made[n] = ctx.enter_context(nc.semaphore("gl_" + n))
            return [made[n] for n in names.split()]

        BY_DVE = "dve_lh dve_t dve_yf dve_hi dve_lo dve_mx dve_neg dve_m0 dve_ql dve_h1 dve_x2 dve_oh dve_ohm dve_res link"
        BY_ACT = "act_sq act_ln act_rs act_yn act_qpre act_qh act_p act_o act_x act_r1 act_r2 act_x2t act_oht act_hid"
        BY_PE = "pe_xc pe_var pe_yt pe_qt pe_mx pe_fix pe_s pe_pv pe_p2 pe_x2t pe_lg pe_oht pe_hid pe_ff"
        dve_lh, dve_t, dve_yf, dve_hi, dve_lo, dve_mx, dve_neg, dve_m0, dve_ql, dve_h1, dve_x2, dve_oh, dve_ohm, dve_res, link = sems(BY_DVE)
        act_sq, act_ln, act_rs, act_yn, act_qpre, act_qh, act_p, act_o, act_x, act_r1, act_r2, act_x2t, act_oht, act_hid = sems(BY_ACT)
        pe_xc, pe_var, pe_yt, pe_qt, pe_mx, pe_fix, pe_s, pe_pv, pe_p2, pe_x2t, pe_lg, pe_oht, pe_hid, pe_ff = sems(BY_PE)
        pool_x, stored, ready, pe_go = sems("pool_x stored ready pe_go")

        def credit(engine, names):
            for n in names.split():
                engine.sem_inc(made[n], CREDIT)

        def after(engine, s, k):
            engine.wait_ge(s, k + CREDIT)

        tile = lambda n, c, dt=fp32, r=128: ctx.enter_context(nc.sbuf_tensor("gl_" + n, [r, c], dt))
        lh, sel, eps = tile("lh", 128), tile("sel", CH), tile("eps", 1)
        two = lambda n, c, dt=fp32: [tile(f"{n}{i}", c, dt) for i in range(2)]
        sq, ln, rs, t = two("sq", NC), two("ln", NC), two("rs", NC), two("t", NC)
        hi = two("hi", NC, f32r)
        yf, yhl, yn = tile("yf", TOK), tile("yhl", TOK, f32r), tile("yn", KT * CH)
        qpre, qh, ql = tile("qpre", QP, f32r), tile("qh", QC, f32r), tile("ql", QC, f32r)
        mp, neg, m0 = tile("mp", MAXES), tile("neg", SUBS), tile("m0", SUBS * 128)
        p = [tile(f"p{i}", QC) for i in range(4)]
        osb, xc, xnat, rden, h1 = tile("o", QP), tile("xc", QP), tile("xnat", SUBS * CH), tile("rden", SUBS), tile("h1", SUBS * CH)
        ms, dev, dsq, vs, lv, rstd, x2 = tile("ms", SUBS), tile("dev", SUBS * CH), tile("dsq", SUBS * CH), tile("vs", SUBS), tile("lv", SUBS), tile("rstd", SUBS), tile("x2", SUBS * CH)
        x2t = tile("x2t", QP, r=CH + 1)
        top, eq, cand, best, oh = tile("top", SUBS), tile("eq", SUBS * EXPERTS), tile("cand", SUBS * EXPERTS), tile("best", SUBS), tile("oh", SUBS * EXPERTS)
        oht, ohm, big = tile("oht", QP, r=EXPERTS), tile("ohm", QP, bf16, EXPERTS), tile("big", 512, bf16, EXPERTS)
        hid = [tile(f"hid{c}", QP) for c in range(4)]
        res = tile("res", SUBS * CH)
        ps_s0, ps_s1, ps_m0, ps_m1, ps_o, ps_q, ps_a, ps_b = (ctx.enter_context(nc.psum_tensor(f"gl_ps{i}", [128, 512], fp32)) for i in range(8))
        ps_s, ps_m = [ps_s0, ps_s1], [ps_m0, ps_m1]
        sub = lambda ap: ap.rearrange("p (a c) -> p a c", a=SUBS)
        block = ctx.enter_context(nc.Block())
        SECOND = {1: "p2", 8: "x2t", 10: "lg", 13: "oht", 16: "hid0", 17: "hid1", 19: "hid2", 20: "hid3", 22: "ff"}
        max_step = lambda k: 1 + k * 22 // MAXES

        @block.tensor
        def _(pe):
            mm, tr = nc.tensor.matmul, nc.tensor.transpose
            credit(pe, BY_PE)

            def rotate(b, c):
                if c == 0:
                    after(pe, dve_lh, b + 1)
                after(pe, dve_t, 8 * b + c - 1)
                mm(ps_s[c % 2][:, 0:NC], lh[:, :], X[:, bass.ds((b // 2) * TOK + c * NC, NC)], start=True, stop=True).then_inc(pe_xc, 1)

            def variance(b, c):
                after(pe, act_sq, NCH * b + c + 1)
                after(pe, act_ln, NCH * b + c - 1)
                mm(ps_m[c % 2][:, 0:NC], w("mean128"), sq[c % 2][:, :], start=True, stop=True).then_inc(pe_var, 1)

            def rows_of_y(b, g):
                after(pe, dve_yf, NCH * b + min(NCH, -(-min(TOK, 1024 * (g + 1)) // NC)))
                after(pe, act_yn, 4 * b + g - 1)
                if g == 0:
                    after(pe, dve_res, CHUNKS * b)
                pe.sem_inc(pe_go, 1)
                for k in range(8 * g, min(KT, 8 * g + 8)):
                    n = rows_of(k)
                    last = tr((ps_a, ps_b)[g % 2][0:n, 64 * (k % 8):64 * (k % 8) + 64], yf[0:CH, 128 * k:128 * k + n], w("ident")[0:CH, 0:CH])
                last.then_inc(pe_yt, 1)

            def queries(n, j):
                after(pe, dve_ql, n)
                at = yhl[:, bass.ds(j * QC, QC)]
                mm(ps_q[:, 0:QC], keep["MH"][:, :], at, start=True, stop=False)
                mm(ps_q[:, 0:QC], keep["ML"][:, :], at, start=False, stop=True).then_inc(pe_qt, 1)

            def maxima(n, k):
                a, c = k // NCH, k % NCH
                if k == 0:
                    after(pe, act_qpre, n + 1)
                after(pe, dve_mx, MAXES * n + k - 1)
                mm(ps_m[k % 2][:, 0:NC], qpre[:, 128 * a:128 * a + 128], yhl[:, c * NC:c * NC + NC], start=True, stop=True).then_inc(pe_mx, 1)

            def take_maxima(n):
                after(pe, dve_m0, n + 1)
                for a in range(SUBS):
                    k = min(128, QC - 128 * a)
                    last = mm(ps_q[:, 128 * a:128 * a + k], m0[:, 128 * a:128 * a + 128], w("ident")[:, 0:k], start=False, stop=True, skip_group_check=True)
                last.then_inc(pe_fix, 1)

            def scores(n, k):
                if k == 0:
                    after(pe, dve_ql, n + 1)
                after(pe, act_p, KT * n + k - 1)
                r = rows_of(k)
                o = ps_s[k % 2][0:r, 0:QC]
                mm(o, yhl[:, 128 * k:128 * k + r], qh[:, :], start=True, stop=False)
                mm(o, yhl[:, 128 * k:128 * k + r], ql[:, :], start=False, stop=True).then_inc(pe_s, 1)

            def weighted(n, k):
                after(pe, act_p, KT * n + k + 1)
                if k == 0:
                    after(pe, act_o, n)
                r, half = rows_of(k), slice(64 * (k % 2), 64 * (k % 2) + 64)
                mm(ps_o[half, 0:QC], yn[0:r, CH * k:CH * k + CH], p[k % 4][0:r, :], start=k < 2, stop=k >= KT - 2).then_inc(pe_pv, 1)

            def second(n, what):
                if what == "p2":
                    after(pe, act_o, n + 1)
                    after(pe, pool_x, n + 1)
                    after(pe, dve_res, n)
                    for a in range(SUBS):
                        mm(ps_a[:, 65 * a:65 * a + 65], osb[:, 128 * a:128 * a + 128], keep["LT"][:, :], start=True, stop=True)
                        last = mm(ps_a[:, 256 + CH * a:256 + CH * a + CH], xc[:, 128 * a:128 * a + 128], sel[:, :], start=True, stop=True)
                    last.then_inc(pe_p2, 1)
                elif what == "x2t":
                    after(pe, dve_x2, n + 1)
                    after(pe, act_hid, 4 * n)
                    pe.sem_inc(pe_go, 1)
                    for a in range(SUBS):
                        last = tr(ps_b[0:CH, 128 * a:128 * a + 128], x2[:, CH * a:CH * a + CH], w("ident"))
                    last.then_inc(pe_x2t, 1)
                elif what == "lg":
                    after(pe, act_x2t, n + 1)
                    for a in range(SUBS):
                        last = mm(ps_a[:, EXPERTS * a:EXPERTS * a + EXPERTS], x2t[:, 128 * a:128 * a + 128], w("rw"), start=True, stop=True)
                    last.then_inc(pe_lg, 1)
                elif what == "oht":
                    after(pe, dve_oh, n + 1)
                    for a in range(SUBS):
                        last = tr(ps_b[0:EXPERTS, 128 * a:128 * a + 128], oh[:, EXPERTS * a:EXPERTS * a + EXPERTS], w("ident"))
                    last.then_inc(pe_oht, 1)
                elif what.startswith("hid"):
                    c = int(what[3])
                    if c == 0:
                        after(pe, dve_ohm, n + 1)
                    if c >= 2:
                        after(pe, act_hid, 4 * n + c - 1)
                    o = (ps_a, ps_b)[c % 2][:, 0:QP]
                    mm(o, w("fw1", 128 * c, 128 * c + 128), x2t[:, :], start=True, stop=False)
                    mm(o, big[:, 128 * c:128 * c + 128], ohm[:, :], start=False, stop=True).then_inc(pe_hid, 1)
                else:
                    after(pe, act_hid, 4 * n + 4)
                    for a in range(SUBS):
                        for c in range(4):
                            mm(ps_a[:, CH * a:CH * a + CH], hid[c][:, 128 * a:128 * a + 128], w("fw2", CH * c, CH * c + CH), start=c == 0, stop=False)
                        last = mm(ps_a[:, CH * a:CH * a + CH], oht[:, 128 * a:128 * a + 128], w("fb2"), start=False, stop=True)
                    last.then_inc(pe_ff, 1)

            def chunk(n, j, first=False, last=False):
                for k in range(KT):
                    scores(n, k)
                    if not last:
                        if k == 0:
                            queries(n + 1, j + 1)
                        for q in range(MAXES):
                            if max_step(q) == k:
                                maxima(n + 1, q)
                    if not first and k in SECOND:
                        second(n - 1, SECOND[k])
                    if k % 2 and k >= 3:
                        weighted(n, k - 3)
                        weighted(n, k - 2)
                for k in range(KT - 3, KT):
                    weighted(n, k)
                if not last:
                    take_maxima(n + 1)

            pe.wait_ge(ready, 1)
            with pe.Fori(0, IMG) as b:
                for c in range(NCH + 1):
                    if c < NCH:
                        rotate(b, c)
                    if c >= 1:
                        variance(b, c - 1)
                for g in range(4):
                    rows_of_y(b, g)
                after(pe, dve_lo, NCH * (b + 1))
                after(pe, act_ln, NCH * (b + 1))
                n0 = b * CHUNKS
                queries(n0, 0)
                for k in range(MAXES):
                    maxima(n0, k)
                take_maxima(n0)
                after(pe, act_yn, 4 * b + 4)
                chunk(n0, 0, first=True)
                with pe.Fori(1, CHUNKS - 1) as j:
                    chunk(n0 + j, j)
                chunk(n0 + (CHUNKS - 1), CHUNKS - 1, last=True)
                for what in SECOND.values():
                    second(n0 + (CHUNKS - 1), what)

        @block.scalar
        def _(act):
            a_ = nc.scalar.activation
            credit(act, BY_ACT)

            def squares(b, c):
                after(act, pe_xc, NCH * b + c + 1)
                after(act, pe_var, NCH * b + c - 1)
                a_(sq[c % 2][:, :], ps_s[c % 2][:, 0:NC], ACT.Square).then_inc(act_sq, 1)

            def scale(b, c):
                after(act, pe_var, NCH * b + c + 1)
                a_(ln[c % 2][:, :], ps_m[c % 2][:, 0:NC], ACT.Ln, bias=eps[:, :]).then_inc(act_ln, 1)
                after(act, act_ln, NCH * b + c + 1)
                after(act, dve_t, NCH * b + c - 1)
                a_(rs[c % 2][:, :], ln[c % 2][:, :], ACT.Exp, scale=-0.5).then_inc(act_rs, 1)

            def rows_of_y(b, g):
                after(act, pe_yt, 4 * b + g + 1)
                k = min(KT, 8 * g + 8) - 8 * g
                r = 128 if k == 8 else rows_of(KT - 1)
                a_(yn[0:r, 512 * g:512 * g + CH * k], (ps_a, ps_b)[g % 2][0:r, 0:CH * k], ACT.Copy).then_inc(act_yn, 1)

            def queries(n):
                after(act, pe_qt, n + 1)
                after(act, pe_mx, MAXES * n)
                a_(qpre[:, 0:QC], ps_q[:, 0:QC], ACT.Copy).then_inc(act_qpre, 1)

            def queries_high(n):
                after(act, pe_fix, n + 1)
                after(act, pe_s, KT * n)
                a_(qh[:, :], ps_q[:, 0:QC], ACT.Copy).then_inc(act_qh, 1)

            def exponentials(n, k):
                r = rows_of(k)
                after(act, pe_s, KT * n + k + 1)
                after(act, pe_pv, KT * n + k - 3 if k > 1 else KT * n)
                a_(p[k % 4][0:r, :], ps_s[k % 2][0:r, 0:QC], ACT.Exp).then_inc(act_p, 1)

            def sums(n):
                after(act, pe_pv, KT * (n + 1))
                after(act, pe_p2, n)
                a_(osb[:, 0:QC], ps_o[:, 0:QC], ACT.Copy).then_inc(act_o, 1)

            def second(n, what):
                if what == "x":
                    after(act, pe_p2, n + 1)
                    after(act, dve_h1, n)
                    a_(xnat[:, :], ps_a[:, 256:256 + SUBS * CH], ACT.Copy).then_inc(act_x, 1)
                elif what == "rstd":
                    after(act, dve_h1, n + 1)
                    a_(lv[:, :], vs[:, :], ACT.Ln, bias=eps[:, :], scale=1.0 / CH).then_inc(act_r1, 1)
                    after(act, act_r1, n + 1)
                    a_(rstd[:, :], lv[:, :], ACT.Exp, scale=-0.5).then_inc(act_r2, 1)
                elif what == "x2t":
                    after(act, pe_x2t, n + 1)
                    after(act, pe_hid, 4 * n)
                    a_(x2t[0:CH, :], ps_b[0:CH, 0:QP], ACT.Copy).then_inc(act_x2t, 1)
                elif what == "oht":
                    after(act, pe_oht, n + 1)
                    after(act, pe_ff, n)
                    a_(oht[:, :], ps_b[0:EXPERTS, 0:QP], ACT.Copy).then_inc(act_oht, 1)
                else:
                    c = int(what[3])
                    after(act, pe_hid, 4 * n + c + 1)
                    a_(hid[c][:, :], (ps_a, ps_b)[c % 2][:, 0:QP], ACT.Relu).then_inc(act_hid, 1)

            parts = {2: "x", 5: "rstd", 9: "x2t", 14: "oht", 17: "hid0", 18: "hid1", 20: "hid2", 21: "hid3"}

            def chunk(n, first=False, last=False):
                for k in range(KT):
                    exponentials(n, k)
                    if k == 0 and not last:
                        queries(n + 1)
                    if not first and k in parts:
                        second(n - 1, parts[k])
                if not last:
                    queries_high(n + 1)
                sums(n)

            nc.scalar.preload_act_table_set("natural_log_exp_and_others")
            act.wait_ge(ready, 1)
            with act.Fori(0, IMG) as b:
                for c in range(NCH + 1):
                    if c < NCH:
                        squares(b, c)
                    if c >= 1:
                        scale(b, c - 1)
                for g in range(4):
                    rows_of_y(b, g)
                n0 = b * CHUNKS
                queries(n0)
                queries_high(n0)
                chunk(n0, first=True)
                with act.Fori(1, CHUNKS - 1) as j:
                    chunk(n0 + j)
                chunk(n0 + (CHUNKS - 1), last=True)
                for what in parts.values():
                    second(n0 + (CHUNKS - 1), what)

        @block.vector
        def _(dve):
            v = nc.vector
            credit(dve, BY_DVE)
            v.memset(m0[:, :], 0.0)
            v.tensor_scalar(qpre[:, QC:QP], w("ident", 0, QP - QC), 0.0, None, ALU.mult)
            v.memset(osb[:, QC:QP], 1.0)
            v.memset(xc[:, QC:QP], 0.0)
            v.memset(x2t[CH:CH + 1, :], 1.0)
            v.tensor_copy(big[:, :], w("big"))
            v.memset(eps[:, :], EPS).then_inc(ready, 1)

            def piece(b, st):
                if st < NCH:
                    c = st
                    after(dve, act_rs, NCH * b + c + 1)
                    after(dve, dve_yf, NCH * b + c - 1)
                    v.tensor_tensor(t[c % 2][:, :], ps_s[c % 2][:, 0:NC], rs[c % 2][:, :], ALU.mult).then_inc(dve_t, 1)
                if 1 <= st < NCH + 1:
                    c = st - 1
                    after(dve, dve_t, NCH * b + c + 1)
                    v.tensor_scalar(yf[:, NC * c:NC * c + NC], t[c % 2][:, :], w("den"), None, ALU.add).then_inc(dve_yf, 1)
                if 2 <= st < NCH + 2:
                    c = st - 2
                    after(dve, dve_yf, NCH * b + c + 1)
                    after(dve, dve_lo, NCH * b + c - 1)
                    v.tensor_copy(yhl[0:64, NC * c:NC * c + NC], yf[0:64, NC * c:NC * c + NC])
                    v.tensor_copy(hi[c % 2][64:128, :], yf[64:128, NC * c:NC * c + NC]).then_inc(dve_hi, 1)
                if st >= 3:
                    c = st - 3
                    after(dve, dve_hi, NCH * b + c + 1)
                    v.tensor_tensor(yhl[64:128, NC * c:NC * c + NC], yf[64:128, NC * c:NC * c + NC], hi[c % 2][64:128, :].bitcast(fp32), ALU.subtract).then_inc(dve_lo, 1)

            def maxima(n, k):
                after(dve, pe_mx, MAXES * n + k + 1)
                v.tensor_reduce(mp[:, k:k + 1], ps_m[k % 2][:, 0:NC], AXX, ALU.max).then_inc(dve_mx, 1)

            def take_maxima(n):
                after(dve, dve_mx, MAXES * (n + 1))
                v.tensor_reduce(neg[:, :], sub(mp[:, :]), AXX, ALU.max, negate=True).then_inc(dve_neg, 1)
                after(dve, dve_neg, n + 1)
                after(dve, pe_fix, n)
                v.tensor_copy(m0[:, :].rearrange("p (a h c) -> p a h c", a=SUBS, h=2)[:, :, :, 0], neg[:, :].unsqueeze(2).to_broadcast([128, SUBS, 2])).then_inc(dve_m0, 1)

            def queries_low(n):
                after(dve, act_qh, n + 1)
                v.tensor_tensor(ql[:, :], ps_q[:, 0:QC], qh[:, :].bitcast(fp32), ALU.subtract).then_inc(dve_ql, 1)

            wide = lambda ap, c: ap.unsqueeze(2).to_broadcast([128, SUBS, c])

            def second(n, what):
                LINKS = 9
                at = {"h1": 0, "oh": 5}.get(what, 0)
                done = [at]

                def linked(ins):
                    done[0] += 1
                    ins.then_inc(link, 1)
                    after(dve, link, LINKS * n + done[0])

                if what == "h1":
                    after(dve, act_x, n + 1)
                    on = sub(ps_a[:, 0:SUBS * 65])
                    linked(v.reciprocal(rden[:, :], on[:, :, 64]))
                    for a in range(SUBS):
                        last = v.scalar_tensor_tensor(h1[:, CH * a:CH * a + CH], on[:, a, 0:CH], rden[:, a:a + 1], xnat[:, CH * a:CH * a + CH], ALU.mult, ALU.add)
                    linked(last)
                    linked(v.tensor_reduce(ms[:, :], sub(h1[:, :]), AXX, ALU.add))
                    linked(v.scalar_tensor_tensor(sub(dev[:, :]), wide(ms[:, :], CH), -1.0 / CH, sub(h1[:, :]), ALU.mult, ALU.add))
                    linked(v.tensor_tensor(dsq[:, :], dev[:, :], dev[:, :], ALU.mult))
                    v.tensor_reduce(vs[:, :], sub(dsq[:, :]), AXX, ALU.add).then_inc(dve_h1, 1)
                elif what == "x2":
                    after(dve, act_r2, n + 1)
                    after(dve, pe_x2t, n)
                    v.tensor_tensor(sub(x2[:, :]), sub(dev[:, :]), wide(rstd[:, :], CH), ALU.mult).then_inc(dve_x2, 1)
                elif what == "oh":
                    after(dve, pe_lg, n + 1)
                    lg = sub(ps_a[:, 0:SUBS * EXPERTS])
                    linked(v.tensor_reduce(top[:, :], lg, AXX, ALU.max))
                    linked(v.tensor_tensor(sub(eq[:, :]), lg, wide(top[:, :], EXPERTS), ALU.is_equal))
                    linked(v.tensor_tensor(sub(cand[:, :]), sub(eq[:, :]), w("revidx").unsqueeze(1).to_broadcast([128, SUBS, EXPERTS]), ALU.mult))
                    linked(v.tensor_reduce(best[:, :], sub(cand[:, :]), AXX, ALU.max))
                    after(dve, pe_oht, n)
                    v.tensor_tensor(sub(oh[:, :]), sub(cand[:, :]), wide(best[:, :], EXPERTS), ALU.is_equal).then_inc(dve_oh, 1)
                elif what == "ohm":
                    after(dve, act_oht, n + 1)
                    after(dve, pe_hid, 4 * n)
                    v.tensor_scalar(ohm[:, :], oht[:, :], -1.0, None, ALU.add).then_inc(dve_ohm, 1)
                else:
                    after(dve, pe_ff, n + 1)
                    after(dve, stored, 32 * n)
                    v.scalar_tensor_tensor(res[:, :], ps_a[:, 0:SUBS * CH], 0.0, h1[:, :], ALU.max, ALU.add).then_inc(dve_res, 1)

            parts = {3: "h1", 6: "x2", 11: "oh", 15: "ohm", 23: "res"}

            def chunk(n, first=False, last=False):
                for k in range(KT):
                    if not last:
                        for q in range(MAXES):
                            if max_step(q) == k:
                                maxima(n + 1, q)
                    if not first and k in parts:
                        second(n - 1, parts[k])
                if not last:
                    take_maxima(n + 1)
                    queries_low(n + 1)

            with dve.Fori(0, IMG) as b:
                n0 = b * CHUNKS
                after(dve, act_o, n0)
                v.tensor_copy(lh[:, :], w("rot", 0, 256)[:, bass.ds((b % 2) * 128, 128)])
                v.tensor_copy(sel[:, :], w("pick", 0, 128)[:, bass.ds((b % 2) * CH, CH)]).then_inc(dve_lh, 1)
                for st in range(NCH + 3):
                    piece(b, st)
                for k in range(MAXES):
                    maxima(n0, k)
                take_maxima(n0)
                queries_low(n0)
                chunk(n0, first=True)
                with dve.Fori(1, CHUNKS - 1) as j:
                    chunk(n0 + j)
                chunk(n0 + (CHUNKS - 1), last=True)
                for what in parts.values():
                    second(n0 + (CHUNKS - 1), what)

        @block.gpsimd
        def _(pool):
            pool.sem_inc(pool_x, CREDIT)
            pool.wait_ge(ready, 1)
            with pool.Fori(0, IMG) as b:
                with pool.Fori(0, CHUNKS) as j:
                    n = b * CHUNKS + j
                    after(pool, pe_p2, n)
                    nc.gpsimd.tensor_copy(xc[:, 0:QC], X[:, bass.ds((b // 2) * TOK + j * QC, QC)]).then_inc(pool_x, 1)

        @block.sync
        def _(sp):
            flat = out.rearrange("b t c -> (b t) c")
            sp.sem_inc(stored, CREDIT)
            with sp.Fori(0, IMG) as b:
                with sp.Fori(0, CHUNKS) as j:
                    after(sp, dve_res, b * CHUNKS + j + 1)
                    at = b * TOK + j * QC
                    sp.dma_start(flat[bass.ds(at, 256), :].rearrange("(a q) c -> q a c", a=2), sub(res[:, :])[:, 0:2, :]).then_inc(stored, 16)
                    sp.dma_start(flat[bass.ds(at + 256, QC - 256), :], sub(res[:, :])[0:QC - 256, 2, :]).then_inc(stored, 16)
            sp.wait_ge(stored, 32 * IMG * CHUNKS + CREDIT)


def kernel(**inputs):
    import numpy as np
    import concourse.bacc as bacc
    from concourse import mybir
    from concourse.bass_utils import run_bass_kernel_spmd

    packed, patches, text = lay_out(inputs["x"], inputs)
    arrays = {"packed": packed, "patches": patches, "text": text}
    nc = bacc.Bacc("TRN2", target_bir_lowering=False, num_devices=1)
    args = [nc.dram_tensor(n, a.shape, mybir.dt.from_np(a.dtype), kind="ExternalInput").ap() for n, a in arrays.items()]
    args.append(nc.dram_tensor("out", (IMG, TOK, CH), mybir.dt.float32, kind="ExternalOutput").ap())
    program(nc, *args)
    got = run_bass_kernel_spmd(nc, [arrays], core_ids=[0]).results[0]["out"]
    shift = WIN // 2
    img = got[:, :SIDE * SIDE].reshape(IMG, STRIPS, STRIPS, WIN, WIN, CH).transpose(0, 1, 3, 2, 4, 5).reshape(IMG, SIDE, SIDE, CH)
    img = np.roll(img, (shift, shift), axis=(1, 2)).reshape(IMG, SIDE * SIDE, CH)
    return np.concatenate([img, got[:, SIDE * SIDE:]], axis=1)
```

```python
IMG, SIDE, WIN, CH, HEADS = 8, 56, 7, 64, 8
PAIRS = IMG // 2
STRIPS = SIDE // WIN
WTOK = WIN * WIN
UTOK = STRIPS * WTOK
UNITS = PAIRS * STRIPS
TXT = 32
TOK = SIDE * SIDE + TXT
EXPERTS, EH = 32, 16
EPS = 1e-5


def pack_columns(parts):
    at, where = 0, {}
    for name, rows, cols in parts:
        where[name] = (rows, at, cols)
        at += cols
    return where, at


PARTS = [
    ("ident", 128, 128), ("center2", 128, 128), ("mean2", 128, 128), ("mean128", 128, 128),
    ("rot", 128, 256), ("pick", 128, 128), ("rot64", 64, 64), ("e0", 128, 1), ("e0row", 1, 128), ("vbmask", 98, 64),
    ("headmask", 128, 8), ("vones", 98, 144), ("winmask", 128, 196), ("den", 128, 1), ("revidx", 128, 32), ("big", 32, 512),
    ("pe_w", 128, 32), ("pe_b", 128, 1), ("pe_g", 128, 1), ("pe_nb", 128, 1),
    *[(f"{n}{l}", r, c) for l in range(2) for n, r, c in (
        ("wq", 128, 128), ("wk", 128, 128), ("wv", 128, 128), ("wp", 64, 128), ("w1", 128, 512), ("w2", 128, 128),
        ("n1g", 128, 1), ("n1b", 128, 1), ("n2g", 128, 1), ("n2b", 128, 1), ("bq", 128, 1), ("bk", 128, 1), ("bv", 128, 1),
        ("bp", 128, 1), ("b1", 128, 2), ("b2", 128, 1), ("rpb", 128, 392))],
    ("awq", 64, 64), ("awk", 64, 64), ("awv", 64, 64), ("abq", 64, 1), ("abk", 64, 1), ("abv", 1, 64),
    ("rw", 65, 32), ("fw1", 128, 512), ("fb1", 128, 4), ("fw2", 128, 256), ("fb2", 32, 64),
    ("tw1", 64, 896), ("tw2", 128, 320), ("tw3", 64, 3), ("tb1", 128, 1), ("tb2", 64, 1), ("tb3", 128, 1),
    ("emb", 64, 68), ("cpos", 128, 64), ("bpos", 128, 1), ("widths", 128, 4), ("scales", 128, 4), ("chan", 64, 1),
]
WHERE, PACKED = pack_columns(PARTS)


def shape_constants():
    import numpy as np
    eye, c = np.eye(CH), {}
    two = lambda m: np.kron(np.eye(2), m)
    c["ident"] = np.eye(128)
    c["center2"] = two(eye - 1.0 / CH)
    c["mean2"] = two(np.full((CH, CH), 1.0 / CH))
    c["mean128"] = np.full((128, 128), 1.0 / 128)
    u = np.full(CH, 1.0 / np.sqrt(CH))
    v = u.copy()
    v[0] -= 1.0
    house = eye - 2.0 * np.outer(v, v) / (v @ v)
    house[0, :] = 0.0
    c["rot"] = np.concatenate([np.concatenate([np.tile(house.T, (1, 2)) if j == i else np.zeros((CH, 128)) for j in range(2)]) for i in range(2)], 1)
    c["pick"] = np.concatenate([np.concatenate([eye if j == i else np.zeros((CH, CH)) for j in range(2)]) for i in range(2)], 1)
    c["rot64"] = house.T
    e0 = np.zeros((128, 1))
    e0[0] = 1.0
    c["e0"] = e0
    c["e0row"] = np.zeros((1, 128))
    c["e0row"][0, [0, 64]] = 1.0
    c["den"] = c["e0row"].T
    row2 = np.repeat(np.arange(2), WTOK)
    vm = (row2[:, None, None] == np.arange(2)[None, :, None]) * np.ones((1, 1, 8))
    c["vbmask"] = np.tile(vm.reshape(98, 16), (1, 4))
    on = np.zeros((98, 4, 2, 18))
    on[:, :, :, 16:] = (row2[:, None] == np.arange(2)[None, :])[:, None, None, :]
    c["vones"] = on.reshape(98, 144)
    c["headmask"] = (np.arange(128)[:, None] % CH // 8 == np.arange(8)[None, :]) * 1.0
    shift = WIN // 2
    part = lambda last: np.where(np.arange(WIN) < WIN - shift, 0, 1) if last else np.zeros(WIN, int)
    wm = np.zeros((128, 4, WTOK))
    for rt in range(2):
        for ct in range(2):
            g = (part(rt)[:, None] * 2 + part(ct)[None, :]).reshape(-1)
            m = np.where(g[:, None] != g[None, :], -100.0, 0.0)
            wm[0:WTOK, rt * 2 + ct] = m
            wm[WTOK:2 * WTOK, rt * 2 + ct] = m
    c["winmask"] = wm.reshape(128, 196)
    c["revidx"] = np.tile(float(EXPERTS) - np.arange(EXPERTS), (128, 1))
    c["big"] = (np.arange(32)[:, None] == np.arange(512)[None, :] // EH) * float(2.0 ** 100)
    c["bpos"] = np.tile(np.linspace(0.0, 1.0, TXT, dtype=np.float32)[:, None], (4, 1))
    c["chan"] = np.arange(CH)[:, None] * 1.0
    return {k: np.asarray(v, np.float32) for k, v in c.items()}


def windows_first(img):
    s = img.shape[:-2]
    a = img.reshape(*s, STRIPS, WIN, STRIPS, WIN)
    k = len(s)
    return a.transpose(*range(k), k, k + 2, k + 1, k + 3)


def lay_out(x, inp):
    import numpy as np
    f = lambda n: np.asarray(inp[n])
    p = dict(shape_constants())

    def diag2(m):
        z = np.zeros((2 * m.shape[0], 2 * m.shape[1]), np.float32)
        z[:m.shape[0], :m.shape[1]] = m
        z[m.shape[0]:, m.shape[1]:] = m
        return z

    twice = lambda v: np.concatenate([v, v]).reshape(128, -1)
    p["pe_w"] = diag2(f("L0_tok_pe_w").reshape(CH, 16))
    p["pe_b"], p["pe_g"], p["pe_nb"] = twice(f("L0_tok_pe_b")), twice(f("L0_tok_pe_ng")), twice(f("L0_tok_pe_nb"))
    for l in range(2):
        qkv, qb = f("L0_tok_qkv_w")[l].reshape(3, CH, CH), f("L0_tok_qkv_b")[l].reshape(3, CH)
        for i, n in enumerate("qkv"):
            p[f"w{n}{l}"], p[f"b{n}{l}"] = diag2(qkv[i].T), twice(qb[i])
        p[f"wp{l}"] = np.concatenate([f("L0_tok_proj_w")[l].T] * 2, 1)
        p[f"bp{l}"] = twice(f("L0_tok_proj_b")[l])
        w1 = f("L0_tok_w1")[l].T
        z = np.zeros((2, CH, 2, 2, 128), np.float32)
        for i in range(2):
            z[i, :, i] = w1.reshape(CH, 2, 128)
        p[f"w1{l}"] = z.reshape(128, 512)
        p[f"w2{l}"] = f("L0_tok_w2")[l].T.reshape(2, 128, CH).transpose(1, 0, 2).reshape(128, 128)
        p[f"b1{l}"] = f("L0_tok_b1")[l].reshape(2, 128).T
        for n in ("n1g", "n1b", "n2g", "n2b", "b2"):
            p[f"{n}{l}"] = twice(f("L0_tok_" + n)[l])
        t = f("L0_tok_rpb")[l].T.reshape(HEADS, 13, 13)
        b = np.zeros((128, HEADS, WIN, WIN), np.float32)
        for qr in range(WIN):
            for qc in range(WIN):
                piece = t[:, qr:qr + WIN, qc:qc + WIN][:, ::-1, ::-1]
                b[qr * WIN + qc] = piece
                b[WTOK + qr * WIN + qc] = piece
        p[f"rpb{l}"] = b.reshape(128, 392)
    p["awq"], p["awk"], p["awv"] = f("L0_attn_Wq").T, f("L0_attn_Wk").T, f("L0_attn_Wv").T
    p["abq"], p["abk"], p["abv"] = f("L0_attn_bq")[:, None], f("L0_attn_bk")[:, None], f("L0_attn_bv")[None, :]
    p["rw"] = np.concatenate([f("L0_ffn_router_w").T, f("L0_ffn_router_b")[None, :]])
    p["fw1"] = np.concatenate([f("L0_ffn_W1").transpose(1, 0, 2).reshape(CH, 512)] * 2)
    p["fb1"] = f("L0_ffn_b1").reshape(4, 128).T
    p["fw2"] = f("L0_ffn_W2").reshape(4, 128, CH).transpose(1, 0, 2).reshape(128, 256)
    p["fb2"] = f("L0_ffn_b2")
    p["tw1"] = f("L0_txt_w1").transpose(1, 2, 0).reshape(64, 7 * 128)
    p["tw2"] = f("L0_txt_w2").transpose(1, 2, 0).reshape(128, 5 * 64)
    p["tw3"] = f("L0_txt_w3")[0]
    p["tb1"], p["tb2"] = f("L0_txt_b1")[:, None], f("L0_txt_b2")[:, None]
    p["tb3"] = np.broadcast_to(f("L0_txt_b3").reshape(1, 1), (128, 1))
    p["emb"] = np.concatenate([f("L0_txt_emb"), f("L0_txt_locality_shapes")], 1)
    cp = f("fside_BS_continuous_positions")
    p["cpos"] = np.broadcast_to(cp.reshape(2, 4, 1, TXT).transpose(1, 2, 0, 3), (4, TXT, 2, TXT)).reshape(128, 64)
    p["widths"] = np.broadcast_to(f("L0_txt_multiscale_widths")[None, :], (128, 4))
    p["scales"] = np.broadcast_to(f("L0_txt_scale_weights")[None, :], (128, 4))
    packed = np.zeros((128, PACKED), np.float32)
    for name, (rows, at, cols) in WHERE.items():
        packed[0:rows, at:at + cols] = p[name]
    a = np.asarray(x).reshape(PAIRS, 2, SIDE, 4, SIDE, 4).transpose(1, 3, 5, 0, 2, 4)
    patches = np.ascontiguousarray(windows_first(a)).reshape(32, UNITS * UTOK)
    text = np.ascontiguousarray(np.broadcast_to(np.asarray(inp["x_txt"]).reshape(1, IMG * TXT), (64, IMG * TXT)))
    return packed, patches, text
def program(nc, packed, patches, text, out):
    import concourse.bass as bass
    from concourse import mybir
    from contextlib import ExitStack
    with ExitStack() as ctx:
        keep = {}
        fp32 = mybir.dt.float32

        def sb(name, cols, dt=fp32, rows=128):
            keep[name] = ctx.enter_context(nc.sbuf_tensor(name, [rows, cols], dt))

        sb("W", PACKED)
        sb("X", PAIRS * TOK)
        for l in range(2):
            for n, c in (("wq", 128), ("wk", 128), ("wv", 128), ("w1", 512), ("bq", 1), ("bk", 1), ("bv", 1), ("bp", 1), ("b1", 2)):
                sb(f"{n}g{l}", c)
        sb("winbias", 4 * 392)
        sb("peT", 128, rows=32)
        sb("peb", 1)
        sb("MH", 128, mybir.dt.float32r)
        sb("ML", 128, mybir.dt.float32r)
        sb("LT", 65)
        arrived = [ctx.enter_context(nc.semaphore(n)) for n in ("patches_first", "patches_rest")]
        setup_phase(nc, keep, packed, patches, arrived)
        with nc.sbuf_tensor("Y", [128, PAIRS * TOK], fp32) as spare:
            streams = [(spare, keep["X"]), (keep["X"], spare)]
            keep["X"], keep["XN"] = streams[0]
            embed_phase(nc, keep, arrived)
            text_phase(nc, keep, text)
            for l in range(2):
                attention_phase(nc, keep, l)
                mlp_phase(nc, keep, l)
                if l == 0:
                    roll_phase(nc, keep)
                    keep["X"], keep["XN"] = streams[1]
        global_phase(nc, keep, out)


def setup_phase(nc, keep, packed, patches, arrived):
    from contextlib import ExitStack
    from concourse import mybir
    fp32, f32r = mybir.dt.float32, mybir.dt.float32r
    ALU = mybir.AluOpType
    W = keep["W"]

    def w(name, a=0, b=None):
        rows, at, cols = WHERE[name]
        return W[0:rows, at + a:at + (cols if b is None else b)]

    with ExitStack() as ctx:
        loaded, pe_one, dve_one, pe_two = (ctx.enter_context(nc.semaphore("set_" + n)) for n in ("loaded", "pe_one", "dve_one", "pe_two"))
        ps = [ctx.enter_context(nc.psum_tensor(f"set_ps{i}", [128, 512], fp32)) for i in range(5)]
        GG = ctx.enter_context(nc.sbuf_tensor("set_G", [64, 128], fp32))
        JJ = ctx.enter_context(nc.sbuf_tensor("set_J", [64, 128], fp32))
        M32 = ctx.enter_context(nc.sbuf_tensor("set_M", [128, 128], fp32))
        block = ctx.enter_context(nc.Block())

        @block.sync
        def _(sp):
            half = PACKED // 2
            sp.dma_start(W[:, 0:half], packed[:, 0:half]).then_inc(loaded, 16)
            sp.dma_start(W[:, half:PACKED], packed[:, half:PACKED]).then_inc(loaded, 16)
            first, n_cols = STRIPS * UTOK, UNITS * UTOK
            sp.dma_start(keep["X"][0:32, 0:first], patches[:, 0:first]).then_inc(arrived[0], 16)
            sp.dma_start(keep["X"][0:32, first:n_cols], patches[:, first:n_cols]).then_inc(arrived[1], 16)

        @block.tensor
        def _(pe):
            pe.wait_ge(loaded, 32)
            mm = nc.tensor.matmul
            mm(ps[0][:, 0:1], w("center2"), w("pe_b"), start=True, stop=True)
            for l in range(2):
                for i, n in enumerate(("wq", "wk", "wv")):
                    mm(ps[0][:, 1 + 8 * l + i:2 + 8 * l + i], w(f"{n}{l}"), w(f"n1b{l}"), start=True, stop=True)
                for h in range(2):
                    mm(ps[0][:, 4 + 8 * l + h:5 + 8 * l + h], w(f"w1{l}", 128 * h, 128 * h + 128), w(f"n2b{l}"), start=True, stop=True)
            mm(ps[1][0:32, 0:128], w("pe_w"), w("center2"), start=True, stop=True)
            mm(ps[2][0:64, 0:64], w("awq"), w("rot64"), start=True, stop=True)
            mm(ps[2][0:64, 64:128], w("awk"), w("rot64"), start=True, stop=True)
            mm(ps[3][:, 0:64], w("rot", 0, 128)[0:64, :], w("awv"), start=True, stop=False)
            mm(ps[3][:, 0:64], w("e0row"), w("abv"), start=False, stop=True).then_inc(pe_one, 1)
            pe.wait_ge(dve_one, 1)
            for l in range(2):
                mm(ps[0][:, 20 + l:21 + l], w(f"wp{l}"), keep[f"bvg{l}"][0:64, :], start=True, stop=True)
            mm(ps[4][:, 0:128], GG[:, :], JJ[:, :], start=True, stop=True).then_inc(pe_two, 1)

        @block.vector
        def _(dve):
            v = nc.vector
            dve.wait_ge(loaded, 32)
            for l in range(2):
                for n in ("wq", "wk", "wv"):
                    v.tensor_scalar(keep[f"{n}g{l}"][:, :], w(f"{n}{l}"), w(f"n1g{l}"), None, ALU.mult)
                v.tensor_scalar(keep[f"w1g{l}"][:, :], w(f"w1{l}"), w(f"n2g{l}"), None, ALU.mult)
            for kind in range(4):
                v.tensor_tensor(keep["winbias"][:, kind * 392:(kind + 1) * 392].rearrange("p (h k) -> p h k", h=HEADS),
                                w("rpb1").rearrange("p (h k) -> p h k", h=HEADS),
                                w("winmask", kind * WTOK, (kind + 1) * WTOK).unsqueeze(1).to_broadcast([128, HEADS, WTOK]), ALU.add)
            v.tensor_copy(keep["LT"][:, 64:65], w("den"))
            dve.wait_ge(pe_one, 1)
            v.tensor_copy(keep["peb"][:, :], ps[0][:, 0:1])
            v.tensor_copy(keep["peT"][:, :], ps[1][0:32, 0:128])
            for l in range(2):
                c = 1 + 8 * l
                v.tensor_scalar(keep[f"bqg{l}"][:, :], ps[0][:, c:c + 1], w(f"bq{l}"), float(8 ** -0.5), ALU.add, ALU.mult)
                v.tensor_scalar(keep[f"bkg{l}"][:, :], ps[0][:, c + 1:c + 2], w(f"bk{l}"), None, ALU.add)
                v.tensor_scalar(keep[f"bvg{l}"][:, :], ps[0][:, c + 2:c + 3], w(f"bv{l}"), None, ALU.add)
                v.tensor_tensor(keep[f"b1g{l}"][:, :], ps[0][:, c + 3:c + 5], w(f"b1{l}"), ALU.add)
            v.tensor_copy(keep["LT"][:, 0:64], ps[3][:, 0:64])
            for i in range(2):
                v.tensor_copy(GG[:, 64 * i + 1:64 * i + 64], ps[2][0:64, 1:64])
                v.tensor_copy(GG[:, 64 * i:64 * i + 1], w("abq"))
                v.tensor_copy(JJ[:, 64 * i + 1:64 * i + 64], ps[2][0:64, 65:128])
                last = v.tensor_copy(JJ[:, 64 * i:64 * i + 1], w("abk"))
            last.then_inc(dve_one, 1)
            dve.wait_ge(pe_two, 1)
            for l in range(2):
                v.tensor_scalar(keep[f"bpg{l}"][:, :], ps[0][:, 20 + l:21 + l], w(f"bp{l}"), None, ALU.add)
            v.tensor_scalar(M32[:, :], ps[4][:, 0:128], float(CH ** -0.5), None, ALU.mult)
            v.tensor_scalar(keep["MH"][:, :], ps[4][:, 0:128], float(CH ** -0.5), None, ALU.mult).then_inc(dve_one, 1)
            dve.wait_ge(dve_one, 2)
            v.tensor_tensor(keep["ML"][:, :], M32[:, :], keep["MH"][:, :].bitcast(fp32), ALU.subtract)


def unit_at(u):
    return u * UTOK + (u // STRIPS) * TXT


def embed_phase(nc, keep, arrived):
    from contextlib import ExitStack
    import concourse.bass as bass
    from concourse import mybir
    fp32, ALU, ACT = mybir.dt.float32, mybir.AluOpType, mybir.ActivationFunctionType
    W, X, XN, peT, peb = keep["W"], keep["X"], keep["XN"], keep["peT"], keep["peb"]
    DEPTH, LAG = 4, 3

    def w(name):
        rows, at, cols = WHERE[name]
        return W[0:rows, at:at + cols]

    with ExitStack() as ctx:
        sem = lambda n: ctx.enter_context(nc.semaphore("emb_" + n))
        pe_xc, act_sq, pe_var, act_ln, act_rs, dve_t, dve_x, eps_set = map(sem, "pe_xc act_sq pe_var act_ln act_rs dve_t dve_x eps_set".split())
        buf = lambda n: [ctx.enter_context(nc.sbuf_tensor(f"emb_{n}{i}", [128, UTOK], fp32)) for i in range(DEPTH)]
        sq, ln, rs, t = buf("sq"), buf("ln"), buf("rs"), buf("t")
        eps = ctx.enter_context(nc.sbuf_tensor("emb_eps", [128, 1], fp32))
        bank = lambda n: [ctx.enter_context(nc.psum_tensor(f"emb_{n}{i}", [128, 512], fp32)) for i in range(DEPTH)]
        xc, var = bank("xc"), bank("var")
        block = ctx.enter_context(nc.Block())

        def used(engine, s, u):
            if not isinstance(u, int) or u >= DEPTH:
                engine.wait_ge(s, u - DEPTH + 1)

        def steps(engine, stages, before_loop=lambda: None):
            def step(s, k):
                for lag, stage in stages:
                    if not isinstance(s, int) or 0 <= s - lag < UNITS:
                        stage(s - lag, (k - lag) % DEPTH)

            for s in range(2 * DEPTH):
                step(s, s)
            before_loop()
            with engine.Fori(2, UNITS // DEPTH) as i:
                for k in range(DEPTH):
                    step(i * DEPTH + k, k)
            for s in range(UNITS, UNITS + LAG):
                step(s, s)

        @block.tensor
        def _(pe):
            def embed(u, k):
                used(pe, dve_t, u)
                nc.tensor.matmul(xc[k][:, 0:UTOK], peT[:, :], XN[0:32, bass.ds(u * UTOK, UTOK)], start=True, stop=True).then_inc(pe_xc, 1)

            def variance(u, k):
                pe.wait_ge(act_sq, u + 1)
                used(pe, act_ln, u)
                nc.tensor.matmul(var[k][:, 0:UTOK], w("mean2"), sq[k][:, :], start=True, stop=True).then_inc(pe_var, 1)

            pe.wait_ge(arrived[0], 16)
            steps(pe, [(0, embed), (1, variance)], lambda: pe.wait_ge(arrived[1], 16))

        @block.scalar
        def _(act):
            def squares(u, k):
                act.wait_ge(pe_xc, u + 1)
                used(act, pe_var, u)
                nc.scalar.activation(sq[k][:, :], xc[k][:, 0:UTOK], ACT.Square, bias=peb[:, :]).then_inc(act_sq, 1)

            def logarithm(u, k):
                act.wait_ge(pe_var, u + 1)
                nc.scalar.activation(ln[k][:, :], var[k][:, 0:UTOK], ACT.Ln, bias=eps[:, :]).then_inc(act_ln, 1)

            def inverse(u, k):
                act.wait_ge(act_ln, u + 1)
                used(act, dve_t, u)
                nc.scalar.activation(rs[k][:, :], ln[k][:, :], ACT.Exp, scale=-0.5).then_inc(act_rs, 1)

            nc.scalar.preload_act_table_set("natural_log_exp_and_others")
            act.wait_ge(eps_set, 1)
            steps(act, [(0, squares), (1, logarithm), (2, inverse)])

        @block.vector
        def _(dve):
            nc.vector.memset(eps[:, :], EPS).then_inc(eps_set, 1)

            def normalised(u, k):
                dve.wait_ge(act_rs, u + 1)
                used(dve, dve_x, u)
                nc.vector.scalar_tensor_tensor(t[k][:, :], xc[k][:, 0:UTOK], peb[:, :], rs[k][:, :], ALU.add, ALU.mult).then_inc(dve_t, 1)

            def gain(u, k):
                dve.wait_ge(dve_t, u + 1)
                nc.vector.tensor_scalar(X[:, bass.ds(unit_at(u), UTOK)], t[k][:, :], w("pe_g"), w("pe_nb"), ALU.mult, ALU.add).then_inc(dve_x, 1)

            steps(dve, [(2, normalised), (3, gain)])


def text_phase(nc, keep, text):
    from contextlib import ExitStack
    import math
    from concourse import mybir
    fp32, i32, ALU, ACT = mybir.dt.float32, mybir.dt.int32, mybir.AluOpType, mybir.ActivationFunctionType
    AXX = mybir.AxisListType.X
    W, X = keep["W"], keep["X"]
    GROUPS, SC, ROUND = 2, 4, float(3 << 22)

    def w(name, a=0, b=None):
        rows, at, cols = WHERE[name]
        return W[0:rows, at + a:at + (cols if b is None else b)]

    with ExitStack() as ctx:
        sem = lambda n: ctx.enter_context(nc.semaphore("txt_" + n))
        loaded, zeroed, coded, pe_c1, act_h1, pe_c2, act_h2, pe_nat, act_gate, dve_z, act_wave, dve_amp, pe_field, link = map(
            sem, "loaded zeroed coded pe_c1 act_h1 pe_c2 act_h2 pe_nat act_gate dve_z act_wave dve_amp pe_field link".split())
        tile = lambda n, c, dt=fp32, r=128: ctx.enter_context(nc.sbuf_tensor("txt_" + n, [r, c], dt))
        tok, tokf = tile("tok", IMG * TXT, i32, 64), tile("tokf", IMG * TXT, r=64)
        code, h1, h2 = tile("code", IMG * (TXT + 6), r=64), tile("h1", IMG * (TXT + 4)), tile("h2", IMG * (TXT + 2), r=64)
        code3, h13, h23 = (t[:, :].rearrange("c (b s) -> c b s", b=IMG) for t in (code, h1, h2))
        emb, lp, gate, amp = tile("emb", 128), tile("lp", 8), tile("gate", 2), tile("amp", 2)
        center, absw, widths, inv, phase, sw2 = tile("center", 2), tile("absw", 2), tile("widths", 8), tile("inv", 8), tile("phase", 2), tile("sw2", 4)
        xd, z, z2, r, whole, frac, basis, wave = tile("xd", 64), tile("z", 256), tile("z2", 256), tile("r", 256), tile("whole", 256), tile("frac", 256), tile("basis", 256), tile("wave", 256)
        field, xr = tile("field", 64), tile("xr", 256)
        ps = [ctx.enter_context(nc.psum_tensor(f"txt_ps{i}", [128, 512], fp32)) for i in range(7)]
        nat = ps[2][:, 0:160].rearrange("p (g c) -> p g c", g=GROUPS)
        block = ctx.enter_context(nc.Block())

        @block.sync
        def _(sp):
            sp.dma_start(tok[:, :], text).then_inc(loaded, 16)

        @block.gpsimd
        def _(pool):
            nc.gpsimd.memset(code[:, :], 0.0).then_inc(zeroed, 1)
            nc.gpsimd.memset(h1[:, :], 0.0).then_inc(zeroed, 1)
            nc.gpsimd.memset(h2[:, :], 0.0).then_inc(zeroed, 1)

        @block.tensor
        def _(pe):
            mm = nc.tensor.matmul
            pe.wait_ge(coded, 1)
            for k in range(7):
                last = mm(ps[0][:, 0:256], w("tw1", 128 * k, 128 * k + 128), code3[:, :, k:k + TXT], start=k == 0, stop=k == 6)
            last.then_inc(pe_c1, 1)
            pe.wait_ge(act_h1, 1)
            for k in range(5):
                last = mm(ps[1][0:64, 0:256], w("tw2", 64 * k, 64 * k + 64), h13[:, :, k:k + TXT], start=k == 0, stop=k == 4)
            last.then_inc(pe_c2, 1)
            pe.wait_ge(act_h2, 1)
            for g in range(GROUPS):
                for j in range(4):
                    image, at = 4 * g + j, slice(32 * j, 32 * j + 32)
                    mm(nat[at, g, 0:68], code3[:, image, 3:3 + TXT], w("emb"), start=True, stop=True)
                    for k in range(3):
                        last = mm(nat[at, g, 68:69], h23[:, image, k:k + TXT], w("tw3", k, k + 1), start=k == 0, stop=k == 2)
            last.then_inc(pe_nat, 1)
            pe.wait_ge(dve_amp, 1)
            for g in range(GROUPS):
                for j in range(4):
                    at, i = slice(32 * j, 32 * j + 32), j % 2
                    last = mm(ps[3 + j][64 * i:64 * i + 64, 32 * g:32 * g + 32], emb[at, 64 * g:64 * g + 64], field[at, 32 * g:32 * g + 32], start=True, stop=True)
            last.then_inc(pe_field, 1)

        @block.scalar
        def _(act):
            a = nc.scalar.activation
            act.wait_ge(zeroed, 3)
            act.wait_ge(pe_c1, 1)
            a(h13[:, :, 2:2 + TXT], ps[0][:, 0:256].rearrange("c (b s) -> c b s", b=IMG), ACT.Gelu, bias=w("tb1")).then_inc(act_h1, 1)
            act.wait_ge(pe_c2, 1)
            a(h23[:, :, 1:1 + TXT], ps[1][0:64, 0:256].rearrange("c (b s) -> c b s", b=IMG), ACT.Gelu, bias=w("tb2")).then_inc(act_h2, 1)
            act.wait_ge(pe_nat, 1)
            a(gate[:, :], nat[:, :, 68], ACT.Sigmoid, bias=w("tb3")).then_inc(act_gate, 1)
            a(amp[:, :], nat[:, :, 66], ACT.Sigmoid).then_inc(act_gate, 1)
            act.wait_ge(dve_z, 1)
            a(basis[:, :], z2[:, :], ACT.Exp, scale=-0.5).then_inc(act_wave, 1)
            act.wait_ge(dve_z, 2)
            a(wave[:, :], frac[:, :], ACT.Sin, scale=2.0 * math.pi).then_inc(act_wave, 1)

        @block.vector
        def _(dve):
            v, n = nc.vector, [0]

            def linked(ins):
                n[0] += 1
                ins.then_inc(link, 1)
                dve.wait_ge(link, n[0])

            dve.wait_ge(loaded, 16)
            linked(v.tensor_copy(tokf[:, :], tok[:, :]))
            dve.wait_ge(zeroed, 3)
            v.tensor_scalar(code3[:, :, 3:3 + TXT], tokf[:, :].rearrange("c (b s) -> c b s", b=IMG), w("chan"), None, ALU.is_equal).then_inc(coded, 1)
            dve.wait_ge(act_gate, 2)
            v.tensor_copy(emb[:, :].rearrange("p (g c) -> p g c", g=GROUPS), nat[:, :, 0:64])
            linked(v.tensor_copy(lp[:, :].rearrange("p (g c) -> p g c", g=GROUPS), nat[:, :, 64:68]))
            lp3 = lp[:, :].rearrange("p (g c) -> p g c", g=GROUPS)
            v.tensor_scalar(center[:, :], lp3[:, :, 0], 0.05, w("bpos"), ALU.mult, ALU.add)
            v.tensor_scalar(phase[:, :], lp3[:, :, 3], 0.5, 0.25, ALU.mult, ALU.add)
            v.tensor_tensor(sw2[:, :], w("scales"), w("scales"), ALU.mult)
            linked(v.scalar_tensor_tensor(absw[:, :], lp3[:, :, 1], -1.0, lp3[:, :, 1], ALU.mult, ALU.max))
            linked(v.tensor_tensor(widths[:, :].rearrange("p (g s) -> p g s", g=GROUPS), absw[:, :].unsqueeze(2).to_broadcast([128, 2, SC]),
                                   w("widths").unsqueeze(1).to_broadcast([128, 2, SC]), ALU.mult))
            linked(v.tensor_scalar(inv[:, :], widths[:, :], 1e-5, None, ALU.add))
            linked(v.reciprocal(widths[:, :], inv[:, :]))
            linked(v.tensor_tensor(xd[:, :].rearrange("p (g t) -> p g t", g=GROUPS), w("cpos").rearrange("p (g t) -> p g t", g=GROUPS),
                                   center[:, :].unsqueeze(2).to_broadcast([128, 2, TXT]), ALU.subtract))
            for g in range(GROUPS):
                last = v.tensor_tensor(z[:, 128 * g:128 * g + 128].rearrange("p (s t) -> p s t", s=SC),
                                       xd[:, TXT * g:TXT * g + TXT].unsqueeze(1).to_broadcast([128, SC, TXT]),
                                       widths[:, SC * g:SC * g + SC].unsqueeze(2).to_broadcast([128, SC, TXT]), ALU.mult)
            linked(last)
            v.tensor_tensor(z2[:, :], z[:, :], z[:, :], ALU.mult).then_inc(dve_z, 1)
            linked(v.tensor_tensor(r[:, :].rearrange("p (g t) -> p g t", g=GROUPS), z[:, :].rearrange("p (g t) -> p g t", g=GROUPS),
                                   phase[:, :].unsqueeze(2).to_broadcast([128, 2, SC * TXT]), ALU.add))
            linked(v.tensor_scalar(whole[:, :], r[:, :], ROUND, ROUND, ALU.add, ALU.subtract))
            linked(v.tensor_tensor(xr[:, :], r[:, :], whole[:, :], ALU.subtract))
            v.tensor_scalar(frac[:, :], xr[:, :], -0.4999999, 0.4999999, ALU.max, ALU.min).then_inc(dve_z, 1)
            dve.wait_ge(act_wave, 2)
            linked(v.tensor_tensor(z[:, :], basis[:, :], wave[:, :], ALU.mult))
            for g in range(GROUPS):
                last = v.tensor_tensor(r[:, 128 * g:128 * g + 128].rearrange("p (s t) -> p s t", s=SC), z[:, 128 * g:128 * g + 128].rearrange("p (s t) -> p s t", s=SC),
                                       sw2[:, :].unsqueeze(2).to_broadcast([128, SC, TXT]), ALU.mult)
            linked(last)
            for g in range(GROUPS):
                v.tensor_reduce(xd[:, TXT * g:TXT * g + TXT], r[:, 128 * g:128 * g + 128].rearrange("p (s t) -> p t s", s=SC), AXX, ALU.add)
            linked(v.tensor_tensor(phase[:, :], gate[:, :], amp[:, :], ALU.mult))
            v.tensor_tensor(field[:, :].rearrange("p (g t) -> p g t", g=GROUPS), xd[:, :].rearrange("p (g t) -> p g t", g=GROUPS),
                            phase[:, :].unsqueeze(2).to_broadcast([128, 2, TXT]), ALU.mult).then_inc(dve_amp, 1)
            dve.wait_ge(pe_field, 1)
            for g in range(GROUPS):
                for j in range(4):
                    pair, i = 2 * g + j // 2, j % 2
                    at = pair * TOK + SIDE * SIDE
                    v.tensor_copy(X[64 * i:64 * i + 64, at:at + TXT], ps[3 + j][64 * i:64 * i + 64, 32 * g:32 * g + 32])
def attention_phase(nc, keep, l):
    from contextlib import ExitStack
    import concourse.bass as bass
    from concourse import mybir
    fp32, ALU, ACT = mybir.dt.float32, mybir.AluOpType, mybir.ActivationFunctionType
    AXX = mybir.AxisListType.X
    W, X, XN = keep["W"], keep["X"], keep["XN"]
    QSCALE = float((CH // HEADS) ** -0.5)
    HP = HEADS // 2
    WQ = 2 * WTOK

    def w(name, a=0, b=None):
        rows, at, cols = WHERE[name]
        return W[0:rows, at + a:at + (cols if b is None else b)]

    g = lambda name: keep[f"{name}{l}"][:, :]
    with ExitStack() as ctx:
        sem = lambda n: ctx.enter_context(nc.semaphore(f"att{l}_{n}"))
        pe_xc, act_sq, pe_var, act_ln, act_rs, dve_xn, pe_q, act_q, pe_k, dve_k, pe_v, dve_v = map(
            sem, "pe_xc act_sq pe_var act_ln act_rs dve_xn pe_q act_q pe_k dve_k pe_v dve_v".split())
        pool_kx, pe_s, dve_add, dve_max, pool_sub, act_exp, pe_tr, act_pt, pe_pv, dve_r, dve_o = map(
            sem, "pool_kx pe_s dve_add dve_max pool_sub act_exp pe_tr act_pt pe_pv dve_r dve_o".split())
        pe_ot, act_ot, pe_pr, dve_x, pe_xc2, act_sq2, pe_var2, act_ln2, act_rs2, dve_xn2, ready, pe_go, dve_o1 = map(
            sem, "pe_ot act_ot pe_pr dve_x pe_xc2 act_sq2 pe_var2 act_ln2 act_rs2 dve_xn2 ready pe_go dve_o1".split())
        tile = lambda n, c, r=128: ctx.enter_context(nc.sbuf_tensor(f"att{l}_{n}", [r, c], fp32))
        sq, ln, rs, ksb = tile("sq", UTOK), tile("ln", UTOK), tile("rs", UTOK), tile("ksb", UTOK)
        xn = tile("xn", 2 * UTOK)
        qbd = [tile(f"qbd{i}", STRIPS * WQ) for i in range(2)]
        kx = [tile(f"kx{i}", HEADS * WTOK) for i in range(4)]
        vx = [tile(f"vx{i}", STRIPS * 144, 2 * WTOK) for i in range(2)]
        t, m = [tile(f"t{i}", 392, WQ) for i in range(2)], [tile(f"m{i}", HEADS, WQ) for i in range(2)]
        t2, e = [tile(f"t2{i}", 392, WQ) for i in range(2)], [tile(f"e{i}", 392, WQ) for i in range(2)]
        pt = [tile(f"pt{i}", HP * WQ, WQ) for i in range(2)]
        rden = tile("rden", 16, WQ)
        o = tile("o", STRIPS * CH, WQ)
        ot = tile("ot", 2 * UTOK, CH)
        sq2, ln2, rs2, eps = tile("sq2", UTOK), tile("ln2", UTOK), tile("rs2", UTOK), tile("eps", 1)
        bank = lambda n: ctx.enter_context(nc.psum_tensor(f"att{l}_ps_{n}", [128, 512], fp32))
        ps_s, ps_pt, ps_o = [bank("s0"), bank("s1")], bank("pt"), bank("o")
        outs = ps_o[0:WQ, 0:144]
        ps_a, ps_b, ps_c, ps_d = bank("a"), bank("b"), bank("c"), bank("d")
        xn4 = xn[:, :].rearrange("p (w r k) -> p w r k", w=STRIPS, r=2)
        by_window = lambda ap: ap.rearrange("p (w k) -> p w k", w=STRIPS)
        by_head = lambda ap: ap.rearrange("p (h k) -> p h k", h=HEADS)
        o3 = o[:, :].rearrange("p (w c) -> p w c", w=STRIPS)
        ot4 = ot[:, :].rearrange("c (i w k) -> c i w k", i=2, w=STRIPS)
        block = ctx.enter_context(nc.Block())

        @block.tensor
        def _(pe):
            mm = nc.tensor.matmul
            ident = w("ident")[0:WQ, 0:WQ]

            def deviations(u):
                if not (isinstance(u, int) and u == 0):
                    pe.wait_ge(dve_v, 2 * u - 1)
                mm(ps_a[:, 0:UTOK], w("center2"), X[:, bass.ds(unit_at(u), UTOK)], start=True, stop=True).then_inc(pe_xc, 1)

            def variance(u):
                pe.wait_ge(act_sq, u + 1)
                if not (isinstance(u, int) and u == 0):
                    pe.wait_ge(dve_v, 2 * u)
                mm(ps_b[:, 0:UTOK], w("mean2"), sq[:, :], start=True, stop=True).then_inc(pe_var, 1)

            def query_key(u):
                pe.wait_ge(dve_xn, u + 1)
                mm(ps_a[:, 0:UTOK], g("wqg"), xn4[:, :, 0, :], start=True, stop=True).then_inc(pe_q, 1)
                mm(ps_b[:, 0:UTOK], g("wkg"), xn4[:, :, 0, :], start=True, stop=True).then_inc(pe_k, 1)

            def values(u, half):
                pe.wait_ge(*((act_q, 2 * (u + 1)) if half == 0 else (dve_k, u + 1)))
                for k in range(4):
                    at = (4 * half + k) * 2 * WTOK
                    last = mm((ps_a, ps_b)[half][0:2 * WTOK, 128 * k:128 * k + 128], xn[:, at:at + 2 * WTOK], g("wvg"), start=True, stop=True)
                last.then_inc(pe_v, 1)

            def scores(u, wi, p):
                n = u * 8 + wi
                pe.wait_ge(pool_kx, n + 1)
                if wi == 0:
                    pe.wait_ge(act_q, 2 * (u + 1))
                if not (isinstance(u, int) and u == 0 and wi < 2):
                    pe.wait_ge(dve_add, n - 1)
                mm(ps_s[wi % 2][0:WQ, 0:392], qbd[p][:, WQ * wi:WQ * wi + WQ], kx[wi % 4][:, :], start=True, stop=True).then_inc(pe_s, 1)

            def transposes(u, wi):
                n = u * 8 + wi
                pe.wait_ge(act_exp, n + 1)
                if not (isinstance(u, int) and u == 0 and wi == 0):
                    pe.wait_ge(act_pt, n)
                for hp in range(HP):
                    last = nc.tensor.transpose(ps_pt[0:98, WQ * hp:WQ * hp + WQ], e[wi % 2][:, 98 * hp:98 * hp + 98], ident)
                last.then_inc(pe_tr, 1)

            def weighted(u, wi, p):
                n = u * 8 + wi
                pe.wait_ge(act_pt, n + 1)
                pe.wait_ge(dve_v, 2 * u + 1 + wi // 4)
                if not (isinstance(u, int) and u == 0 and wi == 0):
                    pe.wait_ge(dve_o, n)
                for hp in range(HP):
                    at = 144 * wi + 36 * hp
                    last = mm(ps_o[0:WQ, 36 * hp:36 * hp + 36], pt[wi % 2][:, WQ * hp:WQ * hp + WQ], vx[p][:, at:at + 36], start=True, stop=True)
                last.then_inc(pe_pv, 1)

            def outputs_transposed(u):
                pe.wait_ge(dve_o, 8 * (u + 1))
                if not (isinstance(u, int) and u == 0):
                    pe.wait_ge(dve_xn2, u)
                pe.sem_inc(pe_go, 1)
                for wi in range(8):
                    last = nc.tensor.transpose((ps_c, ps_d)[wi // 4][0:CH, WQ * (wi % 4):WQ * (wi % 4) + WQ], o3[:, wi, :], ident)
                last.then_inc(pe_ot, 1)

            def project(u):
                pe.wait_ge(act_ot, 2 * (u + 1))
                pe.sem_inc(pe_go, 1)
                for i in range(2):
                    last = mm(ps_c[64 * i:64 * i + 64, 0:UTOK], w(f"wp{l}", 0, 64), ot[:, UTOK * i:UTOK * i + UTOK], start=True, stop=True)
                last.then_inc(pe_pr, 1)

            def deviations2(u):
                pe.wait_ge(dve_x, u + 1)
                mm(ps_d[:, 0:UTOK], w("center2"), X[:, bass.ds(unit_at(u), UTOK)], start=True, stop=True).then_inc(pe_xc2, 1)

            def variance2(u):
                pe.wait_ge(act_sq2, u + 1)
                mm(ps_c[:, 0:UTOK], w("mean2"), sq2[:, :], start=True, stop=True).then_inc(pe_var2, 1)

            def unit(u, p, first=False, last=False):
                for st in range(11):
                    if st < 8:
                        scores(u, st, p)
                    if st == 1 and not first:
                        outputs_transposed(u - 1)
                    if st == 1 and not last:
                        deviations(u + 1)
                    if st == 3 and not last:
                        variance(u + 1)
                    if st == 3 and not first:
                        project(u - 1)
                    if st == 5 and not first:
                        deviations2(u - 1)
                    if 2 <= st < 10:
                        transposes(u, st - 2)
                    if st == 5 and not last:
                        query_key(u + 1)
                    if st == 7 and not first:
                        variance2(u - 1)
                    if st >= 3:
                        weighted(u, st - 3, p)
                    if st in (8, 9) and not last:
                        values(u + 1, st - 8)

            pe.wait_ge(ready, 1)
            deviations(0)
            variance(0)
            query_key(0)
            values(0, 0)
            values(0, 1)
            unit(0, 0, first=True)
            with pe.Fori(0, UNITS // 2 - 1) as i:
                for k in (1, 2):
                    unit(i * 2 + k, k % 2)
            unit(UNITS - 1, 1, last=True)
            outputs_transposed(UNITS - 1)
            project(UNITS - 1)
            deviations2(UNITS - 1)
            variance2(UNITS - 1)

        @block.scalar
        def _(act):
            a = nc.scalar.activation

            def squares(u):
                act.wait_ge(pe_xc, u + 1)
                if not (isinstance(u, int) and u == 0):
                    act.wait_ge(pe_var, u)
                a(sq[:, :], ps_a[:, 0:UTOK], ACT.Square).then_inc(act_sq, 1)

            def deviation_scale(u):
                act.wait_ge(pe_var, u + 1)
                a(ln[:, :], ps_b[:, 0:UTOK], ACT.Ln, bias=eps[:, :]).then_inc(act_ln, 1)
                act.wait_ge(act_ln, u + 1)
                if not (isinstance(u, int) and u == 0):
                    act.wait_ge(dve_xn, u)
                a(rs[:, :], ln[:, :], ACT.Exp, scale=-0.5).then_inc(act_rs, 1)

            def queries(u, p):
                act.wait_ge(pe_q, u + 1)
                if not (isinstance(u, int) and u < 2):
                    act.wait_ge(pe_s, 8 * (u - 1))
                for i in range(2):
                    at = slice(64 * i, 64 * i + 64)
                    a(qbd[p][at, :].rearrange("c (w k) -> c w k", w=STRIPS)[:, :, WTOK * i:WTOK * i + WTOK], by_window(ps_a[at, 0:UTOK]),
                      ACT.Identity, bias=g("bqg")[at, :], scale=QSCALE).then_inc(act_q, 1)

            def exponentials(u, wi):
                n = u * 8 + wi
                act.wait_ge(pool_sub, n + 1)
                if not (isinstance(u, int) and u == 0 and wi < 2):
                    act.wait_ge(pe_tr, n - 1)
                a(e[wi % 2][:, :], t2[wi % 2][:, :], ACT.Exp).then_inc(act_exp, 1)

            def probabilities(u, wi):
                n = u * 8 + wi
                act.wait_ge(pe_tr, n + 1)
                if not (isinstance(u, int) and u == 0 and wi < 2):
                    act.wait_ge(pe_pv, n - 1)
                a(pt[wi % 2][:, :], ps_pt[0:98, 0:HP * WQ], ACT.Copy).then_inc(act_pt, 1)

            def outputs(u):
                act.wait_ge(pe_ot, u + 1)
                if not (isinstance(u, int) and u == 0):
                    act.wait_ge(pe_pr, u)
                for h in range(2):
                    a(ot4[:, :, 4 * h:4 * h + 4, :].rearrange("c i w k -> c w i k"),
                      (ps_c, ps_d)[h][0:CH, 0:4 * WQ].rearrange("c (w i k) -> c w i k", w=4, i=2), ACT.Copy).then_inc(act_ot, 1)

            def squares2(u):
                act.wait_ge(pe_xc2, u + 1)
                if not (isinstance(u, int) and u == 0):
                    act.wait_ge(pe_var2, u)
                a(sq2[:, :], ps_d[:, 0:UTOK], ACT.Square).then_inc(act_sq2, 1)

            def deviation_scale2(u):
                act.wait_ge(pe_var2, u + 1)
                a(ln2[:, :], ps_c[:, 0:UTOK], ACT.Ln, bias=eps[:, :]).then_inc(act_ln2, 1)
                act.wait_ge(act_ln2, u + 1)
                if not (isinstance(u, int) and u == 0):
                    act.wait_ge(dve_xn2, u)
                a(rs2[:, :], ln2[:, :], ACT.Exp, scale=-0.5).then_inc(act_rs2, 1)

            def unit(u, p, first=False, last=False):
                for st in range(11):
                    if 1 <= st <= 8:
                        exponentials(u, st - 1)
                    if st == 1 and not first:
                        outputs(u - 1)
                    if st == 1 and not last:
                        squares(u + 1)
                    if 2 <= st < 10:
                        probabilities(u, st - 2)
                    if st == 3 and not last:
                        deviation_scale(u + 1)
                    if st == 5 and not last:
                        queries(u + 1, 1 - p)
                    if st == 5 and not first:
                        squares2(u - 1)
                    if st == 7 and not first:
                        deviation_scale2(u - 1)

            nc.scalar.preload_act_table_set("natural_log_exp_and_others")
            act.wait_ge(ready, 1)
            squares(0)
            deviation_scale(0)
            queries(0, 0)
            unit(0, 0, first=True)
            with act.Fori(0, UNITS // 2 - 1) as i:
                for k in (1, 2):
                    unit(i * 2 + k, k % 2)
            unit(UNITS - 1, 1, last=True)
            outputs(UNITS - 1)
            squares2(UNITS - 1)
            deviation_scale2(UNITS - 1)

        @block.vector
        def _(dve):
            v = nc.vector
            for i in range(2):
                v.memset(qbd[i][:, :], 0.0)
                for wi in range(STRIPS):
                    last = v.tensor_copy(vx[i][:, 144 * wi:144 * wi + 144], w("vones"))
            v.memset(eps[:, :], EPS).then_inc(ready, 1)

            def normalised(u):
                dve.wait_ge(act_rs, u + 1)
                if not (isinstance(u, int) and u == 0):
                    dve.wait_ge(pe_v, 2 * u)
                v.tensor_tensor(xn4, by_window(ps_a[:, 0:UTOK]).unsqueeze(2).to_broadcast([128, STRIPS, 2, WTOK]),
                                by_window(rs[:, :]).unsqueeze(2).to_broadcast([128, STRIPS, 2, WTOK]), ALU.mult).then_inc(dve_xn, 1)

            def keys(u):
                dve.wait_ge(pe_k, u + 1)
                if not (isinstance(u, int) and u == 0):
                    dve.wait_ge(pool_kx, 8 * u)
                v.tensor_scalar(ksb[:, :], ps_b[:, 0:UTOK], g("bkg"), None, ALU.add).then_inc(dve_k, 1)

            def values(u, half, p):
                dve.wait_ge(pe_v, 2 * u + 1 + half)
                if not (isinstance(u, int) and u < 2):
                    dve.wait_ge(pe_pv, 8 * (u - 1))
                src = (ps_a, ps_b)[half][0:98, :].rearrange("t (w i c) -> t w i c", w=4, i=2)
                dst = vx[p][:, 576 * half:576 * half + 576].rearrange("t (w q i c) -> t w q i c", w=4, q=HP, i=2)
                for i in range(2):
                    last = v.tensor_tensor(dst[:, :, :, i, 0:16], src[:, :, i, :].rearrange("t w (q c) -> t w q c", q=HP),
                                           w("vbmask", 0, 16).unsqueeze(1).unsqueeze(1).to_broadcast([98, 4, HP, 16]), ALU.mult)
                last.then_inc(dve_v, 1)

            def add(u, wi, row_kind):
                n = u * 8 + wi
                dve.wait_ge(pe_s, n + 1)
                if not (isinstance(u, int) and u == 0 and wi < 2):
                    dve.wait_ge(pool_sub, n - 1)
                if l == 0:
                    bias = w("rpb0")[0:WQ, :]
                else:
                    bias = keep["winbias"][0:WQ, bass.ds((row_kind * 2 + int(wi == STRIPS - 1)) * 392, 392)]
                v.tensor_tensor(t[wi % 2][:, :], ps_s[wi % 2][0:WQ, 0:392], bias, ALU.add).then_inc(dve_add, 1)

            def maxima(u, wi):
                n = u * 8 + wi
                dve.wait_ge(dve_add, n + 1)
                v.tensor_reduce(m[wi % 2][:, :], by_head(t[wi % 2][:, :]), AXX, ALU.max).then_inc(dve_max, 1)

            def sums(u, wi):
                n = u * 8 + wi
                dve.wait_ge(pe_pv, n + 1)
                if not (isinstance(u, int) and u == 0 and wi == 0):
                    dve.wait_ge(dve_o, n)
                v.reciprocal(rden[:, :].rearrange("p (q i h) -> p q i h", q=HP, i=2),
                             outs.rearrange("p (q i c) -> p q i c", q=HP, i=2)[:, :, :, 16:18]).then_inc(dve_r, 1)

            def scaled(wi, i, rows):
                return v.tensor_tensor(o3[0:rows, wi, :].rearrange("p (q h c) -> p q h c", q=HP, h=2),
                                       outs[0:rows, :].rearrange("p (q i c) -> p q i c", q=HP, i=2)[:, :, i, 0:16].rearrange("p q (h c) -> p q h c", h=2),
                                       rden[0:rows, :].rearrange("p (q i h) -> p q i h", q=HP, i=2)[:, :, i, :].unsqueeze(3).to_broadcast([rows, HP, 2, 8]), ALU.mult)

            def outputs(u, wi):
                dve.wait_ge(dve_r, u * 8 + wi + 1)
                if wi == 0 and not (isinstance(u, int) and u == 0):
                    dve.wait_ge(pe_ot, u)
                scaled(wi, 1, WQ).then_inc(dve_o1, 1)

            def outputs0(u, wi):
                dve.wait_ge(dve_o1, u * 8 + wi + 1)
                scaled(wi, 0, WTOK).then_inc(dve_o, 1)

            def residual(u):
                dve.wait_ge(pe_pr, u + 1)
                at = X[:, bass.ds(unit_at(u), UTOK)]
                v.scalar_tensor_tensor(at, ps_c[:, 0:UTOK], g("bpg"), at, ALU.add, ALU.add).then_inc(dve_x, 1)

            def normalised2(u):
                dve.wait_ge(act_rs2, u + 1)
                v.tensor_tensor(XN[:, bass.ds(unit_at(u), UTOK)], ps_d[:, 0:UTOK], rs2[:, :], ALU.mult).then_inc(dve_xn2, 1)

            def unit(u, p, first=False, last=False):
                row_kind = 0
                if l == 1:
                    row_kind = (u % STRIPS) // (STRIPS - 1)
                for st in range(12):
                    if st >= 4:
                        sums(u, st - 4)
                    if 1 <= st <= 8:
                        maxima(u, st - 1)
                    if st >= 4:
                        outputs(u, st - 4)
                    if st < 8:
                        add(u, st, row_kind)
                    if st >= 4:
                        outputs0(u, st - 4)
                    if st == 4 and not first:
                        residual(u - 1)
                    if st == 4 and not last:
                        normalised(u + 1)
                    if st == 6 and not last:
                        keys(u + 1)
                    if st == 8 and not first:
                        normalised2(u - 1)
                    if st in (9, 10) and not last:
                        values(u + 1, st - 9, 1 - p)

            normalised(0)
            keys(0)
            values(0, 0, 0)
            values(0, 1, 0)
            unit(0, 0, first=True)
            with dve.Fori(0, UNITS // 2 - 1) as i:
                for k in (1, 2):
                    unit(i * 2 + k, k % 2)
            unit(UNITS - 1, 1, last=True)
            residual(UNITS - 1)
            normalised2(UNITS - 1)

        @block.gpsimd
        def _(pool):
            def expand(u, wi):
                n = u * 8 + wi
                if wi == 0:
                    pool.wait_ge(dve_k, u + 1)
                if not (isinstance(u, int) and u == 0 and wi < 4):
                    pool.wait_ge(pe_s, n - 3)
                nc.gpsimd.tensor_tensor(by_head(kx[wi % 4][:, :]), ksb[:, WTOK * wi:WTOK * wi + WTOK].unsqueeze(1).to_broadcast([128, HEADS, WTOK]),
                                        w("headmask").unsqueeze(2).to_broadcast([128, HEADS, WTOK]), ALU.mult).then_inc(pool_kx, 1)

            def subtract(u, wi):
                n = u * 8 + wi
                pool.wait_ge(dve_max, n + 1)
                if not (isinstance(u, int) and u == 0 and wi < 2):
                    pool.wait_ge(act_exp, n - 1)
                nc.gpsimd.tensor_tensor(by_head(t2[wi % 2][:, :]), by_head(t[wi % 2][:, :]), m[wi % 2][:, :].unsqueeze(2).to_broadcast([WQ, HEADS, WTOK]),
                                        ALU.subtract).then_inc(pool_sub, 1)

            def unit(u, last=False):
                for wi in range(8):
                    if wi + 2 < 8:
                        expand(u, wi + 2)
                    subtract(u, wi)
                if not last:
                    expand(u + 1, 0)
                    expand(u + 1, 1)

            expand(0, 0)
            expand(0, 1)
            unit(0)
            with pool.Fori(0, UNITS // 2 - 1) as i:
                for k in (1, 2):
                    unit(i * 2 + k)
            unit(UNITS - 1, last=True)


def mlp_phase(nc, keep, l):
    from contextlib import ExitStack
    import concourse.bass as bass
    from concourse import mybir
    fp32, ALU, ACT = mybir.dt.float32, mybir.AluOpType, mybir.ActivationFunctionType
    W, X, XN = keep["W"], keep["X"], keep["XN"]
    w1, b1 = keep[f"w1g{l}"], keep[f"b1g{l}"]
    HALVES = [(i, c) for c in range(2) for i in range(2)]

    def w(name, a=0, b=None):
        rows, at, cols = WHERE[name]
        return W[0:rows, at + a:at + (cols if b is None else b)]

    with ExitStack() as ctx:
        sem = lambda n: ctx.enter_context(nc.semaphore(f"mlp{l}_{n}"))
        pe_h, act_h, pe_y, dve_y = map(sem, "pe_h act_h pe_y dve_y".split())
        hid = [[ctx.enter_context(nc.sbuf_tensor(f"mlp{l}_h{p}{k}", [128, UTOK], fp32)) for k in range(4)] for p in range(2)]
        ps_h = [ctx.enter_context(nc.psum_tensor(f"mlp{l}_ps_h{k}", [128, 512], fp32)) for k in range(4)]
        ps_y = [ctx.enter_context(nc.psum_tensor(f"mlp{l}_ps_y{k}", [128, 512], fp32)) for k in range(2)]
        block = ctx.enter_context(nc.Block())

        @block.tensor
        def _(pe):
            mm = nc.tensor.matmul

            def up(u):
                for k, (i, c) in enumerate(HALVES):
                    if not (isinstance(u, int) and u == 0):
                        pe.wait_ge(act_h, 4 * u - 3 + k)
                    at = 256 * i + 128 * c
                    mm(ps_h[k][:, 0:UTOK], w1[:, at:at + 128], XN[:, bass.ds(unit_at(u), UTOK)], start=True, stop=True).then_inc(pe_h, 1)

            def down(u, p):
                if not (isinstance(u, int) and u < 2):
                    pe.wait_ge(dve_y, u - 1)
                for k, (i, c) in enumerate(HALVES):
                    pe.wait_ge(act_h, 4 * u + 1 + k)
                    last = mm(ps_y[p][64 * i:64 * i + 64, 0:UTOK], w(f"w2{l}", 64 * c, 64 * c + 64), hid[p][k][:, :], start=c == 0, stop=c == 1)
                last.then_inc(pe_y, 1)

            up(0)
            up(1)
            down(0, 0)
            with pe.Fori(0, UNITS // 2 - 1) as j:
                for k in range(2):
                    up(j * 2 + (k + 2))
                    down(j * 2 + (k + 1), 1 - k)
            down(UNITS - 1, 1)

        @block.scalar
        def _(act):
            def gelu(u, p):
                if not (isinstance(u, int) and u < 2):
                    act.wait_ge(pe_y, u - 1)
                for k, (i, c) in enumerate(HALVES):
                    act.wait_ge(pe_h, 4 * u + 1 + k)
                    nc.scalar.activation(hid[p][k][:, :], ps_h[k][:, 0:UTOK], ACT.Gelu, bias=b1[:, c:c + 1]).then_inc(act_h, 1)

            gelu(0, 0)
            gelu(1, 1)
            with act.Fori(0, UNITS // 2 - 1) as j:
                for k in range(2):
                    gelu(j * 2 + (k + 2), k)

        @block.vector
        def _(dve):
            with dve.Fori(0, UNITS // 2) as j:
                for k in range(2):
                    u = j * 2 + k
                    dve.wait_ge(pe_y, u + 1)
                    at = X[:, bass.ds(unit_at(u), UTOK)]
                    nc.vector.scalar_tensor_tensor(at, ps_y[k][:, 0:UTOK], w(f"b2{l}"), at, ALU.add, ALU.add).then_inc(dve_y, 1)


def roll_phase(nc, keep):
    import concourse.bass as bass
    X, XN = keep["X"], keep["XN"]
    S = WIN // 2

    def views(t, col):
        return t[:, bass.ds(col, UTOK)].rearrange("p (w r c) -> p w r c", w=STRIPS, r=WIN)

    def shift(copy, u, carry):
        s = u % STRIPS
        src = views(X, (u // STRIPS) * TOK + ((s + carry) % STRIPS) * UTOK)
        dst = views(XN, unit_at(u))
        rd, rs = (slice(0, WIN - S), slice(S, WIN)) if carry == 0 else (slice(WIN - S, WIN), slice(0, S))
        copy(dst[:, :, rd, 0:WIN - S], src[:, :, rs, S:WIN])
        copy(dst[:, 0:STRIPS - 1, rd, WIN - S:WIN], src[:, 1:STRIPS, rs, 0:S])
        copy(dst[:, STRIPS - 1, rd, WIN - S:WIN], src[:, 0, rs, 0:S])

    with nc.Block() as block:
        @block.vector
        def _(dve):
            for pair in range(PAIRS):
                at = pair * TOK + SIDE * SIDE
                nc.vector.tensor_copy(XN[:, at:at + TXT], X[:, at:at + TXT])
            with dve.Fori(0, UNITS) as u:
                shift(nc.vector.tensor_copy, u, 0)

        @block.gpsimd
        def _(pool):
            with pool.Fori(0, UNITS) as u:
                shift(nc.gpsimd.tensor_copy, u, 1)


def global_phase(nc, keep, out):
    from contextlib import ExitStack
    import concourse.bass as bass
    from concourse import mybir
    fp32, f32r, bf16 = mybir.dt.float32, mybir.dt.float32r, mybir.dt.bfloat16
    ALU, ACT, AXX = mybir.AluOpType, mybir.ActivationFunctionType, mybir.AxisListType.X
    W, X = keep["W"], keep["X"]
    QC, SUBS = 352, 3
    CHUNKS, QP = TOK // QC, SUBS * 128
    KT = -(-TOK // 128)
    NC, NCH = 396, TOK // 396
    MAXES = SUBS * NCH
    CREDIT = 2
    PREPARED = 3

    def rows_of(t):
        return min(128, TOK - 128 * t)

    def w(name, a=0, b=None):
        rows, at, cols = WHERE[name]
        return W[0:rows, at + a:at + (cols if b is None else b)]

    with ExitStack() as ctx:
        made = {}

        def sems(names):
            for n in names.split():
                made[n] = ctx.enter_context(nc.semaphore("gl_" + n))
            return [made[n] for n in names.split()]

        BY_DVE = "dve_lh dve_t dve_yf dve_hi dve_lo dve_mx dve_neg dve_m0 dve_ql dve_h1 dve_x2 dve_oh dve_ohm dve_res dve_xlo link"
        BY_ACT = "act_sq act_ln act_rs act_yn act_qpre act_qh act_p act_o act_x act_r1 act_r2 act_x2t act_oht act_hid act_xhl"
        BY_PE = "pe_xc pe_var pe_yt pe_qt pe_mx pe_fix pe_s pe_pv pe_p2 pe_x2t pe_lg pe_oht pe_hid pe_ff"
        dve_lh, dve_t, dve_yf, dve_hi, dve_lo, dve_mx, dve_neg, dve_m0, dve_ql, dve_h1, dve_x2, dve_oh, dve_ohm, dve_res, dve_xlo, link = sems(BY_DVE)
        act_sq, act_ln, act_rs, act_yn, act_qpre, act_qh, act_p, act_o, act_x, act_r1, act_r2, act_x2t, act_oht, act_hid, act_xhl = sems(BY_ACT)
        pe_xc, pe_var, pe_yt, pe_qt, pe_mx, pe_fix, pe_s, pe_pv, pe_p2, pe_x2t, pe_lg, pe_oht, pe_hid, pe_ff = sems(BY_PE)
        pool_x, stored, ready, pe_go = sems("pool_x stored ready pe_go")

        def credit(engine, names):
            for n in names.split():
                engine.sem_inc(made[n], CREDIT)

        def after(engine, s, k):
            engine.wait_ge(s, k + CREDIT)

        tile = lambda n, c, dt=fp32, r=128: ctx.enter_context(nc.sbuf_tensor("gl_" + n, [r, c], dt))
        lh, eps = tile("lh", 128), tile("eps", 1)
        two = lambda n, c, dt=fp32: [tile(f"{n}{i}", c, dt) for i in range(2)]
        sq, ln, rs, t = two("sq", NC), two("ln", NC), two("rs", NC), two("t", NC)
        yf, yhl, yn = tile("yf", TOK), tile("yhl", TOK, f32r), tile("yn", KT * CH)
        qpre, qh, ql = tile("qpre", QP, f32r), tile("qh", QC, f32r), tile("ql", QC, f32r)
        mp, neg, m0 = tile("mp", MAXES), tile("neg", SUBS), tile("m0", SUBS * 128)
        p = [tile(f"p{i}", QC) for i in range(4)]
        osb, xc, xnat, rden, h1 = tile("o", QP), tile("xc", QP), tile("xnat", SUBS * CH), tile("rden", SUBS), tile("h1", SUBS * CH)
        ms, dev, dsq, vs, lv, rstd, x2 = tile("ms", SUBS), tile("dev", SUBS * CH), tile("dsq", SUBS * CH), tile("vs", SUBS), tile("lv", SUBS), tile("rstd", SUBS), tile("x2", QP)
        x2t, xhl = tile("x2t", QP, r=CH + 1), tile("xhl", QP, f32r)
        w1h, w1l, w1z = tile("w1h", 512, f32r), tile("w1l", 512, f32r), tile("w1z", 512)
        top, eq, cand, best, oh = tile("top", SUBS), tile("eq", SUBS * EXPERTS), tile("cand", SUBS * EXPERTS), tile("best", SUBS), tile("oh", SUBS * EXPERTS)
        oht, ohm, big = tile("oht", QP, r=EXPERTS), tile("ohm", QP, bf16, EXPERTS), tile("big", 512, bf16, EXPERTS)
        hid = [tile(f"hid{c}", QP) for c in range(4)]
        res = tile("res", SUBS * CH)
        ps_s0, ps_s1, ps_m0, ps_m1, ps_o, ps_q, ps_a, ps_b = (ctx.enter_context(nc.psum_tensor(f"gl_ps{i}", [128, 512], fp32)) for i in range(8))
        ps_s, ps_m = [ps_s0, ps_s1], [ps_m0, ps_m1]
        ps_x = [ps_s0, ps_s1, ps_o, ps_q]
        sub = lambda ap: ap.rearrange("p (a c) -> p a c", a=SUBS)
        block = ctx.enter_context(nc.Block())
        SECOND = {1: "p2", 10: "x2t", 12: "lg", 16: "oht", 19: "hid0", 20: "hid1", 21: "hid2", 22: "hid3", 24: "ff"}
        max_step = lambda k: 2 + k * 22 // MAXES

        @block.tensor
        def _(pe):
            mm, tr = nc.tensor.matmul, nc.tensor.transpose
            credit(pe, BY_PE)

            def rotate(b, c):
                if c == 0:
                    after(pe, dve_lh, b + 1)
                if c >= 4:
                    after(pe, dve_t, NCH * b + c - 3)
                mm(ps_x[c % 4][:, 0:NC], lh[:, :], X[:, bass.ds((b // 2) * TOK + c * NC, NC)], start=True, stop=True).then_inc(pe_xc, 1)

            def variance(b, c):
                after(pe, act_sq, NCH * b + c + 1)
                after(pe, act_ln, NCH * b + c - 1)
                mm(ps_m[c % 2][:, 0:NC], w("mean128"), sq[c % 2][:, :], start=True, stop=True).then_inc(pe_var, 1)

            def rows_of_y(b, g):
                after(pe, dve_yf, NCH * b + min(NCH, -(-min(TOK, 1024 * (g + 1)) // NC)))
                after(pe, act_yn, 4 * b + g - 1)
                if g == 0:
                    after(pe, dve_res, CHUNKS * b - 1)
                pe.sem_inc(pe_go, 1)
                for k in range(8 * g, min(KT, 8 * g + 8)):
                    n = rows_of(k)
                    last = tr((ps_a, ps_b)[g % 2][0:n, 64 * (k % 8):64 * (k % 8) + 64], yf[0:CH, 128 * k:128 * k + n], w("ident")[0:CH, 0:CH])
                last.then_inc(pe_yt, 1)

            def queries(n, j):
                after(pe, dve_ql, n)
                at = yhl[:, bass.ds(j * QC, QC)]
                mm(ps_q[:, 0:QC], keep["MH"][:, :], at, start=True, stop=False)
                mm(ps_q[:, 0:QC], keep["ML"][:, :], at, start=False, stop=True).then_inc(pe_qt, 1)

            def maxima(n, k):
                a, c = k // NCH, k % NCH
                if k == 0:
                    after(pe, act_qpre, n + 1)
                after(pe, dve_mx, MAXES * n + k - 1)
                mm(ps_m[k % 2][:, 0:NC], qpre[:, 128 * a:128 * a + 128], yhl[:, c * NC:c * NC + NC], start=True, stop=True).then_inc(pe_mx, 1)

            def take_maxima(n):
                after(pe, dve_m0, n + 1)
                for a in range(SUBS):
                    k = min(128, QC - 128 * a)
                    last = mm(ps_q[:, 128 * a:128 * a + k], m0[:, 128 * a:128 * a + 128], w("ident")[:, 0:k], start=False, stop=True, skip_group_check=True)
                last.then_inc(pe_fix, 1)

            def scores(n, k):
                if k == 0:
                    after(pe, dve_ql, n + 1)
                after(pe, act_p, KT * n + k - 1)
                r = rows_of(k)
                o = ps_s[k % 2][0:r, 0:QC]
                mm(o, yhl[:, 128 * k:128 * k + r], qh[:, :], start=True, stop=False)
                mm(o, yhl[:, 128 * k:128 * k + r], ql[:, :], start=False, stop=True).then_inc(pe_s, 1)

            def weighted(n, k):
                after(pe, act_p, KT * n + k + 1)
                if k == 0:
                    after(pe, act_o, n)
                r, half = rows_of(k), slice(64 * (k % 2), 64 * (k % 2) + 64)
                mm(ps_o[half, 0:QC], yn[0:r, CH * k:CH * k + CH], p[k % 4][0:r, :], start=k < 2, stop=k >= KT - 2).then_inc(pe_pv, 1)

            def second(n, what):
                if what == "p2":
                    after(pe, act_o, n + 1)
                    after(pe, pool_x, n + 1)
                    after(pe, dve_res, n)
                    for a in range(SUBS):
                        mm(ps_a[:, 65 * a:65 * a + 65], osb[:, 128 * a:128 * a + 128], keep["LT"][:, :], start=True, stop=True)
                        last = mm(ps_a[:, 256 + CH * a:256 + CH * a + CH], xc[:, 128 * a:128 * a + 128], w("pick", 0, 128)[:, bass.ds(n // CHUNKS % 2 * CH, CH)], start=True, stop=True)
                    last.then_inc(pe_p2, 1)
                elif what == "x2t":
                    after(pe, dve_x2, n + 1)
                    after(pe, act_hid, 4 * n)
                    for a in range(SUBS):
                        last = tr(ps_b[:, 128 * a:128 * a + 128], x2[:, 128 * a:128 * a + 128], w("ident"))
                    last.then_inc(pe_x2t, 1)
                elif what == "lg":
                    after(pe, act_x2t, n + 1)
                    for a in range(SUBS):
                        last = mm(ps_a[:, EXPERTS * a:EXPERTS * a + EXPERTS], x2t[:, 128 * a:128 * a + 128], w("rw"), start=True, stop=True)
                    last.then_inc(pe_lg, 1)
                elif what == "oht":
                    after(pe, dve_oh, n + 1)
                    after(pe, dve_xlo, n + 1)
                    for a in range(SUBS):
                        last = tr(ps_b[0:EXPERTS, 128 * a:128 * a + 128], oh[:, EXPERTS * a:EXPERTS * a + EXPERTS], w("ident"))
                    last.then_inc(pe_oht, 1)
                elif what.startswith("hid"):
                    c = int(what[3])
                    if c == 0:
                        after(pe, dve_ohm, n + 1)
                    if c >= 2:
                        after(pe, act_hid, 4 * n + c - 1)
                    o = (ps_a, ps_b)[c % 2][:, 0:QP]
                    mm(o, w1h[:, 128 * c:128 * c + 128], xhl[:, :], start=True, stop=False)
                    mm(o, w1l[:, 128 * c:128 * c + 128], xhl[:, :], start=False, stop=False)
                    mm(o, big[:, 128 * c:128 * c + 128], ohm[:, :], start=False, stop=True).then_inc(pe_hid, 1)
                else:
                    after(pe, act_hid, 4 * n + 4)
                    for a in range(SUBS):
                        for c in range(4):
                            mm(ps_a[:, CH * a:CH * a + CH], hid[c][:, 128 * a:128 * a + 128], w("fw2", CH * c, CH * c + CH), start=c == 0, stop=False)
                        last = mm(ps_a[:, CH * a:CH * a + CH], oht[:, 128 * a:128 * a + 128], w("fb2"), start=False, stop=True)
                    last.then_inc(pe_ff, 1)

            def chunk(n, j, first=False, last=False):
                for k in range(KT):
                    scores(n, k)
                    if not last:
                        if k == 0:
                            queries(n + 1, j + 1)
                        for q in range(MAXES):
                            if max_step(q) == k:
                                maxima(n + 1, q)
                    if not first and k in SECOND:
                        second(n - 1, SECOND[k])
                    if k % 2 and k >= 3:
                        weighted(n, k - 3)
                        weighted(n, k - 2)
                if not last:
                    take_maxima(n + 1)
                for k in range(KT - 3, KT):
                    weighted(n, k)

            def image(b, first=False):
                rotate(b, 0)
                for c in range(NCH):
                    if c + 1 < NCH:
                        rotate(b, c + 1)
                    variance(b, c)
                n0 = b * CHUNKS
                after(pe, dve_t, NCH * (b + 1))
                after(pe, dve_lo, NCH * b + 1)
                queries(n0, 0)
                for g in range(4):
                    rows_of_y(b, g)
                after(pe, act_ln, NCH * (b + 1))
                for k in range(MAXES):
                    if k < NCH:
                        after(pe, dve_lo, NCH * b + k + 1)
                    maxima(n0, k)
                take_maxima(n0)
                after(pe, act_yn, 4 * b + 4)
                chunk(n0, 0, first=first)
                with pe.Fori(1, CHUNKS - 1) as j:
                    chunk(n0 + j, j)
                chunk(n0 + (CHUNKS - 1), CHUNKS - 1, last=True)

            pe.wait_ge(ready, PREPARED)
            image(0, first=True)
            with pe.Fori(1, IMG) as b:
                image(b)
            for what in SECOND.values():
                second(IMG * CHUNKS - 1, what)

        @block.scalar
        def _(act):
            a_ = nc.scalar.activation
            credit(act, BY_ACT)

            def squares(b, c):
                after(act, pe_xc, NCH * b + c + 1)
                after(act, pe_var, NCH * b + c - 1)
                a_(sq[c % 2][:, :], ps_x[c % 4][:, 0:NC], ACT.Square).then_inc(act_sq, 1)

            def logarithm(b, c):
                after(act, pe_var, NCH * b + c + 1)
                a_(ln[c % 2][:, :], ps_m[c % 2][:, 0:NC], ACT.Ln, bias=eps[:, :]).then_inc(act_ln, 1)

            def inverse(b, c):
                after(act, act_ln, NCH * b + c + 1)
                after(act, dve_t, NCH * b + c - 1)
                a_(rs[c % 2][:, :], ln[c % 2][:, :], ACT.Exp, scale=-0.5).then_inc(act_rs, 1)

            def rows_of_y(b, g):
                after(act, pe_yt, 4 * b + g + 1)
                k = min(KT, 8 * g + 8) - 8 * g
                r = 128 if k == 8 else rows_of(KT - 1)
                a_(yn[0:r, 512 * g:512 * g + CH * k], (ps_a, ps_b)[g % 2][0:r, 0:CH * k], ACT.Copy).then_inc(act_yn, 1)

            def queries(n):
                after(act, pe_qt, n + 1)
                after(act, pe_mx, MAXES * n)
                a_(qpre[:, 0:QC], ps_q[:, 0:QC], ACT.Copy).then_inc(act_qpre, 1)

            def queries_high(n):
                after(act, pe_fix, n + 1)
                after(act, pe_s, KT * n)
                a_(qh[:, :], ps_q[:, 0:QC], ACT.Copy).then_inc(act_qh, 1)

            def exponentials(n, k):
                r = rows_of(k)
                after(act, pe_s, KT * n + k + 1)
                after(act, pe_pv, KT * n + k - 3 if k > 1 else KT * n)
                a_(p[k % 4][0:r, :], ps_s[k % 2][0:r, 0:QC], ACT.Exp).then_inc(act_p, 1)

            def sums(n):
                after(act, pe_pv, KT * (n + 1))
                after(act, pe_p2, n)
                a_(osb[:, 0:QC], ps_o[:, 0:QC], ACT.Copy).then_inc(act_o, 1)

            def second(n, what):
                if what == "x":
                    after(act, pe_p2, n + 1)
                    after(act, dve_h1, n)
                    a_(xnat[:, :], ps_a[:, 256:256 + SUBS * CH], ACT.Copy).then_inc(act_x, 1)
                elif what == "rstd":
                    after(act, dve_h1, n + 1)
                    a_(lv[:, :], vs[:, :], ACT.Ln, bias=eps[:, :], scale=1.0 / CH).then_inc(act_r1, 1)
                    after(act, act_r1, n + 1)
                    a_(rstd[:, :], lv[:, :], ACT.Exp, scale=-0.5).then_inc(act_r2, 1)
                elif what == "x2t":
                    after(act, pe_x2t, n + 1)
                    after(act, pe_hid, 4 * n)
                    a_(x2t[0:CH, :], ps_b[0:CH, 0:QP], ACT.Copy).then_inc(act_x2t, 1)
                    a_(xhl[:, :], ps_b[:, 0:QP], ACT.Copy).then_inc(act_xhl, 1)
                elif what == "oht":
                    after(act, pe_oht, n + 1)
                    after(act, pe_ff, n)
                    a_(oht[:, :], ps_b[0:EXPERTS, 0:QP], ACT.Copy).then_inc(act_oht, 1)
                else:
                    c = int(what[3])
                    after(act, pe_hid, 4 * n + c + 1)
                    a_(hid[c][:, :], (ps_a, ps_b)[c % 2][:, 0:QP], ACT.Relu, bias=w("fb1", c, c + 1)).then_inc(act_hid, 1)

            parts = {2: "x", 8: "rstd", 11: "x2t", 17: "oht", 19: "hid0", 20: "hid1", 21: "hid2", 22: "hid3"}

            def chunk(n, first=False, last=False):
                for k in range(KT):
                    exponentials(n, k)
                    if k == 0 and not last:
                        queries(n + 1)
                    if not first and k in parts:
                        second(n - 1, parts[k])
                if not last:
                    queries_high(n + 1)
                sums(n)

            def image(b, first=False):
                for c in range(NCH + 1):
                    if c >= 1:
                        logarithm(b, c - 1)
                    if c < NCH:
                        squares(b, c)
                    if c >= 1:
                        inverse(b, c - 1)
                n0 = b * CHUNKS
                queries(n0)
                for g in range(4):
                    rows_of_y(b, g)
                queries_high(n0)
                chunk(n0, first=first)
                with act.Fori(1, CHUNKS - 1) as j:
                    chunk(n0 + j)
                chunk(n0 + (CHUNKS - 1), last=True)

            nc.scalar.preload_act_table_set("natural_log_exp_and_others")
            act.wait_ge(ready, PREPARED)
            image(0, first=True)
            with act.Fori(1, IMG) as b:
                image(b)
            for what in parts.values():
                second(IMG * CHUNKS - 1, what)

        @block.vector
        def _(dve):
            v = nc.vector
            credit(dve, BY_DVE)
            v.memset(m0[:, :], 0.0)
            v.tensor_scalar(qpre[:, QC:QP], w("ident", 0, QP - QC), 0.0, None, ALU.mult)
            v.memset(osb[:, QC:QP], 1.0)
            v.memset(xc[:, QC:QP], 0.0)
            v.memset(x2t[CH:CH + 1, :], 1.0)
            v.tensor_copy(big[:, :], w("big"))
            v.memset(w1z[:, :], 0.0)
            v.tensor_copy(w1h[:, :], w("fw1")).then_inc(ready, 1)
            dve.wait_ge(ready, 1)
            v.tensor_tensor(w1z[0:CH, :], w("fw1")[0:CH, :], w1h[0:CH, :].bitcast(fp32), ALU.subtract).then_inc(ready, 1)
            dve.wait_ge(ready, 2)
            v.tensor_copy(w1l[:, :], w1z[:, :])
            v.memset(eps[:, :], EPS).then_inc(ready, 1)

            def piece(b, st):
                if st < NCH:
                    c = st
                    after(dve, act_rs, NCH * b + c + 1)
                    after(dve, dve_yf, NCH * b + c - 1)
                    v.tensor_tensor(t[c % 2][:, :], ps_x[c % 4][:, 0:NC], rs[c % 2][:, :], ALU.mult).then_inc(dve_t, 1)
                if 1 <= st < NCH + 1:
                    c = st - 1
                    after(dve, dve_t, NCH * b + c + 1)
                    v.tensor_scalar(yf[:, NC * c:NC * c + NC], t[c % 2][:, :], w("den"), None, ALU.add).then_inc(dve_yf, 1)
                if 2 <= st < NCH + 2:
                    c = st - 2
                    after(dve, dve_yf, NCH * b + c + 1)
                    v.tensor_copy(yhl[:, NC * c:NC * c + NC], yf[:, NC * c:NC * c + NC]).then_inc(dve_hi, 1)
                if st >= 3:
                    c = st - 3
                    after(dve, dve_hi, NCH * b + c + 1)
                    v.tensor_tensor(yhl[64:128, NC * c:NC * c + NC], yf[64:128, NC * c:NC * c + NC], yhl[64:128, NC * c:NC * c + NC].bitcast(fp32), ALU.subtract).then_inc(dve_lo, 1)

            def maxima(n, k):
                after(dve, pe_mx, MAXES * n + k + 1)
                v.tensor_reduce(mp[:, k:k + 1], ps_m[k % 2][:, 0:NC], AXX, ALU.max).then_inc(dve_mx, 1)

            def take_maxima(n):
                after(dve, dve_mx, MAXES * (n + 1))
                v.tensor_reduce(neg[:, :], sub(mp[:, :]), AXX, ALU.max, negate=True).then_inc(dve_neg, 1)
                after(dve, dve_neg, n + 1)
                after(dve, pe_fix, n)
                v.tensor_copy(m0[:, :].rearrange("p (a h c) -> p a h c", a=SUBS, h=2)[:, :, :, 0], neg[:, :].unsqueeze(2).to_broadcast([128, SUBS, 2])).then_inc(dve_m0, 1)

            def queries_low(n):
                after(dve, act_qh, n + 1)
                v.tensor_tensor(ql[:, :], ps_q[:, 0:QC], qh[:, :].bitcast(fp32), ALU.subtract).then_inc(dve_ql, 1)

            wide = lambda ap, c: ap.unsqueeze(2).to_broadcast([128, SUBS, c])

            CHAIN = ("rden", "h1", "sum", "dev", "dsq", "top", "eq", "cand", "best")

            def chain(n, what):
                after(dve, link, len(CHAIN) * n + CHAIN.index(what) + 1)

            def second(n, what):
                on, lg = sub(ps_a[:, 0:SUBS * 65]), sub(ps_a[:, 0:SUBS * EXPERTS])
                if what == "rden":
                    after(dve, act_x, n + 1)
                    v.reciprocal(rden[:, :], on[:, :, 64]).then_inc(link, 1)
                elif what == "h1":
                    chain(n, "rden")
                    for a in range(SUBS):
                        last = v.scalar_tensor_tensor(h1[:, CH * a:CH * a + CH], on[:, a, 0:CH], rden[:, a:a + 1], xnat[:, CH * a:CH * a + CH], ALU.mult, ALU.add)
                    last.then_inc(link, 1)
                elif what == "sum":
                    chain(n, "h1")
                    v.tensor_reduce(ms[:, :], sub(h1[:, :]), AXX, ALU.add).then_inc(link, 1)
                elif what == "dev":
                    chain(n, "sum")
                    v.scalar_tensor_tensor(sub(dev[:, :]), wide(ms[:, :], CH), -1.0 / CH, sub(h1[:, :]), ALU.mult, ALU.add).then_inc(link, 1)
                elif what == "dsq":
                    chain(n, "dev")
                    v.tensor_tensor(dsq[:, :], dev[:, :], dev[:, :], ALU.mult).then_inc(link, 1)
                elif what == "vs":
                    chain(n, "dsq")
                    v.tensor_reduce(vs[:, :], sub(dsq[:, :]), AXX, ALU.add).then_inc(dve_h1, 1)
                elif what == "x2":
                    after(dve, act_r2, n + 1)
                    after(dve, pe_x2t, n)
                    v.tensor_tensor(x2[:, :].rearrange("p (a h c) -> p a h c", a=SUBS, h=2), sub(dev[:, :]).unsqueeze(2).to_broadcast([128, SUBS, 2, CH]),
                                    rstd[:, :].unsqueeze(2).unsqueeze(3).to_broadcast([128, SUBS, 2, CH]), ALU.mult).then_inc(dve_x2, 1)
                elif what == "xlo":
                    after(dve, act_xhl, n + 1)
                    v.tensor_tensor(xhl[64:128, :], ps_b[64:128, 0:QP], xhl[64:128, :].bitcast(fp32), ALU.subtract).then_inc(dve_xlo, 1)
                elif what == "top":
                    after(dve, pe_lg, n + 1)
                    v.tensor_reduce(top[:, :], lg, AXX, ALU.max).then_inc(link, 1)
                elif what == "eq":
                    chain(n, "top")
                    v.tensor_tensor(sub(eq[:, :]), lg, wide(top[:, :], EXPERTS), ALU.is_equal).then_inc(link, 1)
                elif what == "cand":
                    chain(n, "eq")
                    v.tensor_tensor(sub(cand[:, :]), sub(eq[:, :]), w("revidx").unsqueeze(1).to_broadcast([128, SUBS, EXPERTS]), ALU.mult).then_inc(link, 1)
                elif what == "best":
                    chain(n, "cand")
                    v.tensor_reduce(best[:, :], sub(cand[:, :]), AXX, ALU.max).then_inc(link, 1)
                elif what == "oh":
                    chain(n, "best")
                    after(dve, pe_oht, n)
                    v.tensor_tensor(sub(oh[:, :]), sub(cand[:, :]), wide(best[:, :], EXPERTS), ALU.is_equal).then_inc(dve_oh, 1)
                elif what == "ohm":
                    after(dve, act_oht, n + 1)
                    after(dve, pe_hid, 4 * n)
                    v.tensor_scalar(ohm[:, :], oht[:, :], -1.0, None, ALU.add).then_inc(dve_ohm, 1)
                else:
                    after(dve, pe_ff, n + 1)
                    after(dve, stored, 32 * n)
                    v.scalar_tensor_tensor(res[:, :], ps_a[:, 0:SUBS * CH], 0.0, h1[:, :], ALU.max, ALU.add).then_inc(dve_res, 1)

            parts = {3: ("rden", "h1"), 4: ("sum", "dev"), 5: ("dsq", None), 6: ("vs", None), 9: ("x2", None), 12: ("xlo", None), 13: (None, "top"),
                     14: ("eq", "cand"), 15: ("best", "oh"), 18: ("ohm", None)}

            def chunk(n, first=False, last=False):
                for k in range(KT):
                    before, behind = parts.get(k, (None, None))
                    if not first and before:
                        second(n - 1, before)
                    if not last:
                        for q in range(MAXES):
                            if max_step(q) == k:
                                maxima(n + 1, q)
                        if k == KT - 2:
                            take_maxima(n + 1)
                    if not first and behind:
                        second(n - 1, behind)
                if not last:
                    queries_low(n + 1)
                if not first:
                    second(n - 1, "res")

            def image(b, first=False):
                n0 = b * CHUNKS
                after(dve, act_o, n0)
                v.tensor_copy(lh[:, :], w("rot", 0, 256)[:, bass.ds((b % 2) * 128, 128)]).then_inc(dve_lh, 1)
                for st in range(NCH + 3):
                    piece(b, st)
                for k in range(MAXES):
                    maxima(n0, k)
                take_maxima(n0)
                queries_low(n0)
                chunk(n0, first=first)
                with dve.Fori(1, CHUNKS - 1) as j:
                    chunk(n0 + j)
                chunk(n0 + (CHUNKS - 1), last=True)

            image(0, first=True)
            with dve.Fori(1, IMG) as b:
                image(b)
            for pair in parts.values():
                for what in pair:
                    if what:
                        second(IMG * CHUNKS - 1, what)
            second(IMG * CHUNKS - 1, "res")

        @block.gpsimd
        def _(pool):
            pool.sem_inc(pool_x, CREDIT)
            pool.wait_ge(ready, PREPARED)
            with pool.Fori(0, IMG) as b:
                with pool.Fori(0, CHUNKS) as j:
                    n = b * CHUNKS + j
                    after(pool, pe_p2, n)
                    nc.gpsimd.tensor_copy(xc[:, 0:QC], X[:, bass.ds((b // 2) * TOK + j * QC, QC)]).then_inc(pool_x, 1)

        @block.sync
        def _(sp):
            flat = out.rearrange("b t c -> (b t) c")
            sp.sem_inc(stored, CREDIT)
            with sp.Fori(0, IMG) as b:
                with sp.Fori(0, CHUNKS) as j:
                    after(sp, dve_res, b * CHUNKS + j + 1)
                    at = b * TOK + j * QC
                    sp.dma_start(flat[bass.ds(at, 256), :].rearrange("(a q) c -> q a c", a=2), sub(res[:, :])[:, 0:2, :]).then_inc(stored, 16)
                    sp.dma_start(flat[bass.ds(at + 256, QC - 256), :], sub(res[:, :])[0:QC - 256, 2, :]).then_inc(stored, 16)
            sp.wait_ge(stored, 32 * IMG * CHUNKS + CREDIT)


def kernel(**inputs):
    import numpy as np
    import concourse.bacc as bacc
    from concourse import mybir
    from concourse.bass_utils import run_bass_kernel_spmd

    packed, patches, text = lay_out(inputs["x"], inputs)
    arrays = {"packed": packed, "patches": patches, "text": text}
    nc = bacc.Bacc("TRN2", target_bir_lowering=False, num_devices=1)
    args = [nc.dram_tensor(n, a.shape, mybir.dt.from_np(a.dtype), kind="ExternalInput").ap() for n, a in arrays.items()]
    args.append(nc.dram_tensor("out", (IMG, TOK, CH), mybir.dt.float32, kind="ExternalOutput").ap())
    program(nc, *args)
    got = run_bass_kernel_spmd(nc, [arrays], core_ids=[0]).results[0]["out"]
    shift = WIN // 2
    img = got[:, :SIDE * SIDE].reshape(IMG, STRIPS, STRIPS, WIN, WIN, CH).transpose(0, 1, 3, 2, 4, 5).reshape(IMG, SIDE, SIDE, CH)
    img = np.roll(img, (shift, shift), axis=(1, 2)).reshape(IMG, SIDE * SIDE, CH)
    return np.concatenate([img, got[:, SIDE * SIDE:]], axis=1)
```
